# Optimizing a Trainium2 kernel written in Bass

```python
import numpy as np
import jax
import jax.numpy as jnp

def _softmax(x, axis=-1):
    return jax.nn.softmax(x, axis=axis)

def _gelu(x):
    return jax.nn.gelu(x, approximate=True)

def _silu(x):
    return jax.nn.silu(x)

def _sigmoid(x):
    return jax.nn.sigmoid(x)

def _layernorm(x, axis=-1, eps=1e-05):
    m = jnp.mean(x, axis=axis, keepdims=True)
    v = jnp.var(x, axis=axis, keepdims=True)
    return (x - m) / jnp.sqrt(v + eps)

def _scatter_add(tgt, idx, src, axis=0):
    return tgt.at[idx].add(src)

def _segment_sum(src, seg, n):
    return jax.ops.segment_sum(src, seg, n)
kernel_name = 'mk_flamingo_gated_d2_seqx_r8_d67631'

def setup_inputs(seed: int=0):
    np.random.seed(seed)
    _w = jnp.asarray

    def _rec_inputs():
        import jax
        import jax.numpy as jnp
        _rk = jax.random.key(seed)
        x = 7.22e-05 + 1 * jax.random.normal(jax.random.fold_in(_rk, 1), (16, 128, 128), jnp.float32)
        _lenS = 128 - jax.random.randint(jax.random.fold_in(_rk, 7), (16,), 0, max(1, 128 // 4) + 1, jnp.int32)
        _lenS2 = 77 - jax.random.randint(jax.random.fold_in(_rk, 8), (16,), 0, max(1, 77 // 4) + 1, jnp.int32)
        _ctx_768P = jax.random.normal(jax.random.fold_in(_rk, 11), (16, 16, 96), jnp.float32)
        _ctx_768c = jax.random.dirichlet(jax.random.fold_in(_rk, 511), 0.3 * jnp.ones((16,), jnp.float32), (16, 77))
        _ctx_768t = jnp.einsum('bsk,bkd->bsd', _ctx_768c, _ctx_768P)
        _ctx_768t = _ctx_768t * jax.lax.rsqrt(jnp.mean(jnp.square(_ctx_768t)) + 1e-12) * 0.953939
        ctx_768 = 3.88148e-05 + 0.999967 * (_ctx_768t + 0.3 * jax.random.normal(jax.random.fold_in(_rk, 611), (16, 77, 96), jnp.float32))
        _validS = jnp.arange(128)[None, :] < _lenS[:, None]
        _validS2 = jnp.arange(77)[None, :] < _lenS2[:, None]
        _causal = jnp.tril(jnp.ones((128, 128), dtype=bool))
        mask_BxS_bf1 = jnp.ones((16, 128), dtype=bool)
        mask_BxS2_bf1 = jnp.ones((16, 77), dtype=bool)
        _g = jax.random.normal(jax.random.fold_in(_rk, 9001), (2, 2), jnp.float32)
        _g = jnp.sign(_g) * jnp.maximum(jnp.abs(_g), 1.0) + (_g == 0) * 1.0
        g_xattn = _g[0]
        g_ffn = _g[1]
        return (x, ctx_768, mask_BxS_bf1, mask_BxS2_bf1, g_xattn, g_ffn)
    x, ctx_768, mask_BxS_bf1, mask_BxS2_bf1, g_xattn, g_ffn = _rec_inputs()

    def _L0_xattn_setup():
        import jax, jax.numpy as jnp
        import numpy as np
        B, T, DT, G, DV = (16, 64, 128, 72, 96)
        H, DH = (4, 32)
        INNER = H * DH
        HID = 4 * DT
        N_STATE = 64
        K_TOP = 32

        def layernorm(x, g, b, eps=1e-05):
            m = x.mean(-1, keepdims=True)
            v = x.var(-1, keepdims=True)
            return (x - m) * jax.lax.rsqrt(v + eps) * g + b

        def s4d(x, log_dt, A_re, A_im, C_re, C_im, D_skip):
            Bb, L, D = x.shape
            dt = jnp.exp(log_dt)
            A = A_re + 1j * A_im
            C = C_re + 1j * C_im
            dtA = dt[:, None] * A
            dC = C * (jnp.exp(dtA) - 1.0) / A
            powers = jnp.exp(dtA[:, :, None] * jnp.arange(L))
            K = 2.0 * jnp.einsum('dn,dnl->dl', dC, powers).real
            n = 2 * L
            Kf = jnp.fft.rfft(K, n=n, axis=-1)
            xf = jnp.fft.rfft(x, n=n, axis=1)
            y = jnp.fft.irfft(xf * Kf.T[None], n=n, axis=1)[:, :L]
            return y + x * D_skip
        key = jax.random.key(seed)
        ks = jax.random.split(key, 16)
        s = 0.02
        inp = {'x_text': jax.random.normal(ks[0], (B, T, DT), jnp.float32), 'x_vision': jax.random.normal(ks[1], (B, G, DV), jnp.float32), 'text_mask': jnp.ones((B, T), bool), 'vision_mask': jnp.ones((B, G), bool), 'Wq': jax.random.normal(ks[2], (DT, INNER), jnp.float32) * s, 'Wk': jax.random.normal(ks[3], (DV, INNER), jnp.float32) * s, 'Wv': jax.random.normal(ks[4], (DV, DT), jnp.float32) * s, 'W_film_in': jax.random.normal(ks[5], (DT, 2 * DT), jnp.float32) * s, 'b_film_in': jnp.zeros((2 * DT,), jnp.float32), 'W_film_out': jax.random.normal(ks[6], (DT, 2 * DT), jnp.float32) * s, 'b_film_out': jnp.zeros((2 * DT,), jnp.float32), 'g_norm_in': jnp.ones((DT,), jnp.float32), 'b_norm_in': jnp.zeros((DT,), jnp.float32), 'g_norm_out': jnp.ones((DT,), jnp.float32), 'b_norm_out': jnp.zeros((DT,), jnp.float32), 'g_ffn': jnp.ones((DT,), jnp.float32), 'b_ffn': jnp.zeros((DT,), jnp.float32), 'W1': jax.random.normal(ks[7], (DT, HID), jnp.float32) * s, 'b1': jnp.zeros((HID,), jnp.float32), 'W2': jax.random.normal(ks[8], (HID, DT), jnp.float32) * s, 'b2': jnp.zeros((DT,), jnp.float32), 'log_dt': jnp.log(0.001) + jax.random.uniform(ks[9], (DT,), jnp.float32) * (jnp.log(0.1) - jnp.log(0.001)), 'A_re': -0.5 * jnp.ones((DT, N_STATE), jnp.float32), 'A_im': jnp.tile(jnp.pi * jnp.arange(N_STATE, dtype=jnp.float32), (DT, 1)), 'C_re': jax.random.normal(ks[10], (DT, N_STATE), jnp.float32) * 0.5 ** 0.5, 'C_im': jax.random.normal(ks[11], (DT, N_STATE), jnp.float32) * 0.5 ** 0.5, 'D_skip': jax.random.normal(ks[12], (DT,), jnp.float32), 'mod_gate': jnp.array(0.5, jnp.float32)}
        return inp
    _L0_xattn_all = _L0_xattn_setup()
    _L0_xattn_in = {k: v for k, v in _L0_xattn_all.items() if k in ('Wq', 'Wk', 'Wv', 'W_film_in', 'b_film_in', 'W_film_out', 'b_film_out', 'g_norm_in', 'b_norm_in', 'g_norm_out', 'b_norm_out', 'g_ffn', 'b_ffn', 'W1', 'b1', 'W2', 'b2', 'log_dt', 'A_re', 'A_im', 'C_re', 'C_im', 'D_skip', 'mod_gate')}
    del _L0_xattn_all

    def _L0_ffn_setup():
        import jax, jax.numpy as jnp
        import numpy as np
        NUM_EXPERTS = 8
        TOP_K = 2

        def _moe_forward(x, Wr, br, W1, b1, W2, b2):
            B, S, H = x.shape
            T = B * S
            xf = x.reshape(T, H)
            logits = xf @ Wr + br
            probs = jax.nn.softmax(logits, axis=-1)
            top_p, top_i = jax.lax.top_k(probs, TOP_K)
            weights = top_p / jnp.sum(top_p, axis=-1, keepdims=True)
            one_hot = jax.nn.one_hot(top_i, NUM_EXPERTS, dtype=xf.dtype)
            combine = jnp.einsum('tk,tke->te', weights, one_hot)
            out = jnp.zeros_like(xf)
            for e in range(NUM_EXPERTS):
                h = jax.nn.gelu(xf @ W1[e] + b1[e], approximate=False)
                y = h @ W2[e] + b2[e]
                out = out + combine[:, e:e + 1] * y
            return out.reshape(B, S, H)
        key = jax.random.key(seed)
        ks = jax.random.split(key, 5)
        B, S, H, F, E = (4, 256, 128, 512, NUM_EXPERTS)
        scale_h = 1.0 / np.sqrt(H)
        scale_f = 1.0 / np.sqrt(F)
        return {'hidden_states': jax.random.normal(ks[0], (B, S, H), dtype=jnp.float32), 'Wr': jax.random.normal(ks[1], (H, E), dtype=jnp.float32) * scale_h, 'br': jnp.zeros((E,), dtype=jnp.float32), 'W1': jax.random.normal(ks[2], (E, H, F), dtype=jnp.float32) * scale_h, 'b1': jnp.zeros((E, F), dtype=jnp.float32), 'W2': jax.random.normal(ks[3], (E, F, H), dtype=jnp.float32) * scale_f, 'b2': jnp.zeros((E, H), dtype=jnp.float32)}
    _L0_ffn_all = _L0_ffn_setup()
    _L0_ffn_in = {k: v for k, v in _L0_ffn_all.items() if k in ('Wr', 'br', 'W1', 'b1', 'W2', 'b2')}
    del _L0_ffn_all

    def _L1_xattn_setup():
        import jax, jax.numpy as jnp
        import numpy as np
        N_HEADS = 16
        DIM_EMBED = 128
        DIM_CROSS = 96
        DIM_HEAD = DIM_EMBED // N_HEADS
        key = jax.random.key(seed)
        ks = jax.random.split(key, 10)
        B, Sq, Sk = (8, 512, 77)
        s_e = 1.0 / np.sqrt(DIM_EMBED)
        s_c = 1.0 / np.sqrt(DIM_CROSS)
        return {'x': jax.random.normal(ks[0], (B, Sq, DIM_EMBED), jnp.float32), 'y': jax.random.normal(ks[1], (B, Sk, DIM_CROSS), jnp.float32), 'wq': jax.random.normal(ks[2], (DIM_EMBED, DIM_EMBED), jnp.float32) * s_e, 'bq': jax.random.normal(ks[3], (DIM_EMBED,), jnp.float32) * 0.01, 'wk': jax.random.normal(ks[4], (DIM_CROSS, DIM_EMBED), jnp.float32) * s_c, 'bk': jax.random.normal(ks[5], (DIM_EMBED,), jnp.float32) * 0.01, 'wv': jax.random.normal(ks[6], (DIM_CROSS, DIM_EMBED), jnp.float32) * s_c, 'bv': jax.random.normal(ks[7], (DIM_EMBED,), jnp.float32) * 0.01, 'wo': jax.random.normal(ks[8], (DIM_EMBED, DIM_EMBED), jnp.float32) * s_e, 'bo': jax.random.normal(ks[9], (DIM_EMBED,), jnp.float32) * 0.01}
    _L1_xattn_all = _L1_xattn_setup()
    _L1_xattn_in = {k: v for k, v in _L1_xattn_all.items() if k in ('wq', 'bq', 'wk', 'bk', 'wv', 'bv', 'wo', 'bo')}
    del _L1_xattn_all

    def _L1_ffn_setup():
        import jax, jax.numpy as jnp
        import numpy as np
        DIM = 128
        DEPTH = 6
        HEADS = 16
        DIM_HEAD = 64
        WINDOW = 32
        INNER = HEADS * DIM_HEAD
        DIM_INNER = int(DIM * 4 * 2 / 3)
        QK_SCALE = 8.0

        def shift_tokens(t):
            a, s = jnp.split(t, 2, -1)
            s = jnp.pad(s, ((0, 0), (1, 0), (0, 0)))[:, :-1]
            return jnp.concatenate([a, s], -1)

        def l2norm(t):
            return t / jnp.maximum(jnp.linalg.norm(t, axis=-1, keepdims=True), 1e-12)

        def rotate_half(x):
            x1, x2 = jnp.split(x, 2, -1)
            return jnp.concatenate([-x2, x1], -1)

        def rotary_tables(n):
            half = jnp.arange(0, DIM_HEAD, 2, dtype=jnp.float32)
            inv_freq = 1.0 / 10000.0 ** (half / DIM_HEAD)
            t = jnp.arange(n, dtype=jnp.float32)
            freqs = t[:, None] * inv_freq[None, :]
            freqs = jnp.concatenate([freqs, freqs], -1)
            base_scale = (half + 0.4 * DIM_HEAD) / (1.4 * DIM_HEAD)
            power = (t - n // 2) / (WINDOW // 2)
            scale = base_scale[None, :] ** power[:, None]
            scale = jnp.concatenate([scale, scale], -1)
            return (freqs, scale)

        def local_attention(q, k, v):
            b, h, n, d = q.shape
            w = WINDOW
            nw = n // w
            bq = q.reshape(b, h, nw, w, d)
            bk = k.reshape(b, h, nw, w, d)
            bv = v.reshape(b, h, nw, w, d)

            def look(t):
                p = jnp.pad(t, ((0, 0), (0, 0), (1, 0), (0, 0), (0, 0)))
                return jnp.concatenate([p[:, :, :nw], p[:, :, 1:]], axis=3)
            bk2, bv2 = (look(bk), look(bv))
            seq = jnp.arange(n).reshape(nw, w)
            seq_p = jnp.pad(seq, ((1, 0), (0, 0)), constant_values=-1)
            jt = jnp.concatenate([seq_p[:nw], seq_p[1:]], axis=1)
            it = seq[:, :, None]
            jb = jt[:, None, :]
            mask = (it < jb) | (it > jb + w) | (jb == -1)
            sim = jnp.einsum('bhwie,bhwje->bhwij', bq, bk2) * QK_SCALE
            sim = jnp.where(mask, -jnp.finfo(sim.dtype).max, sim)
            attn = jax.nn.softmax(sim, -1)
            out = jnp.einsum('bhwij,bhwje->bhwie', attn, bv2)
            return out.reshape(b, h, n, d)

        def attn_layer(x, Wqkv, qs, ksc, Wo):
            b, n, _ = x.shape
            qkv = x @ Wqkv
            q, k, v = jnp.split(qkv, 3, -1)
            sh = lambda t: t.reshape(b, n, HEADS, DIM_HEAD).transpose(0, 2, 1, 3)
            q, k, v = (sh(q), sh(k), sh(v))
            q = l2norm(q) * qs
            k = l2norm(k) * ksc
            freqs, scale = rotary_tables(n)
            cos, sin = (jnp.cos(freqs), jnp.sin(freqs))
            q = q * cos * scale + rotate_half(q) * sin * scale
            inv = 1.0 / scale
            k = k * cos * inv + rotate_half(k) * sin * inv
            out = local_attention(q, k, v)
            out = out.transpose(0, 2, 1, 3).reshape(b, n, INNER)
            return out @ Wo

        def ffn_layer(x, g, bln, W1, b1, W2, b2):
            mu = x.mean(-1, keepdims=True)
            var = ((x - mu) ** 2).mean(-1, keepdims=True)
            xn = (x - mu) / jnp.sqrt(var + 1e-05) * g + bln
            hg = xn @ W1 + b1
            a, gate = jnp.split(hg, 2, -1)
            return a * jax.nn.gelu(gate, approximate=False) @ W2 + b2
        key = jax.random.key(seed)
        ks = jax.random.split(key, 8)
        B, N = (2, 256)
        init = lambda k, shape: jax.random.normal(k, shape, jnp.float32) * 0.02
        return {'x': jax.random.normal(ks[0], (B, N, DIM), jnp.float32), 'Wqkv': init(ks[1], (DEPTH, DIM, 3 * INNER)), 'q_scale': jnp.ones((DEPTH, DIM_HEAD), jnp.float32), 'k_scale': jnp.ones((DEPTH, DIM_HEAD), jnp.float32), 'Wo': init(ks[2], (DEPTH, INNER, DIM)), 'ln_g': jnp.ones((DEPTH, DIM), jnp.float32), 'ln_b': jnp.zeros((DEPTH, DIM), jnp.float32), 'W1': init(ks[3], (DEPTH, DIM, 2 * DIM_INNER)), 'b1': jnp.zeros((DEPTH, 2 * DIM_INNER), jnp.float32), 'W2': init(ks[4], (DEPTH, DIM_INNER, DIM)), 'b2': jnp.zeros((DEPTH, DIM), jnp.float32)}
    _L1_ffn_all = _L1_ffn_setup()
    _L1_ffn_in = {k: v for k, v in _L1_ffn_all.items() if k in ('Wqkv', 'q_scale', 'k_scale', 'Wo', 'ln_g', 'ln_b', 'W1', 'b1', 'W2', 'b2')}
    del _L1_ffn_all
    return {'x': x, 'ctx_768': ctx_768, 'mask_BxS_bf1': mask_BxS_bf1, 'mask_BxS2_bf1': mask_BxS2_bf1, 'g_xattn': g_xattn, 'g_ffn': g_ffn, 'L0_xattn_Wq': _L0_xattn_in['Wq'], 'L0_xattn_Wk': _L0_xattn_in['Wk'], 'L0_xattn_Wv': _L0_xattn_in['Wv'], 'L0_xattn_W_film_in': _L0_xattn_in['W_film_in'], 'L0_xattn_b_film_in': _L0_xattn_in['b_film_in'], 'L0_xattn_W_film_out': _L0_xattn_in['W_film_out'], 'L0_xattn_b_film_out': _L0_xattn_in['b_film_out'], 'L0_xattn_g_norm_in': _L0_xattn_in['g_norm_in'], 'L0_xattn_b_norm_in': _L0_xattn_in['b_norm_in'], 'L0_xattn_g_norm_out': _L0_xattn_in['g_norm_out'], 'L0_xattn_b_norm_out': _L0_xattn_in['b_norm_out'], 'L0_xattn_g_ffn': _L0_xattn_in['g_ffn'], 'L0_xattn_b_ffn': _L0_xattn_in['b_ffn'], 'L0_xattn_W1': _L0_xattn_in['W1'], 'L0_xattn_b1': _L0_xattn_in['b1'], 'L0_xattn_W2': _L0_xattn_in['W2'], 'L0_xattn_b2': _L0_xattn_in['b2'], 'L0_xattn_log_dt': _L0_xattn_in['log_dt'], 'L0_xattn_A_re': _L0_xattn_in['A_re'], 'L0_xattn_A_im': _L0_xattn_in['A_im'], 'L0_xattn_C_re': _L0_xattn_in['C_re'], 'L0_xattn_C_im': _L0_xattn_in['C_im'], 'L0_xattn_D_skip': _L0_xattn_in['D_skip'], 'L0_xattn_mod_gate': _L0_xattn_in['mod_gate'], 'L0_ffn_Wr': _L0_ffn_in['Wr'], 'L0_ffn_br': _L0_ffn_in['br'], 'L0_ffn_W1': _L0_ffn_in['W1'], 'L0_ffn_b1': _L0_ffn_in['b1'], 'L0_ffn_W2': _L0_ffn_in['W2'], 'L0_ffn_b2': _L0_ffn_in['b2'], 'L1_xattn_wq': _L1_xattn_in['wq'], 'L1_xattn_bq': _L1_xattn_in['bq'], 'L1_xattn_wk': _L1_xattn_in['wk'], 'L1_xattn_bk': _L1_xattn_in['bk'], 'L1_xattn_wv': _L1_xattn_in['wv'], 'L1_xattn_bv': _L1_xattn_in['bv'], 'L1_xattn_wo': _L1_xattn_in['wo'], 'L1_xattn_bo': _L1_xattn_in['bo'], 'L1_ffn_Wqkv': _L1_ffn_in['Wqkv'], 'L1_ffn_q_scale': _L1_ffn_in['q_scale'], 'L1_ffn_k_scale': _L1_ffn_in['k_scale'], 'L1_ffn_Wo': _L1_ffn_in['Wo'], 'L1_ffn_ln_g': _L1_ffn_in['ln_g'], 'L1_ffn_ln_b': _L1_ffn_in['ln_b'], 'L1_ffn_W1': _L1_ffn_in['W1'], 'L1_ffn_b1': _L1_ffn_in['b1'], 'L1_ffn_W2': _L1_ffn_in['W2'], 'L1_ffn_b2': _L1_ffn_in['b2']}

def reference(x, ctx_768, mask_BxS_bf1, mask_BxS2_bf1, g_xattn, g_ffn, L0_xattn_Wq, L0_xattn_Wk, L0_xattn_Wv, L0_xattn_W_film_in, L0_xattn_b_film_in, L0_xattn_W_film_out, L0_xattn_b_film_out, L0_xattn_g_norm_in, L0_xattn_b_norm_in, L0_xattn_g_norm_out, L0_xattn_b_norm_out, L0_xattn_g_ffn, L0_xattn_b_ffn, L0_xattn_W1, L0_xattn_b1, L0_xattn_W2, L0_xattn_b2, L0_xattn_log_dt, L0_xattn_A_re, L0_xattn_A_im, L0_xattn_C_re, L0_xattn_C_im, L0_xattn_D_skip, L0_xattn_mod_gate, L0_ffn_Wr, L0_ffn_br, L0_ffn_W1, L0_ffn_b1, L0_ffn_W2, L0_ffn_b2, L1_xattn_wq, L1_xattn_bq, L1_xattn_wk, L1_xattn_bk, L1_xattn_wv, L1_xattn_bv, L1_xattn_wo, L1_xattn_bo, L1_ffn_Wqkv, L1_ffn_q_scale, L1_ffn_k_scale, L1_ffn_Wo, L1_ffn_ln_g, L1_ffn_ln_b, L1_ffn_W1, L1_ffn_b1, L1_ffn_W2, L1_ffn_b2):
    import jax
    import jax.numpy as jnp

    def _L0_xattn_ref(x_text, x_vision, text_mask, vision_mask, Wq, Wk, Wv, W_film_in, b_film_in, W_film_out, b_film_out, g_norm_in, b_norm_in, g_norm_out, b_norm_out, g_ffn, b_ffn, W1, b1, W2, b2, log_dt, A_re, A_im, C_re, C_im, D_skip, mod_gate):
        import jax, jax.numpy as jnp
        import numpy as np
        B, T, DT, G, DV = (16, 64, 128, 72, 96)
        H, DH = (4, 32)
        INNER = H * DH
        HID = 4 * DT
        N_STATE = 64
        K_TOP = 32

        def layernorm(x, g, b, eps=1e-05):
            m = x.mean(-1, keepdims=True)
            v = x.var(-1, keepdims=True)
            return (x - m) * jax.lax.rsqrt(v + eps) * g + b

        def s4d(x, log_dt, A_re, A_im, C_re, C_im, D_skip):
            Bb, L, D = x.shape
            dt = jnp.exp(log_dt)
            A = A_re + 1j * A_im
            C = C_re + 1j * C_im
            dtA = dt[:, None] * A
            dC = C * (jnp.exp(dtA) - 1.0) / A
            powers = jnp.exp(dtA[:, :, None] * jnp.arange(L))
            K = 2.0 * jnp.einsum('dn,dnl->dl', dC, powers).real
            n = 2 * L
            Kf = jnp.fft.rfft(K, n=n, axis=-1)
            xf = jnp.fft.rfft(x, n=n, axis=1)
            y = jnp.fft.irfft(xf * Kf.T[None], n=n, axis=1)[:, :L]
            return y + x * D_skip
        Bb, Tt, D = x_text.shape
        Gg = x_vision.shape[1]
        Q = (x_text @ Wq).reshape(Bb, Tt, H, DH)
        K = (x_vision @ Wk).reshape(Bb, Gg, H, DH)
        scores = jnp.einsum('bthd,bghd->bhtg', Q, K) / np.sqrt(DH).astype(np.float32)
        scores = jnp.where(vision_mask[:, None, None, :], scores, -jnp.inf)
        topv, topi = jax.lax.top_k(scores, K_TOP)
        probs = jax.nn.softmax(topv, axis=-1)
        bi = jnp.arange(Bb)[:, None, None, None]
        hi = jnp.arange(H)[None, :, None, None]
        ti = jnp.arange(Tt)[None, None, :, None]
        attn = jnp.zeros_like(scores).at[bi, hi, ti, topi].set(probs)
        attn_mean = attn.mean(axis=1)
        V = x_vision @ Wv
        c_t = jnp.einsum('btg,bgd->btd', attn_mean, V)
        c_t = c_t * text_mask[..., None]
        x = layernorm(x_text, g_norm_in, b_norm_in)
        scale_in, shift_in = jnp.split(c_t @ W_film_in + b_film_in, 2, axis=-1)
        x = x * (1.0 + mod_gate * scale_in) + mod_gate * shift_in
        y = s4d(x, log_dt, A_re, A_im, C_re, C_im, D_skip)
        scale_out, shift_out = jnp.split(c_t @ W_film_out + b_film_out, 2, axis=-1)
        y = y * (1.0 + mod_gate * scale_out) + mod_gate * shift_out
        xt = x_text + y
        h = layernorm(xt, g_ffn, b_ffn)
        h = jax.nn.gelu(h @ W1 + b1, approximate=False) @ W2 + b2
        xt = xt + h
        return layernorm(xt, g_norm_out, b_norm_out)

    def _L0_ffn_ref(hidden_states, Wr, br, W1, b1, W2, b2):
        import jax, jax.numpy as jnp
        import numpy as np
        NUM_EXPERTS = 8
        TOP_K = 2

        def _moe_forward(x, Wr, br, W1, b1, W2, b2):
            B, S, H = x.shape
            T = B * S
            xf = x.reshape(T, H)
            logits = xf @ Wr + br
            probs = jax.nn.softmax(logits, axis=-1)
            top_p, top_i = jax.lax.top_k(probs, TOP_K)
            weights = top_p / jnp.sum(top_p, axis=-1, keepdims=True)
            one_hot = jax.nn.one_hot(top_i, NUM_EXPERTS, dtype=xf.dtype)
            combine = jnp.einsum('tk,tke->te', weights, one_hot)
            out = jnp.zeros_like(xf)
            for e in range(NUM_EXPERTS):
                h = jax.nn.gelu(xf @ W1[e] + b1[e], approximate=False)
                y = h @ W2[e] + b2[e]
                out = out + combine[:, e:e + 1] * y
            return out.reshape(B, S, H)
        return _moe_forward(hidden_states, Wr, br, W1, b1, W2, b2)

    def _L1_xattn_ref(x, y, wq, bq, wk, bk, wv, bv, wo, bo):
        import jax, jax.numpy as jnp
        import numpy as np
        N_HEADS = 16
        DIM_EMBED = 128
        DIM_CROSS = 96
        DIM_HEAD = DIM_EMBED // N_HEADS
        B, Sq, E = x.shape
        H, D = (N_HEADS, DIM_HEAD)
        q = (x @ wq + bq).reshape(B, Sq, H, D).transpose(0, 2, 1, 3)
        k = (y @ wk + bk).reshape(B, -1, H, D).transpose(0, 2, 1, 3)
        v = (y @ wv + bv).reshape(B, -1, H, D).transpose(0, 2, 1, 3)
        scores = jnp.einsum('bhqd,bhkd->bhqk', q, k) / jnp.sqrt(jnp.asarray(D, x.dtype))
        attn = jax.nn.softmax(scores, axis=-1)
        out = jnp.einsum('bhqk,bhkd->bhqd', attn, v)
        out = out.transpose(0, 2, 1, 3).reshape(B, Sq, E)
        return out @ wo + bo

    def _L1_ffn_ref(x, Wqkv, q_scale, k_scale, Wo, ln_g, ln_b, W1, b1, W2, b2):
        import jax, jax.numpy as jnp
        import numpy as np
        DIM = 128
        DEPTH = 6
        HEADS = 16
        DIM_HEAD = 64
        WINDOW = 32
        INNER = HEADS * DIM_HEAD
        DIM_INNER = int(DIM * 4 * 2 / 3)
        QK_SCALE = 8.0

        def shift_tokens(t):
            a, s = jnp.split(t, 2, -1)
            s = jnp.pad(s, ((0, 0), (1, 0), (0, 0)))[:, :-1]
            return jnp.concatenate([a, s], -1)

        def l2norm(t):
            return t / jnp.maximum(jnp.linalg.norm(t, axis=-1, keepdims=True), 1e-12)

        def rotate_half(x):
            x1, x2 = jnp.split(x, 2, -1)
            return jnp.concatenate([-x2, x1], -1)

        def rotary_tables(n):
            half = jnp.arange(0, DIM_HEAD, 2, dtype=jnp.float32)
            inv_freq = 1.0 / 10000.0 ** (half / DIM_HEAD)
            t = jnp.arange(n, dtype=jnp.float32)
            freqs = t[:, None] * inv_freq[None, :]
            freqs = jnp.concatenate([freqs, freqs], -1)
            base_scale = (half + 0.4 * DIM_HEAD) / (1.4 * DIM_HEAD)
            power = (t - n // 2) / (WINDOW // 2)
            scale = base_scale[None, :] ** power[:, None]
            scale = jnp.concatenate([scale, scale], -1)
            return (freqs, scale)

        def local_attention(q, k, v):
            b, h, n, d = q.shape
            w = WINDOW
            nw = n // w
            bq = q.reshape(b, h, nw, w, d)
            bk = k.reshape(b, h, nw, w, d)
            bv = v.reshape(b, h, nw, w, d)

            def look(t):
                p = jnp.pad(t, ((0, 0), (0, 0), (1, 0), (0, 0), (0, 0)))
                return jnp.concatenate([p[:, :, :nw], p[:, :, 1:]], axis=3)
            bk2, bv2 = (look(bk), look(bv))
            seq = jnp.arange(n).reshape(nw, w)
            seq_p = jnp.pad(seq, ((1, 0), (0, 0)), constant_values=-1)
            jt = jnp.concatenate([seq_p[:nw], seq_p[1:]], axis=1)
            it = seq[:, :, None]
            jb = jt[:, None, :]
            mask = (it < jb) | (it > jb + w) | (jb == -1)
            sim = jnp.einsum('bhwie,bhwje->bhwij', bq, bk2) * QK_SCALE
            sim = jnp.where(mask, -jnp.finfo(sim.dtype).max, sim)
            attn = jax.nn.softmax(sim, -1)
            out = jnp.einsum('bhwij,bhwje->bhwie', attn, bv2)
            return out.reshape(b, h, n, d)

        def attn_layer(x, Wqkv, qs, ksc, Wo):
            b, n, _ = x.shape
            qkv = x @ Wqkv
            q, k, v = jnp.split(qkv, 3, -1)
            sh = lambda t: t.reshape(b, n, HEADS, DIM_HEAD).transpose(0, 2, 1, 3)
            q, k, v = (sh(q), sh(k), sh(v))
            q = l2norm(q) * qs
            k = l2norm(k) * ksc
            freqs, scale = rotary_tables(n)
            cos, sin = (jnp.cos(freqs), jnp.sin(freqs))
            q = q * cos * scale + rotate_half(q) * sin * scale
            inv = 1.0 / scale
            k = k * cos * inv + rotate_half(k) * sin * inv
            out = local_attention(q, k, v)
            out = out.transpose(0, 2, 1, 3).reshape(b, n, INNER)
            return out @ Wo

        def ffn_layer(x, g, bln, W1, b1, W2, b2):
            mu = x.mean(-1, keepdims=True)
            var = ((x - mu) ** 2).mean(-1, keepdims=True)
            xn = (x - mu) / jnp.sqrt(var + 1e-05) * g + bln
            hg = xn @ W1 + b1
            a, gate = jnp.split(hg, 2, -1)
            return a * jax.nn.gelu(gate, approximate=False) @ W2 + b2
        for i in range(DEPTH):
            x = attn_layer(shift_tokens(x), Wqkv[i], q_scale[i], k_scale[i], Wo[i]) + x
            x = ffn_layer(shift_tokens(x), ln_g[i], ln_b[i], W1[i], b1[i], W2[i], b2[i]) + x
        return x
    x = x + jnp.tanh(g_xattn[0]) * _L0_xattn_ref(_layernorm(x, axis=-1), ctx_768, mask_BxS_bf1, mask_BxS2_bf1, L0_xattn_Wq, L0_xattn_Wk, L0_xattn_Wv, L0_xattn_W_film_in, L0_xattn_b_film_in, L0_xattn_W_film_out, L0_xattn_b_film_out, L0_xattn_g_norm_in, L0_xattn_b_norm_in, L0_xattn_g_norm_out, L0_xattn_b_norm_out, L0_xattn_g_ffn, L0_xattn_b_ffn, L0_xattn_W1, L0_xattn_b1, L0_xattn_W2, L0_xattn_b2, L0_xattn_log_dt, L0_xattn_A_re, L0_xattn_A_im, L0_xattn_C_re, L0_xattn_C_im, L0_xattn_D_skip, L0_xattn_mod_gate)
    x = x + jnp.tanh(g_ffn[0]) * _L0_ffn_ref(_layernorm(x, axis=-1), L0_ffn_Wr, L0_ffn_br, L0_ffn_W1, L0_ffn_b1, L0_ffn_W2, L0_ffn_b2)
    x = x + jnp.tanh(g_xattn[1]) * _L1_xattn_ref(_layernorm(x, axis=-1), ctx_768, L1_xattn_wq, L1_xattn_bq, L1_xattn_wk, L1_xattn_bk, L1_xattn_wv, L1_xattn_bv, L1_xattn_wo, L1_xattn_bo)
    x = x + jnp.tanh(g_ffn[1]) * _L1_ffn_ref(_layernorm(x, axis=-1), L1_ffn_Wqkv, L1_ffn_q_scale, L1_ffn_k_scale, L1_ffn_Wo, L1_ffn_ln_g, L1_ffn_ln_b, L1_ffn_W1, L1_ffn_b1, L1_ffn_W2, L1_ffn_b2)
    return x

_drawn_inputs = setup_inputs


def setup_inputs(seed=0):
    import zlib

    import numpy as np

    out = dict(_drawn_inputs(seed))
    spreads = {'g_ffn': (-1.0, 0.2),
     'L0_xattn_b_film_in': (0.0, 0.1),
     'L0_xattn_b_film_out': (0.0, 0.1),
     'L0_xattn_g_norm_in': (1.0, 0.2),
     'L0_xattn_b_norm_in': (0.0, 0.1),
     'L0_xattn_g_norm_out': (1.0, 0.2),
     'L0_xattn_b_norm_out': (0.0, 0.1),
     'L0_xattn_g_ffn': (1.0, 0.6),
     'L0_xattn_b_ffn': (0.0, 2.0),
     'L0_xattn_b1': (0.0, 0.565),
     'L0_xattn_b2': (0.0, 0.1),
     'L0_xattn_A_re': (-0.5, 0.2),
     'L0_ffn_br': (0.0, 0.1),
     'L0_ffn_b1': (0.0, 0.369),
     'L0_ffn_b2': (0.0, 0.1),
     'L1_ffn_q_scale': (1.0, 0.6),
     'L1_ffn_k_scale': (1.0, 0.6),
     'L1_ffn_ln_g': (1.0, 0.6),
     'L1_ffn_ln_b': (0.0, 0.8),
     'L1_ffn_b1': (0.0, 0.546),
     'L1_ffn_b2': (0.0, 0.1)}
    factors = {'L0_xattn_Wq': 8.0,
     'L0_xattn_Wk': 8.0,
     'L0_xattn_Wv': 3.905,
     'L0_xattn_W_film_in': 4.45,
     'L0_xattn_W_film_out': 5.208,
     'L1_xattn_bq': 39.947,
     'L1_xattn_bk': 64.0,
     'L1_xattn_bv': 8.0,
     'L1_xattn_bo': 8.0}
    for name, (base, spread) in spreads.items():
        noise = np.random.default_rng([zlib.crc32(name.encode()), seed]).standard_normal(out[name].shape)
        drawn = base * np.exp(spread * noise) if base else spread * noise
        out[name] = jnp.asarray(drawn.astype(out[name].dtype))
    for name, factor in factors.items():
        out[name] = (out[name] * factor).astype(out[name].dtype)
    return out
```

```python
from contextlib import ExitStack

import numpy as np

import concourse.bass as bass
from concourse import mybir

F32 = mybir.dt.float32
I32 = mybir.dt.int32
U8 = mybir.dt.uint8
BF16 = mybir.dt.bfloat16
ALU = mybir.AluOpType
ACT = mybir.ActivationFunctionType
AX = mybir.AxisListType

B = 16
T = 128
D = 128
S2 = 77
DC = 96
EPS = 1e-5
BIG = 1.0e30
BIG16 = -(2.0 ** 100)
GONE = -3.0e38

H0, DH0 = 4, 32
TOPK = 32
HID = 4 * D
NS = 64
NJ, NI = 16, 8
TURN = 6.283185
ROUND = 1.5 * 2.0 ** 23
NE, FE = 8, 512
GB = 4
NG = B // GB
H1, DH1 = 16, 8
SCALE1 = float(1.0 / np.sqrt(DH1))
SPANS = [(0, 5), (5, 5), (10, 6)]

DEPTH = 6
NH = 16
E = 64
WINDOW = 32
INNER = NH * E
FF = int(D * 4 * 2 / 3)
QK_SCALE = 8.0
FC = 3
W_QKV, W_O, W_1, W_2 = 0, 3 * INNER, 3 * INNER + INNER, 3 * INNER + INNER + 2 * FF
W_ALL = W_2 + FC * D
R_G, R_B, R_B1, R_B2, R_QS, R_KS = 0, D, 2 * D, 2 * D + 2 * FF, 3 * D + 2 * FF, 3 * D + 2 * FF + 2 * E
R_ALL = R_KS + 2 * E

def offsets(*sizes):
    at, o = {}, 0
    for name, n in sizes:
        at[name] = (o, n)
        o += n
    return at, o


N_CONST = 10
R0_AT, R0_ALL = offsets(("g_in", D), ("b_in", D), ("g_ffn", D), ("b_ffn", D), ("g_out", D), ("b_out", D), ("b2", D), ("film", 4 * D),
                        ("br", NE), ("bo", D), ("gates", 4), ("mod", 1), ("log_dt", D), ("dskip", D), ("experts", NE))
W0_AT, W0_ALL = offsets(("Wq", 128), ("film", 512), ("W1", HID), ("W2", HID), ("Wr", NE), ("wq1", 128), ("wo1", 128), ("k0", 128), ("v0", 128),
                        ("k1", 128), ("v1", 128), ("Fc", 128), ("Fs", 128), ("Gc", 128), ("Gs", 128), ("are", 128), ("aim", 128), ("cre", 128),
                        ("cim", 128), ("hm0", H0), ("hm1", H1), ("j", NJ), ("i", NI))
C_AT, C_ALL = offsets(("b1", 4), ("bq", 1), ("mb1", 4 * NE), ("m0", 1), ("m1", 1), ("-m0", 1), ("-m1", 1), ("off", 1), ("nz", 1), ("z", 1))

RSQRT_MAGIC = float(0x5F3759DF)
RSQRT_STEPS = 3
RSQRT = ["shift", "guess"] + [f"{s}{i}" for i in range(RSQRT_STEPS) for s in ("square", "half", "newton")]
SETUP = [
    "identb", "band",
    "dta_re", "dta_im", "turns", "cos_turns", "cos_whole", "cos_frac", "sin_turns", "sin_whole", "sin_frac", "e_re", "e_im",
    "e_re_less_1", "c_e_rr", "c_e_ii", "num_re", "c_e_ri", "c_e_ir", "num_im", "a_rr", "a_ii", "a_abs2", "a_inv", "scale", "n_a_rr",
    "n_a_ii", "dc_re_num", "dc_re", "n_a_ir", "n_a_ri", "dc_im_num", "dc_im", "row_cos_0", "row_cos", "row_sin_0", "row_sin",
    "sin_i_turns", "cos_i_turns", "cos_i_whole", "cos_i_frac", "sin_i_whole", "sin_i_frac", "wave_j_turns", "wave_j_off",
    "wave_j_whole", "wave_j_frac", "arg_i", "arg_j", "cos_i_mag", "sin_i_mag", "row_i_cos", "row_i_sin", "row_i", "power_j", "rows",
    "f_cos", "f_sin", "f_half", "f_flip", "text_mask", "context_mask",
]


class Steps:

    def __init__(self, sem, names, lead=1):
        self.sem, self.names, self.lead, self.turn = sem, names, lead, 0

    def start(self):
        return self.lead * len(self.names)

    def at(self, name, n):
        return n * len(self.names) + (self.start() + self.names.index(name) + 1)

    def step(self, name):
        assert self.names[self.turn % len(self.names)] == name, (name, self.names[self.turn % len(self.names)])
        self.turn += 1
        return 1


def pipeline(eng, body, depth, count, base):
    for t in range(depth - 1):
        body([(t - s, base + (t - s)) if s <= t else None for s in range(depth)])
    with eng.Fori(depth - 1, count) as i:
        body([(i - s, i - s + base) if s else (i, i + base) for s in range(depth)])
    for t in range(count, count + depth - 1):
        body([(t - s, base + (t - s)) if t - s < count else None for s in range(depth)])


def rsqrt(dve, S, n, pre, y, h, v):
    yi, vi = y.bitcast(I32), v.bitcast(I32)
    dve.tensor_scalar(yi, vi, 1, None, ALU.logical_shift_right).then_inc(S.sem, S.step(pre + "shift"))
    dve.wait_ge(S.sem, S.at(pre + "shift", n))
    dve.tensor_scalar(yi, yi, -1.0, RSQRT_MAGIC, ALU.mult, ALU.add).then_inc(S.sem, S.step(pre + "guess"))
    last = "guess"
    for i in range(RSQRT_STEPS):
        dve.wait_ge(S.sem, S.at(pre + last, n))
        dve.tensor_tensor(h, y, y, ALU.mult).then_inc(S.sem, S.step(pre + f"square{i}"))
        dve.wait_ge(S.sem, S.at(pre + f"square{i}", n))
        dve.scalar_tensor_tensor(h, h, -0.5, v, ALU.mult, ALU.mult).then_inc(S.sem, S.step(pre + f"half{i}"))
        dve.wait_ge(S.sem, S.at(pre + f"half{i}", n))
        dve.scalar_tensor_tensor(y, h, 1.5, y, ALU.add, ALU.mult).then_inc(S.sem, S.step(pre + f"newton{i}"))
        last = f"newton{i}"


NORM = ["stats", "aggr", "eps"] + RSQRT + ["xn"]


def normalise(dve, S, n, pre, out, x, N, s_pass):
    stats, mv, vv, rr, rh = N[:, 0:6], N[:, 6:8], N[:, 8:9], N[:, 9:10], N[:, 10:11]
    dve.sem_inc(s_pass, 1)
    dve.bn_stats(stats, x).then_inc(S.sem, S.step(pre + "stats"))
    dve.wait_ge(S.sem, S.at(pre + "stats", n))
    dve.sem_inc(s_pass, 1)
    dve.bn_aggr(mv, stats).then_inc(S.sem, S.step(pre + "aggr"))
    dve.wait_ge(S.sem, S.at(pre + "aggr", n))
    dve.tensor_scalar(vv, mv[:, 1:2], EPS, None, ALU.add).then_inc(S.sem, S.step(pre + "eps"))
    dve.wait_ge(S.sem, S.at(pre + "eps", n))
    rsqrt(dve, S, n, pre, rr, rh, vv)
    dve.wait_ge(S.sem, S.at(pre + f"newton{RSQRT_STEPS - 1}", n))
    dve.tensor_scalar(out, x, mv[:, 0:1], rr, ALU.subtract, ALU.mult).then_inc(S.sem, S.step(pre + "xn"))


def flamingo(nc, a, out):
    with ExitStack() as ctx:
        def sb(name, shape, dt=F32):
            return ctx.enter_context(nc.sbuf_tensor(name, shape, dt))

        def sem(name):
            return ctx.enter_context(nc.semaphore(name))

        def steps(name, names, lead=1):
            return Steps(sem(name), names, lead)

        X = sb("X", [T, B, D])
        XD = sb("XD", [T, B, D])
        XS = sb("XS", [T, B, D])
        ident = sb("ident_sb", [128, 128])
        zeros = sb("zeros", [128, 128])
        identb = sb("identb_sb", [128, 128], BF16)

        band = sb("band_sb", [128, 4, 128], BF16)
        rope = sb("rope_sb", [128, 4, E])
        arena = sb("arena", [128, 18 * 1024])
        taken = [0]

        def part(*shape, at=None):
            n = int(np.prod(shape))
            o = taken[0] if at is None else at
            taken[0] = o + n
            assert taken[0] <= 18 * 1024
            ap = arena[:, o:o + n]
            if len(shape) == 2:
                return ap.rearrange("p (a b) -> p a b", a=shape[0])
            if len(shape) == 3:
                return ap.rearrange("p (a b c) -> p a b c", a=shape[0], b=shape[1])
            return ap

        WL = sb("WL", [128, 2, W_ALL])
        RL = sb("RL", [128, 2, R_ALL])
        RT = sb("RT", [128, 2, 4, E])
        xc = sb("xc", [T, D])
        xsT = sb("xsT", [D, T])
        sq = part(2, INNER)
        ss = sb("ss", [T, 2, NH])
        rn = sb("rn", [T, 2, NH])
        rh = sb("rh", [T, 2, NH])
        qn = part(2, INNER)
        rc = part(2, INNER)
        rs = part(2, INNER)
        qT = part(8, T)
        kbd = part(8, 2, T)
        v = part(INNER)
        mx = sb("mx", [T, NH])
        nm = sb("nm", [T, NH])
        prob = part(NH, T)
        psums = sb("psums", [T, NH])
        rsum = sb("rsum", [T, NH])
        probT = part(NH, T)
        on = part(INNER)
        oT = part(8, T)

        R0 = sb("R0", [128, R0_ALL])
        W0 = sb("W0", [128, W0_ALL])
        CO = sb("CO", [128, C_ALL])
        CX = sb("CX", [DC + 1, B, S2])
        b2m = sb("b2m_sb", [NE, D])
        tm8 = sb("tm8", [T, B], U8)
        vm8 = sb("vm8", [1, B * S2], U8)
        tm = sb("tm", [T, B])
        vm = sb("vm", [1, B, S2])
        ones = sb("ones", [1, 128])
        tg = sb("tg", [128, 4])
        KF = sb("KF", [128, 3, 128])
        CB = sb("CB", [T, B, NE])
        N1 = sb("N1", [T, 11])
        N2 = sb("N2", [T, 11])

        def w0(name, n=None, k=128):
            o, m = W0_AT[name]
            return W0[0:k, o:o + (n or m)]

        def r0(name):
            o, m = R0_AT[name]
            return R0[:, o:o + m]

        def co(name, i=0):
            o, m = C_AT[name]
            return CO[:, o + i:o + i + 1]

        MW1 = part(NE, FE, at=0)
        MW2 = part(NE, 4, 128, at=4096)
        FO = part(B, 2 * D, at=8192)
        U = part(B, D, at=12288)
        f0 = 14336
        sP, sT1, sT2 = part(128, NJ, at=f0), part(128, NJ, at=f0 + 2048), part(128, NJ, at=8192)
        sQ, sQ2, sQ3, sQc = part(128, NI, at=8192 + 2048), part(128, NI, at=8192 + 3072), part(128, NI, at=12288), part(128, NI, at=12288 + 1024)
        sS = XS[:].rearrange("p b d -> p (b d)")
        KS = XD[:].rearrange("p b d -> p (b d)")[:, 0:1024].rearrange("p (i d) -> p i d", i=NI)
        KT = sS[:, 15 * 128:16 * 128]
        ax, axT, aqT = part(D, at=f0), part(T, at=f0 + 128), part(T, at=f0 + 256)
        akb, work, esub, eexp = (part(H0, S2, at=f0 + 384 + 308 * i) for i in range(4))
        esel = part(H0, S2, at=f0 + 384 + 308 * 4)
        o = f0 + 384 + 308 * 5
        m8 = part(H0, 8, at=o)
        m8r = part(2, H0, 8, at=o + 700 + 140)
        es = part(H0, at=o + 32)
        ew = part(H0, at=o + 36)
        at_ = part(S2, at=o + 40)
        aT, avT = part(T, at=o + 120), part(S2, at=o + 248)
        avf = part(512, at=o + 328)
        a2, ag, ay, u1 = (sb(f"front{i}", [T, D]) for i in range(4))
        fb = sb("film_b", [T, 512])
        fm = sb("film_m", [T, 256])
        t1, t2, t3, t4 = (part(512, at=f0 + 512 * i) for i in range(4))
        Yr, Yi = part(512, at=f0 + 2048), part(512, at=f0 + 2560)
        chT = part(T, at=f0)
        cgT = part(4, T, at=f0 + 128)
        cy, cx, cx2 = part(D, at=f0 + 640), part(D, at=f0 + 768), part(D, at=f0 + 896)
        ACC = XD
        XTA = part(B, T, at=8192)
        gT = [part(4, 512, at=8192 + 2048), part(4, 512, at=12288)]
        mxT = part(T, at=f0 + 512)
        l8, e8, i8f, c0, c1, c2 = (part(NE, at=f0 + 128 + 8 * i) for i in range(6))
        i8 = part(NE, at=f0 + 200)
        ed = part(4, at=f0 + 208)
        cT = part(T, at=f0 + 256)
        dx, dxT, dqT, dk, dcx = part(D, at=0), part(T, at=128), part(T, at=256), part(S2, at=384), part(S2, at=512)
        dkb, dsub, dpr = part(H1, S2, at=1024), part(H1, S2, at=3072), part(H1, S2, at=5120)
        dpT = part(H1, T, at=7168)
        dv, do_, doT, dyb = part(D, at=9216), part(D, at=9344), part(T, at=9472), part(D, at=9600)
        dmx, dsum, dinv = part(H1, at=9728), part(H1, at=9744), part(H1, at=9760)

        pA = ctx.enter_context(nc.psum_tensor("pA", [128, 2, 512], F32))
        pB = ctx.enter_context(nc.psum_tensor("pB", [128, 2, 512], F32))
        pC = ctx.enter_context(nc.psum_tensor("pC", [128, 2, 512], F32))
        pD = ctx.enter_context(nc.psum_tensor("pD", [128, 2, 512], F32))

        def heads(p):
            return p[:].rearrange("p b (h e) -> p (b h) e", e=E)

        def blocks(p):
            return p[:].rearrange("p b (c t) -> p (b c) t", t=128)

        def flat(p):
            return p[:].rearrange("p b n -> p (b n)")

        ld = sem("ld")
        ldc = sem("ldc")
        s_w = [sem("w_even"), sem("w_odd")]
        s_zero = sem("zeroed")
        s_xd = sem("xd_ready")
        s_sh = sem("shift_attn")
        s_shf = sem("shift_ffn")
        s_out = sem("s_out")
        s_pass = sem("wait_passed")

        AP1 = steps("attn_proj_pe", ["xT", "q", "k", "v", "qT", "kT"])
        AP2 = steps("attn_core_pe", ["S0", "S1", "PT0", "PT1", "O", "oT", "y"])
        AA1 = steps("attn_proj_act", ["xsT", "q_sq", "k_sq", "v_out", "qT_out", "kT_out"])
        AA2 = steps("attn_core_act", ["exp0", "exp1", "pT0", "oT_out"])
        AV1 = steps("attn_proj_dve", ["q_ss", "k_ss", "floor"] + RSQRT + ["q_n", "k_n", "q_s", "q_r", "k_s", "k_r"])
        AV2 = steps("attn_core_dve", ["max0", "neg0", "max1", "neg1", "pT1", "rsum", "o_n", "x_out"])
        AG1 = steps("attn_proj_pool", ["xc", "q_c", "k_c"])
        AG2 = steps("attn_core_pool", ["xs"])
        GT = steps("tables_pool", ["qc", "qs", "kc", "ks"])

        NF = sb("NF", [T, 11])
        xn = sb("xn", [T, D])
        xg = sb("xg", [T, D])
        xb = sb("xb", [T, D])
        xnT = sb("xnT", [D, T])
        hb = sb("hb", [T, 2, FF])
        gg = sb("gg", [T, FF])
        mg = sb("mg", [T, FC * 128])
        mT = sb("mT", [128, FC, T])
        yb = sb("yb", [T, D])
        FV1 = steps("ffn_norm_dve", NORM)
        FG1 = steps("ffn_norm_pool", ["g", "b"])
        FP2 = steps("ffn_up_pe", ["xT", "h"])
        FA2 = steps("ffn_up_act", ["xT_out"])
        FV3 = steps("ffn_gate_dve", ["bias", "gated"])
        FA3 = steps("ffn_gate_act", ["gelu"])
        FP4 = steps("ffn_down_pe", ["mT", "y"])
        FA4 = steps("ffn_down_act", ["mT_out"])
        FV4 = steps("ffn_down_dve", ["yb", "x_out"])
        FG4 = steps("ffn_down_pool", ["xs"], lead=B)

        s_mw, s_kt, s_set, s_x = sem("expert_weights"), sem("kernel_turned"), sem("front_set"), sem("x_loaded")
        s_clear, s_shx = sem("cleared"), sem("shift_x1")
        s_sp, s_ks = sem("setup_pe"), sem("kernel_rows")
        V1a = steps("x0_norm_dve", NORM + ["keep"])
        P1b = steps("x0_score_pe", ["xT", "k", "Q", "S"])
        A1b = steps("x0_score_act", ["xT_out", "Q_out"])
        V1b = steps("x0_score_dve", ["kbd"])
        A1c = steps("x0_topk_act", ["work", "exp"])
        V1c = steps("x0_topk_dve", [f"{x}{r}" for r in range(TOPK // 8) for x in ("max", "rep")] + ["sub", "sel", "sum", "inv", "tm", "wt", "mean"])
        P1d = steps("x0_film_pe", ["vT", "aT", "vf", "film"])
        A1d = steps("x0_film_act", ["vT_out", "aT_out", "vf_out"])
        V1d = steps("x0_film_dve", NORM + ["fb", "u1", "u"])
        G1d = steps("x0_film_pool", ["g", "b", "fm", "fo"])
        P2a = steps("conv_pe", ["F"])
        V2a = steps("conv_dve", ["t1", "t2", "Yr", "t3", "t4", "Yi"])
        P2b = steps("conv_back_pe", ["G"])
        A2b = steps("conv_back_act", ["cv"])
        V3a = steps("f0_norm_dve", ["z1", "z", "xt"] + NORM)
        G3a = steps("f0_norm_pool", ["g", "b"])
        P3b = steps("f0_up_pe", ["hT", "h"])
        A3b = steps("f0_up_act", ["hT_out", "gelu"])
        P3c = steps("f0_down_pe", ["y"])
        V3c = steps("f0_down_dve", ["yb", "xt"] + NORM)
        G3c = steps("f0_down_pool", ["g", "b"])
        V3d = steps("f0_out_dve", ["x_out"])
        V4a = steps("moe_norm_dve", NORM)
        P4b = steps("moe_route_pe", ["xT", "lg"])
        A4b = steps("moe_route_act", ["xT_out"])
        G4b = steps("moe_route_pool", ["keep"])
        V4c = steps("moe_top_dve", ["lb", "max", "idx", "idxf", "gap", "den", "w0", "w1", "c0", "c1", "cb", "keep"])
        A4c = steps("moe_top_act", ["exp"])
        P4d = steps("moe_bias_pe", ["cT", "bb"])
        A4d = steps("moe_bias_act", ["cT_out"])
        V4d = steps("moe_bias_dve", ["acc"])
        pe_experts = [f"h{e}{c}" for c in range(4) for e in [0]]
        for e in range(1, NE + 1):
            pe_experts += ([f"h{e}{c}" for c in range(4)] if e < NE else []) + [f"y{e - 1}"]
        P4e = steps("expert_pe", pe_experts)
        A4e = steps("expert_act", [f"g{e}{c}" for e in range(NE) for c in range(4)])
        V4e = steps("expert_dve", [f"acc{e}" for e in range(NE)])
        V5a = steps("x1_norm_dve", ["x_in"] + NORM)
        P5b = steps("x1_score_pe", ["xT", "q", "k", "S"])
        A5b = steps("x1_score_act", ["xT_out", "q_out", "k_out"])
        G5b = steps("x1_score_pool", ["kbd"])
        V5c = steps("x1_soft_dve", ["max", "sub", "sum", "inv"])
        A5c = steps("x1_soft_act", ["exp"])
        G5d = steps("x1_out_pool", ["cx"])
        P5d = steps("x1_out_pe", ["v", "PT0", "PT1", "O", "oT", "y"])
        A5d = steps("x1_out_act", ["v_out", "pT0", "oT_out"])
        V5d = steps("x1_out_dve", ["pT1", "o_n", "yb", "x_out"])
        V5e = steps("x1_next_dve", NORM)
        G5e = steps("x1_next_pool", ["xs"])
        VF = steps("final_dve", ["x"])
        front = (V1a, P1b, A1b, V1b, A1c, V1c, P1d, A1d, V1d, G1d, P2a, V2a, P2b, A2b, V3a, G3a, P3b, A3b, P3c, V3c, G3c,
                 V3d, V4a, P4b, A4b, G4b, V4c, A4c, P4d, A4d, V4d, P4e, A4e, V4e, V5a, P5b, A5b, G5b, V5c, A5c, G5d, P5d, A5d, V5d, V5e, G5e, VF)

        def after(eng, last, *done):
            for S in done:
                eng.wait_ge(S.sem, S.at(S.names[-1], last))

        q = [sS[:, 128 * i:128 * i + 128] for i in range(15)]
        (dt, dta_re, dta_im, turns, cos, sin, e_re, e_im, mag, num_re, num_im, scale, dc_re, dc_im, spare) = q
        are, aim, cre, cim = w0("are"), w0("aim"), w0("cre"), w0("cim")
        SV = steps("setup_dve", SETUP, lead=0)
        SA = steps("setup_act", ["dt", "gates", "cos", "sin", "mag", "cos_i", "sin_i", "wave_j", "mag_i", "mag_j"], lead=0)

        block = ctx.enter_context(nc.Block())

        def shifted(sp, b):
            return XS[1:T, b, D // 2:D], XD[0:T - 1, b, D // 2:D]

        @block.sync
        def _(sp):
            sp.dma_start(ident[:], a["ident"]).then_inc(ldc, 16)
            sp.dma_start(xg[:], a["band"]).then_inc(ldc, 16)
            sp.dma_start(rope[:], a["rope"].rearrange("p (a b) -> p a b", a=4)).then_inc(ldc, 16)
            sp.dma_start(W0[:], a["w0"]).then_inc(ldc, 16)
            sp.dma_start(R0[:], a["r0"].partition_broadcast(128)).then_inc(ldc, 16)
            sp.dma_start(CO[:], a["cols"]).then_inc(ldc, 16)
            sp.dma_start(CX[:], a["ctx"].rearrange("p (b s) -> p b s", b=B)).then_inc(ldc, 16)
            sp.dma_start(b2m[:], a["b2m"]).then_inc(ldc, 16)
            sp.dma_start(tm8[:], a["tmask"]).then_inc(ldc, 16)
            sp.dma_start(vm8[:], a["vmask"]).then_inc(ldc, 16)
            sp.dma_start(X[:], a["x"].rearrange("b t d -> t b d")).then_inc(s_x, 16)
            sp.dma_start(MW1[:], a["mw1"].rearrange("p (e f) -> p e f", e=NE)).then_inc(s_mw, 16)
            sp.dma_start(MW2[:], a["mw2"].rearrange("p (e c d) -> p e c d", e=NE, c=4)).then_inc(s_mw, 16)
            sp.wait_ge(s_ks, 1)
            for i in range(NI):
                sp.dma_start(KT[NJ * i:NJ * i + NJ, :], KS[0:NJ, i, :]).then_inc(s_kt, 16)
            for l in range(2):
                sp.dma_start(WL[:, l, :], a["w_l1"][l]).then_inc(s_w[l], 16)
                sp.dma_start(RL[:, l, :], a["r_l1"][l].partition_broadcast(128)).then_inc(s_w[l], 16)

            def x1(u):
                if u[4]:
                    b, n = u[4]
                    sp.wait_ge(V5e.sem, V5e.at("xn", n))
                    sp.sem_inc(s_pass, 1)
                    sp.wait_ge(s_shx, n * 16 + 16)
                    dst, src = shifted(sp, b)
                    sp.sem_inc(s_pass, 1)
                    sp.dma_start(dst, src).then_inc(s_shx, 16)

            pipeline(sp, x1, 5, B, 0)

            def attn(u):
                if u[1]:
                    b, n = u[1]
                    sp.wait_ge(AV2.sem, AV2.at("x_out", n))
                    sp.sem_inc(s_pass, 1)
                    dst, src = shifted(sp, b)
                    sp.wait_ge(s_sh, n * 16 + 16)
                    sp.sem_inc(s_pass, 1)
                    sp.dma_start(dst, src).then_inc(s_sh, 16)

            def ffn(u):
                if u[3]:
                    b, n = u[3]
                    sp.wait_ge(FV4.sem, FV4.at("x_out", n))
                    sp.sem_inc(s_pass, 1)
                    dst, src = shifted(sp, b)
                    sp.wait_ge(s_shf, n * 16 + 16 * B)
                    sp.sem_inc(s_pass, 1)
                    sp.dma_start(dst, src).then_inc(s_shf, 16)

            def layer(base):
                pipeline(sp, attn, 2, B, base)
                pipeline(sp, ffn, 4, B, base)

            with sp.Fori(0, DEPTH // 2 - 1) as lp:
                for half in range(2):
                    base = lp * (2 * B) + half * B
                    layer(base)
                    sp.wait_ge(FP4.sem, FP4.at("y", base + (B - 1)))
                    sp.wait_ge(FV4.sem, FV4.at("x_out", base + (B - 1)))
                    sp.sem_inc(s_pass, 1)
                    sp.dma_start(WL[:, half, :], a["w_l1"][lp * 2 + (half + 2)]).then_inc(s_w[half], 16)
                    sp.dma_start(RL[:, half, :], a["r_l1"][lp * 2 + (half + 2)].partition_broadcast(128)).then_inc(s_w[half], 16)
            for l in range(DEPTH - 2, DEPTH):
                layer(l * B)
            n = B * DEPTH - 1
            sp.wait_ge(FV4.sem, FV4.at("x_out", n))
            for g in range(NG):
                sp.wait_ge(VF.sem, VF.at("x", g))
                sp.dma_start(out.rearrange("b t d -> t b d")[:, GB * g:GB * g + GB, :], X[:, GB * g:GB * g + GB, :]).then_inc(s_out, 16)
            sp.wait_ge(s_out, 16 * NG)
            sp.wait_ge(s_shx, 16 * (B + 1))
            sp.wait_ge(s_sh, 16 * (n + 2))
            sp.wait_ge(s_shf, 16 * (n + 1 + B))
            for half in range(2):
                sp.wait_ge(s_w[half], 32 * (DEPTH // 2))

        @block.gpsimd
        def _(pool):
            for c in (AP1, AP2, AA1, AA2, AV1, AV2, AG1, AG2, FV1, FG1, FP2, FA2, FV3, FA3, FP4, FA4, FV4, FG4):
                pool.sem_inc(c.sem, c.start())
            pool.sem_inc(s_shf, 16 * B)
            pool.sem_inc(s_sh, 16)
            pool.sem_inc(s_shx, 16)
            for c in front:
                pool.sem_inc(c.sem, c.start())
            pool.memset(ones[:], 1.0).then_inc(s_zero, 1)
            pool.memset(zeros[:], 0.0).then_inc(s_zero, 1)
            pool.memset(mg[:], 0.0).then_inc(s_zero, 1)
            pool.sem_inc(s_zero, 1)
            pool.wait_ge(s_zero, 4)
            pool.wait_ge(ldc, 16 * N_CONST)
            pool.wait_ge(s_set, 1)
            pool.memset(XS[0:1, :, D // 2:D], 0.0).then_inc(s_clear, 1)

            def x0(u):
                if u[3]:
                    b, n = u[3]
                    pool.wait_ge(V1d.sem, V1d.at("xn", n))
                    pool.wait_ge(G1d.sem, G1d.at("b", n - 1))
                    pool.tensor_tensor(ag[:], a2[:], r0("g_in"), ALU.mult).then_inc(G1d.sem, G1d.step("g"))
                    pool.wait_ge(G1d.sem, G1d.at("g", n))
                    pool.wait_ge(V1d.sem, V1d.at("u1", n - 1))
                    pool.tensor_tensor(ay[:], ag[:], r0("b_in"), ALU.add).then_inc(G1d.sem, G1d.step("b"))
                    pool.wait_ge(V1d.sem, V1d.at("fb", n))
                    pool.wait_ge(V1d.sem, V1d.at("u", n - 1))
                    mod = r0("mod").to_broadcast([T, 2 * D])
                    pool.tensor_tensor(fm[:], fb[:, 0:2 * D], mod, ALU.mult).then_inc(G1d.sem, G1d.step("fm"))
                    pool.tensor_tensor(FO[:, b, :], fb[:, 2 * D:4 * D], mod, ALU.mult).then_inc(G1d.sem, G1d.step("fo"))

            def f0(u):
                if u[2]:
                    b, n = u[2]
                    pool.wait_ge(V3c.sem, V3c.at("xn", n))
                    pool.wait_ge(G3c.sem, G3c.at("b", n - 1))
                    pool.tensor_tensor(ag[:], a2[:], r0("g_out"), ALU.mult).then_inc(G3c.sem, G3c.step("g"))
                    pool.wait_ge(G3c.sem, G3c.at("g", n))
                    pool.wait_ge(V3d.sem, V3d.at("x_out", n - 1))
                    pool.tensor_tensor(ay[:], ag[:], r0("b_out"), ALU.add).then_inc(G3c.sem, G3c.step("b"))
                if u[0]:
                    b, n = u[0]
                    pool.wait_ge(V3a.sem, V3a.at("xn", n))
                    pool.wait_ge(G3a.sem, G3a.at("b", n - 1))
                    pool.tensor_tensor(cx2[:], cx[:], r0("g_ffn"), ALU.mult).then_inc(G3a.sem, G3a.step("g"))
                    pool.wait_ge(G3a.sem, G3a.at("g", n))
                    pool.wait_ge(P3b.sem, P3b.at("hT", n - 1))
                    pool.tensor_tensor(cy[:], cx2[:], r0("b_ffn"), ALU.add).then_inc(G3a.sem, G3a.step("b"))

            def route(u):
                if u[1]:
                    b, n = u[1]
                    pool.wait_ge(A4b.sem, A4b.at("xT_out", n))
                    pool.tensor_tensor(XTA[:, b, :], mxT[:], zeros[:], ALU.add).then_inc(G4b.sem, G4b.step("keep"))

            def x1(u):
                if u[4]:
                    b, n = u[4]
                    pool.wait_ge(V5e.sem, V5e.at("xn", n))
                    pool.tensor_tensor(XS[:, b, 0:D // 2], XD[:, b, 0:D // 2], zeros[:, 0:D // 2], ALU.add).then_inc(G5e.sem, G5e.step("xs"))
                if u[3]:
                    b, n = u[3]
                    pool.wait_ge(P5d.sem, P5d.at("v", n - 1))
                    pool.tensor_tensor(dcx[0:DC + 1, :], CX[:, b, :], zeros[0:DC + 1, 0:S2], ALU.add).then_inc(G5d.sem, G5d.step("cx"))
                if u[1]:
                    b, n = u[1]
                    pool.wait_ge(A5b.sem, A5b.at("k_out", n))
                    pool.wait_ge(P5b.sem, P5b.at("S", n - 1))
                    pool.tensor_tensor(dkb[:], dk[:].unsqueeze(1).to_broadcast([128, H1, S2]), w0("hm1").unsqueeze(2).to_broadcast([128, H1, S2]),
                                       ALU.mult).then_inc(G5b.sem, G5b.step("kbd"))

            pipeline(pool, x0, 4, B, 0)
            after(pool, NG - 1, A2b)
            pipeline(pool, f0, 4, B, 0)
            after(pool, B - 1, V3d)
            pipeline(pool, route, 4, B, 0)
            after(pool, NG - 1, V4e)
            pipeline(pool, x1, 5, B, 0)
            after(pool, B - 1, V5e)
            pool.memset(kbd[:], 0.0).then_inc(s_clear, 1)
            pool.wait_ge(s_shx, 16 * (B + 1))
            pool.sem_inc(s_clear, 1)
            pool.wait_ge(s_clear, 3)

            def tables(half, lp, n):
                pool.wait_ge(s_w[half], lp * 32 + 32)
                for j, (name, o) in enumerate([("qc", R_QS), ("qs", R_QS + E), ("kc", R_KS), ("ks", R_KS + E)]):
                    pool.tensor_tensor(RT[:, half, j, :], rope[:, j, :], RL[:, half, o:o + E], ALU.mult).then_inc(GT.sem, GT.step(name))

            def attn(half):
                def body(u):
                    if u[0]:
                        b, n = u[0]
                        pool.wait_ge(AP1.sem, AP1.at("xT", n - 1))
                        pool.wait_ge(s_shf, n * 16 + 16)
                        pool.wait_ge(FG4.sem, FG4.at("xs", n - B))
                        pool.tensor_tensor(xc[:], XS[:, b, :], zeros[:], ALU.add).then_inc(AG1.sem, AG1.step("xc"))
                        for j, (name, qk) in enumerate([("q_c", "q"), ("k_c", "k")]):
                            pool.wait_ge(AV1.sem, AV1.at(f"{qk}_n", n))
                            r3 = rc[:, j, :].rearrange("p (h e) -> p h e", e=E)
                            q3 = qn[:, j, :].rearrange("p (h e) -> p h e", e=E)
                            cs = RT[:, half, 2 * j, :].unsqueeze(1).to_broadcast([T, NH, E])
                            pool.tensor_tensor(r3, q3, cs, ALU.mult).then_inc(AG1.sem, AG1.step(name))
                    if u[1]:
                        b, n = u[1]
                        pool.wait_ge(AV2.sem, AV2.at("x_out", n))
                        pool.tensor_tensor(XS[:, b, 0:D // 2], XD[:, b, 0:D // 2], zeros[:, 0:D // 2], ALU.add).then_inc(AG2.sem, AG2.step("xs"))
                return body

            def ffn(half):
                def body(u):
                    if u[3]:
                        b, n = u[3]
                        pool.wait_ge(FV4.sem, FV4.at("x_out", n))
                        pool.tensor_tensor(XS[:, b, 0:D // 2], XD[:, b, 0:D // 2], zeros[:, 0:D // 2], ALU.add).then_inc(FG4.sem, FG4.step("xs"))
                    if u[0]:
                        b, n = u[0]
                        pool.wait_ge(FG1.sem, FG1.at("b", n - 1))
                        pool.wait_ge(FV1.sem, FV1.at("xn", n))
                        pool.tensor_tensor(xg[:], xn[:], RL[:, half, R_G:R_G + D], ALU.mult).then_inc(FG1.sem, FG1.step("g"))
                        pool.wait_ge(FG1.sem, FG1.at("g", n))
                        pool.wait_ge(FP2.sem, FP2.at("xT", n - 1))
                        pool.tensor_tensor(xb[:], xg[:], RL[:, half, R_B:R_B + D], ALU.add).then_inc(FG1.sem, FG1.step("b"))
                return body

            with pool.Fori(0, DEPTH // 2) as lp:
                for half in range(2):
                    base = lp * (2 * B) + half * B
                    tables(half, lp, lp)
                    pipeline(pool, attn(half), 2, B, base)
                    pipeline(pool, ffn(half), 4, B, base)

        @block.tensor
        def _(pe):
            pe.wait_ge(s_zero, 4)
            pe.wait_ge(ldc, 16 * N_CONST)
            pe.wait_ge(SV.sem, SV.at("power_j", 0))
            for d in range(128):
                ins = pe.matmul(pA[0:NJ, d // 64, (d % 64) * NI:(d % 64) * NI + NI], sP[:, d, :], sQc[:, d, :], start=True, stop=True)
            ins.then_inc(s_sp, 1)
            pe.wait_ge(s_kt, 16 * NI)
            pe.matmul(pB[:, 0, 0:128], w0("Fc"), KT, start=True, stop=True)
            pe.matmul(pB[:, 0, 128:256], w0("Fs"), KT, start=True, stop=True).then_inc(s_sp, 1)
            pe.wait_ge(s_set, 1)

            def x0(u):
                if u[3]:
                    b, n = u[3]
                    pe.wait_ge(A1d.sem, A1d.at("vT_out", n - 1))
                    pe.wait_ge(A1d.sem, A1d.at("aT_out", n - 1))
                    pe.matmul(pC[:, 0, 0:S2], w0("v0", k=DC), CX[0:DC, b, :], start=True, stop=True).then_inc(P1d.sem, P1d.step("vT"))
                    pe.wait_ge(V1c.sem, V1c.at("mean", n))
                    pe.wait_ge(A1d.sem, A1d.at("vT_out", n))
                    pe.transpose(pC[0:S2, 0, 128:256], at_, ident[:]).then_inc(P1d.sem, P1d.step("aT"))
                    pe.wait_ge(A1d.sem, A1d.at("vf_out", n - 1))
                    pe.matmul(pC[0:S2, 1, :], avT, w0("film"), start=True, stop=True).then_inc(P1d.sem, P1d.step("vf"))
                    pe.wait_ge(A1d.sem, A1d.at("vf_out", n))
                    pe.wait_ge(V1d.sem, V1d.at("fb", n - 1))
                    pe.matmul(pD[:, 0, :], aT[0:S2, :], avf[0:S2, :], start=True, stop=True).then_inc(P1d.sem, P1d.step("film"))
                if u[1]:
                    b, n = u[1]
                    pe.wait_ge(V1a.sem, V1a.at("xn", n))
                    pe.wait_ge(A1b.sem, A1b.at("xT_out", n - 1))
                    pe.transpose(pA[:, 0, 0:T], ax, ident[:]).then_inc(P1b.sem, P1b.step("xT"))
                    pe.wait_ge(V1b.sem, V1b.at("kbd", n - 1))
                    pe.matmul(pB[:, 0, 0:S2], w0("k0", k=DC), CX[0:DC, b, :], start=True, stop=True).then_inc(P1b.sem, P1b.step("k"))
                    pe.wait_ge(A1b.sem, A1b.at("xT_out", n))
                    pe.wait_ge(A1b.sem, A1b.at("Q_out", n - 1))
                    pe.matmul(pA[:, 1, 0:T], w0("Wq"), axT, start=True, stop=True).then_inc(P1b.sem, P1b.step("Q"))
                    pe.wait_ge(V1c.sem, V1c.at("sub", n - 1))
                    pe.wait_ge(A1c.sem, A1c.at("work", n - 1))
                    pe.matmul(pB[:, 1, 0:H0 * S2], ones[:], vm[:, b, :].unsqueeze(1).to_broadcast([1, H0, S2]), start=True, stop=False)
                    pe.wait_ge(A1b.sem, A1b.at("Q_out", n))
                    pe.wait_ge(V1b.sem, V1b.at("kbd", n))
                    pe.matmul(pB[:, 1, 0:H0 * S2], aqT, akb.rearrange("p h s -> p (h s)"), start=False, stop=True).then_inc(P1b.sem, P1b.step("S"))

            def conv(u):
                if u[1]:
                    c, n = u[1]
                    pe.wait_ge(V2a.sem, V2a.at("Yi", n))
                    pe.wait_ge(A2b.sem, A2b.at("cv", n - 1))
                    pe.matmul(pB[:, 0, :], w0("Gc"), Yr, start=True, stop=False)
                    pe.matmul(pB[:, 0, :], w0("Gs"), Yi, start=False, stop=True).then_inc(P2b.sem, P2b.step("G"))
                if u[0]:
                    c, n = u[0]
                    uc = U[:, bass.ts(c, GB), :].rearrange("p b d -> p (b d)")
                    pe.wait_ge(V2a.sem, V2a.at("t4", n - 1))
                    pe.matmul(pA[:, 0, :], w0("Fc"), uc, start=True, stop=True)
                    pe.matmul(pA[:, 1, :], w0("Fs"), uc, start=True, stop=True).then_inc(P2a.sem, P2a.step("F"))

            def f0(u):
                if u[2]:
                    b, n = u[2]
                    pe.wait_ge(A3b.sem, A3b.at("gelu", n))
                    pe.wait_ge(V3c.sem, V3c.at("yb", n - 1))
                    for c in range(4):
                        ins = pe.matmul(pC[:, 0, 0:D], cgT[:, c, :], w0("W2")[:, 128 * c:128 * c + 128], start=(c == 0), stop=(c == 3))
                    ins.then_inc(P3c.sem, P3c.step("y"))
                if u[1]:
                    b, n = u[1]
                    pe.wait_ge(G3a.sem, G3a.at("b", n))
                    pe.wait_ge(A3b.sem, A3b.at("hT_out", n - 1))
                    pe.transpose(pA[:, 0, 0:T], cy, ident[:]).then_inc(P3b.sem, P3b.step("hT"))
                    pe.wait_ge(A3b.sem, A3b.at("hT_out", n))
                    pe.wait_ge(A3b.sem, A3b.at("gelu", n - 1))
                    for c in range(4):
                        ins = pe.matmul(pB[:, 0, 128 * c:128 * c + 128], w0("W1")[:, 128 * c:128 * c + 128], chT, start=True, stop=True)
                    ins.then_inc(P3b.sem, P3b.step("h"))

            def route(u):
                if u[3]:
                    b, n = u[3]
                    pe.wait_ge(V4c.sem, V4c.at("cb", n))
                    pe.wait_ge(A4d.sem, A4d.at("cT_out", n - 1))
                    pe.transpose(pC[0:NE, 0, 0:128], c2, ident[:]).then_inc(P4d.sem, P4d.step("cT"))
                    pe.wait_ge(A4d.sem, A4d.at("cT_out", n))
                    pe.wait_ge(V4d.sem, V4d.at("acc", n - 1))
                    pe.matmul(pC[:, 1, 0:D], cT[0:NE, :], b2m[:], start=True, stop=True).then_inc(P4d.sem, P4d.step("bb"))
                if u[1]:
                    b, n = u[1]
                    pe.wait_ge(V4a.sem, V4a.at("xn", n))
                    pe.wait_ge(A4b.sem, A4b.at("xT_out", n - 1))
                    pe.transpose(pA[:, 0, 0:T], ax, ident[:]).then_inc(P4b.sem, P4b.step("xT"))
                    pe.wait_ge(A4b.sem, A4b.at("xT_out", n))
                    pe.wait_ge(V4c.sem, V4c.at("lb", n - 1))
                    pe.matmul(pA[:, 1, 0:NE], mxT, w0("Wr"), start=True, stop=True).then_inc(P4b.sem, P4b.step("lg"))

            def up(g, n, e):
                xt = XTA[:, bass.ts(g, GB), :].rearrange("p b t -> p (b t)")
                for c in range(4):
                    pe.wait_ge(A4e.sem, A4e.at(f"g{(e - 1) % NE}{c}", n - (e == 0)))
                    pe.matmul((pA, pB)[c // 2][:, c % 2, :], MW1[:, e, 128 * c:128 * c + 128], xt, start=True, stop=True).then_inc(P4e.sem, P4e.step(f"h{e}{c}"))

            def down(g, n, e):
                pe.wait_ge(A4e.sem, A4e.at(f"g{e}3", n))
                pe.wait_ge(V4e.sem, V4e.at(f"acc{(e - 2) % NE}", n - (e < 2)))
                for t in range(GB):
                    for c in range(4):
                        ins = pe.matmul(pC[:, e % 2, 128 * t:128 * t + 128], gT[e % 2][:, c, 128 * t:128 * t + 128], MW2[:, e, c, :],
                                        start=(c == 0), stop=(c == 3))
                ins.then_inc(P4e.sem, P4e.step(f"y{e}"))

            def x1(u):
                if u[3]:
                    b, n = u[3]
                    pe.wait_ge(G5d.sem, G5d.at("cx", n))
                    pe.wait_ge(V5d.sem, V5d.at("yb", n - 1))
                    pe.matmul(pD[0:S2, 1, 0:128], dcx[0:DC + 1, :], w0("v1", k=DC + 1), start=True, stop=True).then_inc(P5d.sem, P5d.step("v"))
                    for g in range(2):
                        if g == 0:
                            pe.wait_ge(A5c.sem, A5c.at("exp", n))
                            pe.wait_ge(V5d.sem, V5d.at("pT1", n - 1))
                        else:
                            pe.wait_ge(A5d.sem, A5d.at("pT0", n))
                        for c in range(8):
                            ins = pe.transpose(blocks(pB)[0:S2, c, :], dpr[:, 8 * g + c, :], ident[:])
                        ins.then_inc(P5d.sem, P5d.step(f"PT{g}"))
                    pe.wait_ge(A5d.sem, A5d.at("v_out", n))
                    pe.wait_ge(V5d.sem, V5d.at("pT1", n))
                    for h in range(H1):
                        ins = pe.matmul(pD[:, 1, DH1 * h:DH1 * h + DH1], dpT[0:S2, h, :], dv[0:S2, DH1 * h:DH1 * h + DH1], start=True, stop=True)
                    ins.then_inc(P5d.sem, P5d.step("O"))
                    pe.wait_ge(V5d.sem, V5d.at("o_n", n))
                    pe.transpose(pD[:, 1, 128:256], do_, ident[:]).then_inc(P5d.sem, P5d.step("oT"))
                    pe.wait_ge(A5d.sem, A5d.at("oT_out", n))
                    pe.matmul(pD[:, 1, 256:384], doT, w0("wo1"), start=True, stop=True).then_inc(P5d.sem, P5d.step("y"))
                if u[1]:
                    b, n = u[1]
                    pe.wait_ge(V5a.sem, V5a.at("xn", n))
                    pe.wait_ge(A5b.sem, A5b.at("xT_out", n - 1))
                    pe.transpose(pA[:, 0, 0:T], dx, ident[:]).then_inc(P5b.sem, P5b.step("xT"))
                    pe.wait_ge(A5b.sem, A5b.at("xT_out", n))
                    pe.wait_ge(A5b.sem, A5b.at("k_out", n - 1))
                    pe.matmul(pA[:, 1, 0:128], w0("wq1"), dxT, start=True, stop=True).then_inc(P5b.sem, P5b.step("q"))
                    pe.wait_ge(A5b.sem, A5b.at("q_out", n))
                    pe.matmul(pA[:, 1, 128:128 + S2], w0("k1", k=DC + 1), CX[:, b, :], start=True, stop=True).then_inc(P5b.sem, P5b.step("k"))
                    pe.wait_ge(G5b.sem, G5b.at("kbd", n))
                    pe.wait_ge(V5c.sem, V5c.at("sub", n - 1))
                    for (h, m), p in zip(SPANS, (pC[:, 0, :], pC[:, 1, :], pD[:, 0, :])):
                        ins = pe.matmul(p[:, 0:m * S2], dqT, dkb[:, h:h + m, :].rearrange("p h s -> p (h s)"), start=True, stop=True)
                    ins.then_inc(P5b.sem, P5b.step("S"))

            pipeline(pe, x0, 4, B, 0)
            after(pe, B - 1, V1d)
            pipeline(pe, conv, 2, NG, 0)
            after(pe, NG - 1, A2b)
            pipeline(pe, f0, 4, B, 0)
            after(pe, B - 1, V3d)
            pipeline(pe, route, 4, B, 0)
            after(pe, B - 1, V4d, G4b)
            pe.wait_ge(s_mw, 32)
            with pe.Fori(0, NG) as g:
                up(g, g, 0)
                for e in range(1, NE + 1):
                    if e < NE:
                        up(g, g, e)
                    down(g, g, e - 1)
            after(pe, NG - 1, V4e)
            pipeline(pe, x1, 5, B, 0)
            after(pe, B - 1, V5e)
            pe.wait_ge(s_clear, 3)

            def attn(half):
                def proj(n, name, p, part, free):
                    for c in range(2):
                        o = W_QKV + part * INNER + 512 * c
                        ins = pe.matmul(p[:, c, :], xsT[:], WL[:, half, o:o + 512], start=True, stop=True)
                    ins.then_inc(AP1.sem, AP1.step(name))

                def scores(n, g, p):
                    for c in range(2):
                        pe.matmul(p[:, c, :], identb[:], band[:].rearrange("p a b -> p (a b)"), start=True, stop=False, skip_group_check=True)
                        for j in range(2):
                            h2 = 4 * g + 2 * c + j
                            ins = pe.matmul(p[:, c, 256 * j:256 * j + 256], qT[:, h2, :],
                                            kbd[:, h2, :, :].rearrange("p a t -> p (a t)"), start=False, stop=(j == 1), skip_group_check=True)
                    ins.then_inc(AP2.sem, AP2.step(f"S{g}"))

                def turn(p, src):
                    for c in range(8):
                        ins = pe.transpose(blocks(p)[:, c, :], src(c), ident[:])
                    return ins

                def body(u):
                    if u[1]:
                        b, n = u[1]
                        pe.wait_ge(AA1.sem, AA1.at("kT_out", n))
                        pe.wait_ge(AA2.sem, AA2.at("oT_out", n - 1))
                        pe.wait_ge(AV2.sem, AV2.at("x_out", n - 1))
                        scores(n, 0, pA)
                    if u[0]:
                        b, n = u[0]
                        pe.wait_ge(AG1.sem, AG1.at("xc", n))
                        pe.wait_ge(AA1.sem, AA1.at("kT_out", n - 1))
                        pe.transpose(pD[:, 0, 0:T], xc[:], ident[:]).then_inc(AP1.sem, AP1.step("xT"))
                        pe.wait_ge(AA1.sem, AA1.at("xsT", n))
                        proj(n, "q", pB, 0, None)
                    if u[1]:
                        b, n = u[1]
                        scores(n, 1, pC)
                    if u[0]:
                        b, n = u[0]
                        proj(n, "k", pD, 1, None)
                    if u[1]:
                        b, n = u[1]
                        pe.wait_ge(AA2.sem, AA2.at("exp0", n))
                        turn(pA, lambda c: prob[:, c, :]).then_inc(AP2.sem, AP2.step("PT0"))
                        pe.wait_ge(AA2.sem, AA2.at("exp1", n))
                        turn(pC, lambda c: prob[:, 8 + c, :]).then_inc(AP2.sem, AP2.step("PT1"))
                        pe.wait_ge(AA2.sem, AA2.at("pT0", n))
                        pe.wait_ge(AV2.sem, AV2.at("pT1", n))
                        for h in range(NH):
                            ins = pe.matmul(heads(pA)[:, h, :], probT[:, h, :], v[:, h * E:(h + 1) * E], start=True, stop=True)
                        ins.then_inc(AP2.sem, AP2.step("O"))
                    if u[0]:
                        b, n = u[0]
                        proj(n, "v", pC, 2, None)
                        pe.wait_ge(AV1.sem, AV1.at("q_r", n))
                        turn(pB, lambda c: rc[:, 0, 128 * c:128 * c + 128]).then_inc(AP1.sem, AP1.step("qT"))
                    if u[1]:
                        b, n = u[1]
                        pe.wait_ge(AV2.sem, AV2.at("o_n", n))
                        turn(pA, lambda c: on[:, 128 * c:128 * c + 128]).then_inc(AP2.sem, AP2.step("oT"))
                    if u[0]:
                        b, n = u[0]
                        pe.wait_ge(AV1.sem, AV1.at("k_r", n))
                        turn(pD, lambda c: rc[:, 1, 128 * c:128 * c + 128]).then_inc(AP1.sem, AP1.step("kT"))
                    if u[1]:
                        b, n = u[1]
                        pe.wait_ge(AA2.sem, AA2.at("oT_out", n))
                        for c in range(8):
                            o = W_O + D * c
                            ins = pe.matmul(pA[:, 0, 0:D], oT[:, c, :], WL[:, half, o:o + D], start=(c == 0), stop=(c == 7))
                        ins.then_inc(AP2.sem, AP2.step("y"))
                return body

            def ffn(half):
                def body(u):
                    if u[3]:
                        b, n = u[3]
                        pe.wait_ge(FV3.sem, FV3.at("gated", n))
                        pe.wait_ge(FA4.sem, FA4.at("mT_out", n - 1))
                        for c in range(FC):
                            ins = pe.transpose(pC[:, 0, 128 * c:128 * c + 128], mg[:, 128 * c:128 * c + 128], ident[:])
                        ins.then_inc(FP4.sem, FP4.step("mT"))
                        pe.wait_ge(FA4.sem, FA4.at("mT_out", n))
                        pe.wait_ge(FV4.sem, FV4.at("yb", n - 1))
                        for c in range(FC):
                            o = W_2 + D * c
                            ins = pe.matmul(pC[:, 1, 0:D], mT[:, c, :], WL[:, half, o:o + D], start=(c == 0), stop=(c == FC - 1))
                        ins.then_inc(FP4.sem, FP4.step("y"))
                    if u[1]:
                        b, n = u[1]
                        pe.wait_ge(FG1.sem, FG1.at("b", n))
                        pe.wait_ge(FA2.sem, FA2.at("xT_out", n - 1))
                        pe.transpose(pD[:, 0, 0:T], xb[:], ident[:]).then_inc(FP2.sem, FP2.step("xT"))
                        pe.wait_ge(FA2.sem, FA2.at("xT_out", n))
                        pe.wait_ge(FV3.sem, FV3.at("bias", n - 1))
                        for c in range(2):
                            o = W_1 + FF * c
                            ins = pe.matmul(pB[:, c, 0:FF], xnT[:], WL[:, half, o:o + FF], start=True, stop=True)
                        ins.then_inc(FP2.sem, FP2.step("h"))
                return body

            with pe.Fori(0, DEPTH // 2) as lp:
                for half in range(2):
                    base = lp * (2 * B) + half * B
                    pe.wait_ge(s_w[half], lp * 32 + 32)
                    pe.wait_ge(FV4.sem, FV4.at("yb", base - 1))
                    pipeline(pe, attn(half), 2, B, base)
                    pe.wait_ge(AA1.sem, AA1.at("kT_out", base + (B - 1)))
                    pe.wait_ge(AV2.sem, AV2.at("x_out", base + (B - 1)))
                    pipeline(pe, ffn(half), 4, B, base)

        @block.scalar
        def _(act):
            def attn(u):
                def head_exp(n, g, p):
                    act.wait_ge(AV2.sem, AV2.at(f"neg{g}", n))
                    if g == 0:
                        act.wait_ge(AP2.sem, AP2.at("PT1", n - 1))
                        act.wait_ge(AV2.sem, AV2.at("rsum", n - 1))
                    for c in range(8):
                        h = 8 * g + c
                        ins = act.activation(prob[:, h, :], blocks(p)[:, c, :], ACT.Exp, bias=nm[:, h:h + 1], scale=QK_SCALE,
                                             accum_out=psums[:, h:h + 1])
                    ins.then_inc(AA2.sem, AA2.step(f"exp{g}"))

                if u[0]:
                    b, n = u[0]
                    act.wait_ge(AP1.sem, AP1.at("xT", n))
                    act.wait_ge(AP1.sem, AP1.at("v", n - 1))
                    act.copy(xsT[:], pD[:, 0, 0:T]).then_inc(AA1.sem, AA1.step("xsT"))
                    act.wait_ge(AP1.sem, AP1.at("q", n))
                    act.wait_ge(AV1.sem, AV1.at("k_ss", n - 1))
                    act.activation(sq[:, 0, :], flat(pB), ACT.Square).then_inc(AA1.sem, AA1.step("q_sq"))
                if u[1]:
                    b, n = u[1]
                    head_exp(n, 0, pA)
                if u[0]:
                    b, n = u[0]
                    act.wait_ge(AP1.sem, AP1.at("k", n))
                    act.activation(sq[:, 1, :], flat(pD), ACT.Square).then_inc(AA1.sem, AA1.step("k_sq"))
                if u[1]:
                    b, n = u[1]
                    head_exp(n, 1, pC)
                    act.wait_ge(AP2.sem, AP2.at("PT0", n))
                    act.wait_ge(AP2.sem, AP2.at("O", n - 1))
                    act.copy(probT[:, 0:8, :], blocks(pA)).then_inc(AA2.sem, AA2.step("pT0"))
                if u[0]:
                    b, n = u[0]
                    act.wait_ge(AP1.sem, AP1.at("v", n))
                    act.copy(v[:], flat(pC)).then_inc(AA1.sem, AA1.step("v_out"))
                    act.wait_ge(AP1.sem, AP1.at("qT", n))
                    act.copy(qT[:], blocks(pB)).then_inc(AA1.sem, AA1.step("qT_out"))
                if u[1]:
                    b, n = u[1]
                    act.wait_ge(AP2.sem, AP2.at("oT", n))
                    act.copy(oT[:], blocks(pA)).then_inc(AA2.sem, AA2.step("oT_out"))
                if u[0]:
                    b, n = u[0]
                    act.wait_ge(AP1.sem, AP1.at("kT", n))
                    act.copy(kbd[0:E, :, 0, :], blocks(pD)[0:E])
                    act.copy(kbd[E:2 * E, :, 1, :], blocks(pD)[E:2 * E]).then_inc(AA1.sem, AA1.step("kT_out"))

            def ffn(u):
                if u[3]:
                    b, n = u[3]
                    act.wait_ge(FP4.sem, FP4.at("mT", n))
                    act.copy(mT[:].rearrange("p a b -> p (a b)"), pC[:, 0, 0:FC * 128]).then_inc(FA4.sem, FA4.step("mT_out"))
                if u[2]:
                    b, n = u[2]
                    act.wait_ge(FV3.sem, FV3.at("bias", n))
                    act.activation(gg[:], hb[:, 1, :], ACT.Gelu).then_inc(FA3.sem, FA3.step("gelu"))
                if u[1]:
                    b, n = u[1]
                    act.wait_ge(FP2.sem, FP2.at("xT", n))
                    act.wait_ge(FP2.sem, FP2.at("h", n - 1))
                    act.copy(xnT[:], pD[:, 0, 0:T]).then_inc(FA2.sem, FA2.step("xT_out"))

            act.wait_ge(s_zero, 4)
            act.wait_ge(s_zero, 4)
            act.wait_ge(ldc, 16 * N_CONST)
            act.activation(dt, r0("log_dt"), ACT.Exp).then_inc(SA.sem, SA.step("dt"))
            act.activation(tg[:], r0("gates"), ACT.Tanh).then_inc(SA.sem, SA.step("gates"))
            act.wait_ge(SV.sem, SV.at("cos_frac", 0))
            act.activation(cos, cos, ACT.Sin, scale=TURN).then_inc(SA.sem, SA.step("cos"))
            act.wait_ge(SV.sem, SV.at("sin_frac", 0))
            act.activation(sin, sin, ACT.Sin, scale=TURN).then_inc(SA.sem, SA.step("sin"))
            act.wait_ge(SV.sem, SV.at("dta_re", 0))
            act.activation(mag, dta_re, ACT.Exp).then_inc(SA.sem, SA.step("mag"))
            act.wait_ge(SV.sem, SV.at("cos_i_frac", 0))
            act.activation(sQ2, sQ2, ACT.Sin, scale=TURN).then_inc(SA.sem, SA.step("cos_i"))
            act.wait_ge(SV.sem, SV.at("sin_i_frac", 0))
            act.activation(sQ, sQ, ACT.Sin, scale=TURN).then_inc(SA.sem, SA.step("sin_i"))
            act.wait_ge(SV.sem, SV.at("wave_j_frac", 0))
            act.activation(sT1, sT1, ACT.Sin, scale=TURN).then_inc(SA.sem, SA.step("wave_j"))
            act.wait_ge(SV.sem, SV.at("arg_i", 0))
            act.activation(sQ3, sQ3, ACT.Exp).then_inc(SA.sem, SA.step("mag_i"))
            act.wait_ge(SV.sem, SV.at("arg_j", 0))
            act.activation(sP, sP, ACT.Exp).then_inc(SA.sem, SA.step("mag_j"))
            act.wait_ge(s_set, 1)

            def x0(u):
                if u[3]:
                    b, n = u[3]
                    act.wait_ge(P1d.sem, P1d.at("vT", n))
                    act.wait_ge(P1d.sem, P1d.at("vf", n - 1))
                    act.copy(avT, pC[:, 0, 0:S2]).then_inc(A1d.sem, A1d.step("vT_out"))
                    act.wait_ge(P1d.sem, P1d.at("aT", n))
                    act.wait_ge(P1d.sem, P1d.at("film", n - 1))
                    act.copy(aT[0:S2, :], pC[0:S2, 0, 128:256]).then_inc(A1d.sem, A1d.step("aT_out"))
                    act.wait_ge(P1d.sem, P1d.at("vf", n))
                    act.copy(avf[0:S2, :], pC[0:S2, 1, :]).then_inc(A1d.sem, A1d.step("vf_out"))
                if u[2]:
                    b, n = u[2]
                    act.wait_ge(P1b.sem, P1b.at("S", n))
                    act.wait_ge(V1c.sem, V1c.at("sel", n - 1))
                    act.copy(work.rearrange("p h s -> p (h s)"), pB[:, 1, 0:H0 * S2]).then_inc(A1c.sem, A1c.step("work"))
                    act.wait_ge(V1c.sem, V1c.at("sub", n))
                    act.activation(eexp, esub, ACT.Exp).then_inc(A1c.sem, A1c.step("exp"))
                if u[1]:
                    b, n = u[1]
                    act.wait_ge(P1b.sem, P1b.at("xT", n))
                    act.wait_ge(P1b.sem, P1b.at("Q", n - 1))
                    act.copy(axT, pA[:, 0, 0:T]).then_inc(A1b.sem, A1b.step("xT_out"))
                    act.wait_ge(P1b.sem, P1b.at("Q", n))
                    act.wait_ge(P1b.sem, P1b.at("S", n - 1))
                    act.mul(aqT, pA[:, 1, 0:T], float(1.0 / np.sqrt(DH0))).then_inc(A1b.sem, A1b.step("Q_out"))

            def conv(u):
                if u[1]:
                    c, n = u[1]
                    act.wait_ge(P2b.sem, P2b.at("G", n))
                    act.copy(U[:, bass.ts(c, GB), :].rearrange("p b d -> p (b d)"), pB[:, 0, :]).then_inc(A2b.sem, A2b.step("cv"))

            def f0(u):
                if u[1]:
                    b, n = u[1]
                    act.wait_ge(P3b.sem, P3b.at("hT", n))
                    act.wait_ge(P3b.sem, P3b.at("h", n - 1))
                    act.copy(chT, pA[:, 0, 0:T]).then_inc(A3b.sem, A3b.step("hT_out"))
                    act.wait_ge(P3b.sem, P3b.at("h", n))
                    act.wait_ge(P3c.sem, P3c.at("y", n - 1))
                    for c in range(4):
                        ins = act.activation(cgT[:, c, :], pB[:, 0, 128 * c:128 * c + 128], ACT.Gelu, bias=co("b1", c))
                    ins.then_inc(A3b.sem, A3b.step("gelu"))

            def route(u):
                if u[3]:
                    b, n = u[3]
                    act.wait_ge(P4d.sem, P4d.at("cT", n))
                    act.wait_ge(P4d.sem, P4d.at("bb", n - 1))
                    act.copy(cT[0:NE, :], pC[0:NE, 0, 0:128]).then_inc(A4d.sem, A4d.step("cT_out"))
                if u[2]:
                    b, n = u[2]
                    act.wait_ge(V4c.sem, V4c.at("gap", n))
                    act.activation(ed[:, 1:2], ed[:, 0:1], ACT.Exp).then_inc(A4c.sem, A4c.step("exp"))
                if u[1]:
                    b, n = u[1]
                    act.wait_ge(P4b.sem, P4b.at("xT", n))
                    act.wait_ge(P4b.sem, P4b.at("lg", n - 1))
                    act.wait_ge(G4b.sem, G4b.at("keep", n - 1))
                    act.copy(mxT, pA[:, 0, 0:T]).then_inc(A4b.sem, A4b.step("xT_out"))

            def experts(g, n):
                for e in range(NE):
                    for c in range(4):
                        act.wait_ge(P4e.sem, P4e.at(f"h{e}{c}", n))
                        if c == 0:
                            act.wait_ge(P4e.sem, P4e.at(f"y{(e - 2) % NE}", n - (e < 2)))
                        act.activation(gT[e % 2][:, c, :], (pA, pB)[c // 2][:, c % 2, :], ACT.Gelu, bias=co("mb1", 4 * e + c)).then_inc(A4e.sem, A4e.step(f"g{e}{c}"))

            def x1(u):
                if u[3]:
                    b, n = u[3]
                    act.wait_ge(P5d.sem, P5d.at("v", n))
                    act.wait_ge(P5d.sem, P5d.at("O", n - 1))
                    act.copy(dv[0:S2, :], pD[0:S2, 1, 0:128]).then_inc(A5d.sem, A5d.step("v_out"))
                    act.wait_ge(P5d.sem, P5d.at("PT0", n))
                    act.copy(dpT[0:S2, 0:8, :], blocks(pB)[0:S2]).then_inc(A5d.sem, A5d.step("pT0"))
                    act.wait_ge(P5d.sem, P5d.at("oT", n))
                    act.wait_ge(P5d.sem, P5d.at("y", n - 1))
                    act.copy(doT, pD[:, 1, 128:256]).then_inc(A5d.sem, A5d.step("oT_out"))
                if u[2]:
                    b, n = u[2]
                    act.wait_ge(V5c.sem, V5c.at("sub", n))
                    act.wait_ge(P5d.sem, P5d.at("PT1", n - 1))
                    act.activation(dpr, dsub, ACT.Exp, scale=SCALE1).then_inc(A5c.sem, A5c.step("exp"))
                if u[1]:
                    b, n = u[1]
                    act.wait_ge(P5b.sem, P5b.at("xT", n))
                    act.wait_ge(P5b.sem, P5b.at("q", n - 1))
                    act.copy(dxT, pA[:, 0, 0:T]).then_inc(A5b.sem, A5b.step("xT_out"))
                    act.wait_ge(P5b.sem, P5b.at("q", n))
                    act.wait_ge(P5b.sem, P5b.at("S", n - 1))
                    act.add(dqT, pA[:, 1, 0:128], co("bq")).then_inc(A5b.sem, A5b.step("q_out"))
                    act.wait_ge(P5b.sem, P5b.at("k", n))
                    act.wait_ge(G5b.sem, G5b.at("kbd", n - 1))
                    act.copy(dk, pA[:, 1, 128:128 + S2]).then_inc(A5b.sem, A5b.step("k_out"))

            pipeline(act, x0, 4, B, 0)
            after(act, B - 1, V1d)
            pipeline(act, conv, 2, NG, 0)
            pipeline(act, f0, 4, B, 0)
            after(act, B - 1, V3d)
            pipeline(act, route, 4, B, 0)
            after(act, B - 1, V4d, G4b)
            with act.Fori(0, NG) as g:
                experts(g, g)
            after(act, NG - 1, V4e)
            pipeline(act, x1, 5, B, 0)
            after(act, B - 1, V5e)
            act.wait_ge(s_clear, 3)
            with act.Fori(0, DEPTH // 2) as lp:
                for half in range(2):
                    base = lp * (2 * B) + half * B
                    pipeline(act, attn, 2, B, base)
                    pipeline(act, ffn, 4, B, base)

        @block.vector
        def _(dve):
            def attn(half):
                def rot(n, j, name):
                    q4 = qn[:, j, :].rearrange("p (h two e) -> p h two e", two=2, e=E // 2)
                    s4 = rs[:, j, :].rearrange("p (h two e) -> p h two e", two=2, e=E // 2)
                    for c in range(2):
                        tab = RT[:, half, 2 * j + 1, c * (E // 2):(c + 1) * (E // 2)].unsqueeze(1).to_broadcast([T, NH, E // 2])
                        ins = dve.tensor_tensor(s4[:, :, c, :], q4[:, :, 1 - c, :], tab, ALU.mult)
                    ins.then_inc(AV1.sem, AV1.step(f"{name}_s"))
                    dve.wait_ge(AV1.sem, AV1.at(f"{name}_s", n))
                    dve.wait_ge(AG1.sem, AG1.at(f"{name}_c", n))
                    dve.tensor_tensor(rc[:, j, :], rc[:, j, :], rs[:, j, :], ALU.add).then_inc(AV1.sem, AV1.step(f"{name}_r"))

                def head_max(n, g, p):
                    dve.wait_ge(AP2.sem, AP2.at(f"S{g}", n))
                    dve.tensor_reduce(mx[:, 8 * g:8 * g + 8], blocks(p), AX.X, ALU.max).then_inc(AV2.sem, AV2.step(f"max{g}"))
                    dve.wait_ge(AV2.sem, AV2.at(f"max{g}", n))
                    dve.wait_ge(AA2.sem, AA2.at(f"exp{g}", n - 1))
                    dve.tensor_scalar(nm[:, 8 * g:8 * g + 8], mx[:, 8 * g:8 * g + 8], -QK_SCALE, None, ALU.mult).then_inc(AV2.sem, AV2.step(f"neg{g}"))

                def body(u):
                    if u[1]:
                        b, n = u[1]
                        head_max(n, 0, pA)
                    if u[0]:
                        b, n = u[0]
                        dve.wait_ge(AA1.sem, AA1.at("q_sq", n))
                        dve.tensor_reduce(ss[:, 0, :], sq[:, 0, :].rearrange("p (h e) -> p h e", e=E), AX.X, ALU.add).then_inc(AV1.sem, AV1.step("q_ss"))
                    if u[1]:
                        b, n = u[1]
                        head_max(n, 1, pC)
                    if u[0]:
                        b, n = u[0]
                        dve.wait_ge(AA1.sem, AA1.at("k_sq", n))
                        dve.tensor_reduce(ss[:, 1, :], sq[:, 1, :].rearrange("p (h e) -> p h e", e=E), AX.X, ALU.add).then_inc(AV1.sem, AV1.step("k_ss"))
                        dve.wait_ge(AV1.sem, AV1.at("k_ss", n))
                        dve.tensor_scalar(ss[:], ss[:], 1e-24, None, ALU.max).then_inc(AV1.sem, AV1.step("floor"))
                        dve.wait_ge(AV1.sem, AV1.at("floor", n))
                        rsqrt(dve, AV1, n, "", rn[:], rh[:], ss[:])
                        dve.wait_ge(AV1.sem, AV1.at(f"newton{RSQRT_STEPS - 1}", n))
                        for j, (name, p) in enumerate([("q", pB), ("k", pD)]):
                            q3 = qn[:, j, :].rearrange("p (h e) -> p h e", e=E)
                            dve.tensor_tensor(q3, heads(p), rn[:, j, :].unsqueeze(2).to_broadcast([T, NH, E]), ALU.mult).then_inc(AV1.sem, AV1.step(f"{name}_n"))
                        dve.wait_ge(AV1.sem, AV1.at("k_n", n))
                        rot(n, 0, "q")
                        rot(n, 1, "k")
                    if u[1]:
                        b, n = u[1]
                        dve.wait_ge(AP2.sem, AP2.at("PT1", n))
                        dve.tensor_copy(probT[:, 8:16, :], blocks(pC)).then_inc(AV2.sem, AV2.step("pT1"))
                        dve.wait_ge(AA2.sem, AA2.at("exp1", n))
                        dve.reciprocal(rsum[:], psums[:]).then_inc(AV2.sem, AV2.step("rsum"))
                        dve.wait_ge(AV2.sem, AV2.at("rsum", n))
                        dve.wait_ge(AP2.sem, AP2.at("O", n))
                        dve.tensor_tensor(on[:].rearrange("p (h e) -> p h e", e=E), heads(pA), rsum[:].unsqueeze(2).to_broadcast([T, NH, E]), ALU.mult).then_inc(AV2.sem, AV2.step("o_n"))
                        dve.wait_ge(AP2.sem, AP2.at("y", n))
                        dve.tensor_tensor(XD[:, b, :], pA[:, 0, 0:D], XD[:, b, :], ALU.add).then_inc(AV2.sem, AV2.step("x_out"))
                return body

            def ffn(half):
                def body(u):
                    if u[3]:
                        b, n = u[3]
                        dve.wait_ge(FP4.sem, FP4.at("y", n))
                        dve.tensor_tensor(yb[:], pC[:, 1, 0:D], RL[:, half, R_B2:R_B2 + D], ALU.add).then_inc(FV4.sem, FV4.step("yb"))
                        dve.wait_ge(FV4.sem, FV4.at("yb", n))
                        dve.tensor_tensor(XD[:, b, :], yb[:], XD[:, b, :], ALU.add).then_inc(FV4.sem, FV4.step("x_out"))
                    if u[2]:
                        b, n = u[2]
                        dve.wait_ge(FP2.sem, FP2.at("h", n))
                        dve.tensor_tensor(hb[:], pB[:, :, 0:FF], RL[:, half, R_B1:R_B1 + 2 * FF].rearrange("p (a f) -> p a f", a=2), ALU.add).then_inc(FV3.sem, FV3.step("bias"))
                        dve.wait_ge(FA3.sem, FA3.at("gelu", n))
                        dve.wait_ge(FP4.sem, FP4.at("mT", n - 1))
                        dve.tensor_tensor(mg[:, 0:FF], hb[:, 0, :], gg[:], ALU.mult).then_inc(FV3.sem, FV3.step("gated"))
                    if u[0]:
                        b, n = u[0]
                        dve.wait_ge(s_sh, (n + 2) * 16)
                        dve.wait_ge(AG2.sem, AG2.at("xs", n))
                        dve.wait_ge(FG1.sem, FG1.at("g", n - 1))
                        normalise(dve, FV1, n, "", xn[:], XS[:, b, :], NF, s_pass)
                return body

            dve.wait_ge(s_zero, 4)
            def done(name, ins):
                ins.then_inc(SV.sem, SV.step(name))
                dve.wait_ge(SV.sem, SV.at(name, 0))

            def tt(name, out_, x, y, o):
                done(name, dve.tensor_tensor(out_, x, y, o))

            def ts(name, out_, x, s1, s2, o1, o2=None):
                done(name, dve.tensor_scalar(out_, x, s1, s2, o1, o2) if o2 else dve.tensor_scalar(out_, x, s1, s2, o1))

            def over(x, m):
                return x.unsqueeze(2).to_broadcast([128, 128, m])

            def along(x, m):
                return x.unsqueeze(1).to_broadcast([128, 128, m])

            def whole_turns_off(name, x, k):
                ts(name + "_whole", k, x, ROUND, -ROUND, ALU.add, ALU.add)
                tt(name + "_frac", x, x, k, ALU.subtract)

            dve.wait_ge(ldc, 16 * N_CONST)
            done("identb", dve.tensor_copy(identb[:], ident[:]))
            done("band", dve.tensor_copy(band[:], xg[:].unsqueeze(1).to_broadcast([128, 4, 128])))
            dve.wait_ge(SA.sem, SA.at("dt", 0))
            tt("dta_re", dta_re, dt, are, ALU.mult)
            tt("dta_im", dta_im, dt, aim, ALU.mult)
            ts("turns", turns, dta_im, float(1 / (2 * np.pi)), None, ALU.mult)
            ts("cos_turns", cos, turns, 0.25, None, ALU.add)
            whole_turns_off("cos", cos, spare)
            ts("sin_turns", sin, turns, 0.0, None, ALU.add)
            whole_turns_off("sin", sin, spare)
            dve.wait_ge(SA.sem, SA.at("mag", 0))
            tt("e_re", e_re, cos, mag, ALU.mult)
            tt("e_im", e_im, sin, mag, ALU.mult)
            ts("e_re_less_1", e_re, e_re, -1.0, None, ALU.add)
            tt("c_e_rr", num_re, cre, e_re, ALU.mult)
            tt("c_e_ii", spare, cim, e_im, ALU.mult)
            tt("num_re", num_re, num_re, spare, ALU.subtract)
            tt("c_e_ri", num_im, cre, e_im, ALU.mult)
            tt("c_e_ir", spare, cim, e_re, ALU.mult)
            tt("num_im", num_im, num_im, spare, ALU.add)
            tt("a_rr", scale, are, are, ALU.mult)
            tt("a_ii", spare, aim, aim, ALU.mult)
            tt("a_abs2", spare, scale, spare, ALU.add)
            done("a_inv", dve.reciprocal(scale, spare))
            ts("scale", scale, scale, 2.0, None, ALU.mult)
            tt("n_a_rr", dc_re, num_re, are, ALU.mult)
            tt("n_a_ii", spare, num_im, aim, ALU.mult)
            tt("dc_re_num", dc_re, dc_re, spare, ALU.add)
            tt("dc_re", dc_re, dc_re, scale, ALU.mult)
            tt("n_a_ir", dc_im, num_im, are, ALU.mult)
            tt("n_a_ri", spare, num_re, aim, ALU.mult)
            tt("dc_im_num", dc_im, dc_im, spare, ALU.subtract)
            tt("dc_im", dc_im, dc_im, scale, ALU.mult)
            ts("row_cos_0", spare, dc_re, co("m0"), None, ALU.mult)
            done("row_cos", dve.scalar_tensor_tensor(num_re, dc_im, co("-m1"), spare, ALU.mult, ALU.add))
            ts("row_sin_0", spare, dc_im, co("-m0"), None, ALU.mult)
            done("row_sin", dve.scalar_tensor_tensor(num_im, dc_re, co("-m1"), spare, ALU.mult, ALU.add))
            tt("sin_i_turns", sQ, over(turns, NI), along(w0("i"), NI), ALU.mult)
            ts("cos_i_turns", sQ2, sQ, 0.25, None, ALU.add)
            whole_turns_off("cos_i", sQ2, sQ3)
            whole_turns_off("sin_i", sQ, sQ3)
            tt("wave_j_turns", sP, over(turns, NJ), along(w0("j"), NJ), ALU.mult)
            ts("wave_j_off", sT1, sP, co("off"), None, ALU.add)
            whole_turns_off("wave_j", sT1, sT2)
            tt("arg_i", sQ3, over(dta_re, NI), along(w0("i"), NI), ALU.mult)
            tt("arg_j", sP, over(dta_re, NJ), along(w0("j"), NJ), ALU.mult)
            dve.wait_ge(SA.sem, SA.at("mag_i", 0))
            tt("cos_i_mag", sQ2, sQ2, sQ3, ALU.mult)
            tt("sin_i_mag", sQ, sQ, sQ3, ALU.mult)
            tt("row_i_cos", sQc, sQ2, over(num_re, NI), ALU.mult)
            tt("row_i_sin", sQ3, sQ, over(num_im, NI), ALU.mult)
            tt("row_i", sQc, sQc, sQ3, ALU.add)
            dve.wait_ge(SA.sem, SA.at("mag_j", 0))
            tt("power_j", sP, sP, sT1, ALU.mult)
            dve.wait_ge(s_sp, 1)
            done("rows", dve.tensor_copy(KS[0:NJ].rearrange("j i d -> j d i"), pA[0:NJ].rearrange("p b (d i) -> p (b d) i", i=NI)))
            dve.tensor_tensor(KS[0:1, 0, :], KS[0:1, 0, :], r0("dskip")[0:1], ALU.add).then_inc(s_ks, 1)
            dve.wait_ge(s_sp, 2)
            done("f_cos", dve.tensor_copy(KF[:, 0, :], pB[:, 0, 0:128]))
            ts("f_sin", KF[:, 1, :], pB[:, 0, 128:256], co("nz"), None, ALU.mult)
            ts("f_half", KF[:, 2, :], pB[:, 0, 128:256], co("z"), None, ALU.mult)
            done("f_flip", dve.scalar_tensor_tensor(KF[:, 2, :], KF[:, 0, :], co("nz"), KF[:, 2, :], ALU.mult, ALU.add))
            ts("text_mask", tm[:], tm8[:], 1.0 / H0, None, ALU.mult)
            ts("context_mask", vm[:].rearrange("p b s -> p (b s)"), vm8[:], -1.0, BIG, ALU.add, ALU.mult)
            dve.sem_inc(s_set, 1)
            dve.wait_ge(s_x, 16)

            def x0(u):
                if u[3]:
                    b, n = u[3]
                    dve.wait_ge(G1d.sem, G1d.at("g", n - 1))
                    normalise(dve, V1d, n, "", a2[:], XD[:, b, :], N2, s_pass)
                    dve.wait_ge(P1d.sem, P1d.at("film", n))
                    dve.wait_ge(G1d.sem, G1d.at("fo", n - 1))
                    dve.tensor_tensor(fb[:], pD[:, 0, :], r0("film"), ALU.add).then_inc(V1d.sem, V1d.step("fb"))
                    dve.wait_ge(G1d.sem, G1d.at("fm", n))
                    dve.scalar_tensor_tensor(u1[:], fm[:, 0:D], 1.0, ay[:], ALU.add, ALU.mult).then_inc(V1d.sem, V1d.step("u1"))
                    dve.wait_ge(V1d.sem, V1d.at("u1", n))
                    dve.tensor_tensor(U[:, b, :], u1[:], fm[:, D:2 * D], ALU.add).then_inc(V1d.sem, V1d.step("u"))
                if u[2]:
                    b, n = u[2]
                    dve.wait_ge(A1c.sem, A1c.at("work", n))
                    dve.sem_inc(s_pass, 1)
                    for r in range(TOPK // 8):
                        for h in range(H0):
                            ins = dve.max(m8r[:, r % 2, h, :] if r else m8[:, h, :], work[:, h, :])
                        ins.then_inc(V1c.sem, V1c.step(f"max{r}"))
                        dve.wait_ge(V1c.sem, V1c.at(f"max{r}", n))
                        dve.sem_inc(s_pass, 1)
                        for h in range(H0):
                            ins = dve.match_replace(work[:, h, :], m8r[:, r % 2, h, :] if r else m8[:, h, :], work[:, h, :], GONE)
                        ins.then_inc(V1c.sem, V1c.step(f"rep{r}"))
                        dve.wait_ge(V1c.sem, V1c.at(f"rep{r}", n))
                        dve.sem_inc(s_pass, 1)
                    dve.wait_ge(A1c.sem, A1c.at("exp", n - 1))
                    dve.tensor_tensor(esub, pB[:, 1, 0:H0 * S2].rearrange("p (h s) -> p h s", h=H0), m8[:, :, 0:1].to_broadcast([T, H0, S2]),
                                      ALU.subtract).then_inc(V1c.sem, V1c.step("sub"))
                    dve.wait_ge(A1c.sem, A1c.at("exp", n))
                    dve.scalar_tensor_tensor(esel, work, GONE / 2, eexp, ALU.is_le, ALU.mult).then_inc(V1c.sem, V1c.step("sel"))
                    dve.wait_ge(V1c.sem, V1c.at("sel", n))
                    dve.tensor_reduce(es, esel, AX.X, ALU.add).then_inc(V1c.sem, V1c.step("sum"))
                    dve.wait_ge(V1c.sem, V1c.at("sum", n))
                    dve.reciprocal(ew, es).then_inc(V1c.sem, V1c.step("inv"))
                    dve.wait_ge(V1c.sem, V1c.at("inv", n))
                    dve.tensor_tensor(ew, ew, tm[:, bass.ds(b, 1)].to_broadcast([T, H0]), ALU.mult).then_inc(V1c.sem, V1c.step("tm"))
                    dve.wait_ge(V1c.sem, V1c.at("tm", n))
                    dve.tensor_tensor(esel, esel, ew.unsqueeze(2).to_broadcast([T, H0, S2]), ALU.mult).then_inc(V1c.sem, V1c.step("wt"))
                    dve.wait_ge(V1c.sem, V1c.at("wt", n))
                    dve.wait_ge(P1d.sem, P1d.at("aT", n - 1))
                    dve.tensor_reduce(at_, esel.rearrange("p h s -> p s h"), AX.X, ALU.add).then_inc(V1c.sem, V1c.step("mean"))
                if u[1]:
                    b, n = u[1]
                    dve.wait_ge(P1b.sem, P1b.at("k", n))
                    dve.wait_ge(P1b.sem, P1b.at("S", n - 1))
                    dve.tensor_tensor(akb, pB[:, 0, 0:S2].unsqueeze(1).to_broadcast([128, H0, S2]), w0("hm0").unsqueeze(2).to_broadcast([128, H0, S2]),
                                      ALU.mult).then_inc(V1b.sem, V1b.step("kbd"))
                if u[0]:
                    b, n = u[0]
                    dve.wait_ge(P1b.sem, P1b.at("xT", n - 1))
                    normalise(dve, V1a, n, "", ax, X[:, b, :], N1, s_pass)
                    dve.wait_ge(V1a.sem, V1a.at("xn", n))
                    dve.tensor_copy(XD[:, b, :], ax).then_inc(V1a.sem, V1a.step("keep"))

            def conv(u):
                if u[0]:
                    c, n = u[0]
                    re, im = pA[:, 0, :].rearrange("p (b d) -> p b d", b=GB), pA[:, 1, :].rearrange("p (b d) -> p b d", b=GB)
                    K = [KF[:, i, :].unsqueeze(1).to_broadcast([128, GB, D]) for i in range(3)]
                    v4 = lambda t: t.rearrange("p (b d) -> p b d", b=GB)
                    dve.wait_ge(P2a.sem, P2a.at("F", n))
                    dve.wait_ge(V2a.sem, V2a.at("Yi", n - 1))
                    dve.tensor_tensor(v4(t1), re, K[0], ALU.mult).then_inc(V2a.sem, V2a.step("t1"))
                    dve.tensor_tensor(v4(t2), im, K[1], ALU.mult).then_inc(V2a.sem, V2a.step("t2"))
                    dve.wait_ge(V2a.sem, V2a.at("t2", n))
                    dve.wait_ge(P2b.sem, P2b.at("G", n - 1))
                    dve.tensor_tensor(Yr, t1, t2, ALU.subtract).then_inc(V2a.sem, V2a.step("Yr"))
                    dve.tensor_tensor(v4(t3), re, K[1], ALU.mult).then_inc(V2a.sem, V2a.step("t3"))
                    dve.tensor_tensor(v4(t4), im, K[2], ALU.mult).then_inc(V2a.sem, V2a.step("t4"))
                    dve.wait_ge(V2a.sem, V2a.at("t4", n))
                    dve.tensor_tensor(Yi, t3, t4, ALU.add).then_inc(V2a.sem, V2a.step("Yi"))

            def f0(u):
                if u[3]:
                    b, n = u[3]
                    dve.wait_ge(G3c.sem, G3c.at("b", n))
                    dve.scalar_tensor_tensor(X[:, b, :], ay[:], tg[:, 0:1], X[:, b, :], ALU.mult, ALU.add).then_inc(V3d.sem, V3d.step("x_out"))
                if u[2]:
                    b, n = u[2]
                    dve.wait_ge(P3c.sem, P3c.at("y", n))
                    dve.wait_ge(V3c.sem, V3c.at("xt", n - 1))
                    dve.tensor_tensor(fb[:, 0:D], pC[:, 0, 0:D], r0("b2"), ALU.add).then_inc(V3c.sem, V3c.step("yb"))
                    dve.wait_ge(V3c.sem, V3c.at("yb", n))
                    dve.wait_ge(V3c.sem, V3c.at("xn", n - 1))
                    dve.tensor_tensor(fb[:, D:2 * D], fb[:, 0:D], U[:, b, :], ALU.add).then_inc(V3c.sem, V3c.step("xt"))
                    dve.wait_ge(V3c.sem, V3c.at("xt", n))
                    dve.wait_ge(G3c.sem, G3c.at("g", n - 1))
                    normalise(dve, V3c, n, "", a2[:], fb[:, D:2 * D], N2, s_pass)
                if u[0]:
                    b, n = u[0]
                    dve.wait_ge(V3a.sem, V3a.at("z", n - 1))
                    dve.scalar_tensor_tensor(u1[:], FO[:, b, 0:D], 1.0, U[:, b, :], ALU.add, ALU.mult).then_inc(V3a.sem, V3a.step("z1"))
                    dve.wait_ge(V3a.sem, V3a.at("z1", n))
                    dve.wait_ge(V3a.sem, V3a.at("xt", n - 1))
                    dve.tensor_tensor(fm[:, 0:D], u1[:], FO[:, b, D:2 * D], ALU.add).then_inc(V3a.sem, V3a.step("z"))
                    dve.wait_ge(V3a.sem, V3a.at("z", n))
                    dve.tensor_tensor(U[:, b, :], fm[:, 0:D], XD[:, b, :], ALU.add).then_inc(V3a.sem, V3a.step("xt"))
                    dve.wait_ge(V3a.sem, V3a.at("xt", n))
                    dve.wait_ge(G3a.sem, G3a.at("g", n - 1))
                    normalise(dve, V3a, n, "", cx, U[:, b, :], N1, s_pass)

            def route(u):
                if u[3]:
                    b, n = u[3]
                    dve.wait_ge(P4d.sem, P4d.at("bb", n))
                    dve.tensor_copy(ACC[:, b, :], pC[:, 1, 0:D]).then_inc(V4d.sem, V4d.step("acc"))
                if u[2]:
                    b, n = u[2]
                    S = V4c
                    dve.wait_ge(P4b.sem, P4b.at("lg", n))
                    dve.wait_ge(S.sem, S.at("keep", n - 1))
                    dve.tensor_tensor(l8, pA[:, 1, 0:NE], r0("br"), ALU.add).then_inc(S.sem, S.step("lb"))
                    dve.wait_ge(S.sem, S.at("lb", n))
                    dve.sem_inc(s_pass, 1)
                    dve.max(e8, l8).then_inc(S.sem, S.step("max"))
                    dve.wait_ge(S.sem, S.at("max", n))
                    dve.sem_inc(s_pass, 1)
                    dve.max_index(i8.bitcast(mybir.dt.uint32), e8, l8).then_inc(S.sem, S.step("idx"))
                    dve.wait_ge(S.sem, S.at("idx", n))
                    dve.tensor_copy(i8f, i8.bitcast(mybir.dt.uint32)).then_inc(S.sem, S.step("idxf"))
                    dve.tensor_tensor(ed[:, 0:1], e8[:, 1:2], e8[:, 0:1], ALU.subtract).then_inc(S.sem, S.step("gap"))
                    dve.wait_ge(A4c.sem, A4c.at("exp", n))
                    dve.tensor_scalar(ed[:, 2:3], ed[:, 1:2], 1.0, None, ALU.add).then_inc(S.sem, S.step("den"))
                    dve.wait_ge(S.sem, S.at("den", n))
                    dve.reciprocal(ed[:, 3:4], ed[:, 2:3]).then_inc(S.sem, S.step("w0"))
                    dve.wait_ge(S.sem, S.at("w0", n))
                    dve.tensor_tensor(ed[:, 2:3], ed[:, 3:4], ed[:, 1:2], ALU.mult).then_inc(S.sem, S.step("w1"))
                    dve.wait_ge(S.sem, S.at("w1", n))
                    dve.tensor_scalar(c0, r0("experts"), i8f[:, 0:1], ed[:, 3:4], ALU.is_equal, ALU.mult).then_inc(S.sem, S.step("c0"))
                    dve.tensor_scalar(c1, r0("experts"), i8f[:, 1:2], ed[:, 2:3], ALU.is_equal, ALU.mult).then_inc(S.sem, S.step("c1"))
                    dve.wait_ge(S.sem, S.at("c1", n))
                    dve.wait_ge(P4d.sem, P4d.at("cT", n - 1))
                    dve.tensor_tensor(c2, c0, c1, ALU.add).then_inc(S.sem, S.step("cb"))
                    dve.tensor_tensor(CB[:, b, :], c0, c1, ALU.add).then_inc(S.sem, S.step("keep"))
                if u[0]:
                    b, n = u[0]
                    dve.wait_ge(P4b.sem, P4b.at("xT", n - 1))
                    normalise(dve, V4a, n, "", ax, X[:, b, :], N1, s_pass)

            def experts(g, n):
                for e in range(NE):
                    dve.wait_ge(P4e.sem, P4e.at(f"y{e}", n))
                    dve.wait_ge(V4e.sem, V4e.at(f"acc{(e - 1) % NE}", n - (e == 0)))
                    for t in range(GB):
                        b = g * GB + t
                        ins = dve.scalar_tensor_tensor(ACC[:, b, :], pC[:, e % 2, 128 * t:128 * t + 128], CB[:, b, e:e + 1], ACC[:, b, :],
                                                       ALU.mult, ALU.add)
                    ins.then_inc(V4e.sem, V4e.step(f"acc{e}"))

            def x1(u):
                if u[4]:
                    b, n = u[4]
                    dve.wait_ge(V5d.sem, V5d.at("x_out", n))
                    normalise(dve, V5e, n, "", XD[:, b, :], X[:, b, :], N2, s_pass)
                if u[3]:
                    b, n = u[3]
                    dve.wait_ge(P5d.sem, P5d.at("PT1", n))
                    dve.tensor_copy(dpT[0:S2, 8:16, :], blocks(pB)[0:S2]).then_inc(V5d.sem, V5d.step("pT1"))
                    dve.wait_ge(P5d.sem, P5d.at("O", n))
                    dve.tensor_tensor(do_.rearrange("p (h e) -> p h e", e=DH1), pD[:, 1, 0:D].rearrange("p (h e) -> p h e", e=DH1),
                                      dinv.unsqueeze(2).to_broadcast([T, H1, DH1]), ALU.mult).then_inc(V5d.sem, V5d.step("o_n"))
                    dve.wait_ge(P5d.sem, P5d.at("y", n))
                    dve.wait_ge(V5d.sem, V5d.at("x_out", n - 1))
                    dve.tensor_tensor(dyb, pD[:, 1, 256:384], r0("bo"), ALU.add).then_inc(V5d.sem, V5d.step("yb"))
                    dve.wait_ge(V5d.sem, V5d.at("yb", n))
                    dve.scalar_tensor_tensor(X[:, b, :], dyb, tg[:, 2:3], X[:, b, :], ALU.mult, ALU.add).then_inc(V5d.sem, V5d.step("x_out"))
                if u[2]:
                    b, n = u[2]
                    dve.wait_ge(P5b.sem, P5b.at("S", n))
                    dve.wait_ge(V5c.sem, V5c.at("sub", n - 1))
                    for (h, m), p in zip(SPANS, (pC[:, 0, :], pC[:, 1, :], pD[:, 0, :])):
                        ins = dve.tensor_reduce(dmx[:, h:h + m], p[:, 0:m * S2].rearrange("p (h s) -> p h s", s=S2), AX.X, ALU.max)
                    ins.then_inc(V5c.sem, V5c.step("max"))
                    dve.wait_ge(V5c.sem, V5c.at("max", n))
                    dve.wait_ge(A5c.sem, A5c.at("exp", n - 1))
                    for (h, m), p in zip(SPANS, (pC[:, 0, :], pC[:, 1, :], pD[:, 0, :])):
                        ins = dve.tensor_tensor(dsub[:, h:h + m, :], p[:, 0:m * S2].rearrange("p (h s) -> p h s", s=S2),
                                                dmx[:, h:h + m].unsqueeze(2).to_broadcast([T, m, S2]), ALU.subtract)
                    ins.then_inc(V5c.sem, V5c.step("sub"))
                    dve.wait_ge(A5c.sem, A5c.at("exp", n))
                    dve.tensor_reduce(dsum, dpr, AX.X, ALU.add).then_inc(V5c.sem, V5c.step("sum"))
                    dve.wait_ge(V5c.sem, V5c.at("sum", n))
                    dve.wait_ge(V5d.sem, V5d.at("o_n", n - 1))
                    dve.reciprocal(dinv, dsum).then_inc(V5c.sem, V5c.step("inv"))
                if u[0]:
                    b, n = u[0]
                    dve.scalar_tensor_tensor(X[:, b, :], ACC[:, b, :], tg[:, 1:2], X[:, b, :], ALU.mult, ALU.add).then_inc(V5a.sem, V5a.step("x_in"))
                    dve.wait_ge(V5a.sem, V5a.at("x_in", n))
                    dve.wait_ge(P5b.sem, P5b.at("xT", n - 1))
                    normalise(dve, V5a, n, "", dx, X[:, b, :], N1, s_pass)

            pipeline(dve, x0, 4, B, 0)
            pipeline(dve, conv, 2, NG, 0)
            after(dve, NG - 1, A2b)
            pipeline(dve, f0, 4, B, 0)
            after(dve, B - 1, V3d)
            pipeline(dve, route, 4, B, 0)
            after(dve, B - 1, V4d)
            with dve.Fori(0, NG) as g:
                experts(g, g)
            after(dve, NG - 1, V4e)
            pipeline(dve, x1, 5, B, 0)
            after(dve, B - 1, V5e)
            dve.wait_ge(s_clear, 3)
            with dve.Fori(0, DEPTH // 2) as lp:
                for half in range(2):
                    base = lp * (2 * B) + half * B
                    dve.wait_ge(GT.sem, (lp * 2 + (half + 1)) * 4)
                    dve.wait_ge(s_w[half], lp * 32 + 32)
                    pipeline(dve, attn(half), 2, B, base)
                    pipeline(dve, ffn(half), 4, B, base)
            after(dve, B * DEPTH - 1, FV4)
            for g in range(NG):
                at = slice(GB * g, GB * g + GB)
                dve.scalar_tensor_tensor(X[:, at, :], XD[:, at, :], tg[:, 3:4], X[:, at, :], ALU.mult, ALU.add).then_inc(VF.sem, VF.step("x"))


def rope_tables():
    half = np.arange(0, E, 2, dtype=np.float32)
    inv_freq = (1.0 / 10000.0 ** (half / E)).astype(np.float32)
    t = np.arange(T, dtype=np.float32)
    f = t[:, None] * inv_freq[None, :]
    f = np.concatenate([f, f], -1).astype(np.float32)
    base = (half + 0.4 * E) / (1.4 * E)
    power = (t - T // 2) / (WINDOW // 2)
    s = base[None, :] ** power[:, None]
    s = np.concatenate([s, s], -1)
    sign = np.concatenate([-np.ones(E // 2), np.ones(E // 2)])
    c, sn = np.cos(f), np.sin(f) * sign
    return np.stack([c * s, sn * s, c / s, sn / s], 1).reshape(T, 4 * E).astype(np.float32)


def constants():
    i, j = np.arange(T)[:, None], np.arange(T)[None, :]
    band = np.where((j <= i) & (j >= i - WINDOW), 0.0, BIG16).astype(np.float32)
    return {
        "ident": np.eye(128, dtype=np.float32),
        "band": band,
        "rope": rope_tables(),
    }


def layout(inputs):
    w = {k: np.asarray(x) for k, x in inputs.items()}
    wall = np.zeros((DEPTH, 128, W_ALL), np.float32)
    wall[:, :, W_QKV:W_O] = w["L1_ffn_Wqkv"]
    wall[:, :, W_O:W_1] = w["L1_ffn_Wo"].reshape(DEPTH, 8, 128, D).transpose(0, 2, 1, 3).reshape(DEPTH, 128, 8 * D)
    wall[:, :, W_1:W_2] = w["L1_ffn_W1"]
    w2 = np.zeros((DEPTH, FC * 128, D), np.float32)
    w2[:, :FF] = w["L1_ffn_W2"]
    wall[:, :, W_2:] = w2.reshape(DEPTH, FC, 128, D).transpose(0, 2, 1, 3).reshape(DEPTH, 128, FC * D)
    swap = lambda s: np.concatenate([s[:, E // 2:], s[:, :E // 2]], 1)
    qs, ks = w["L1_ffn_q_scale"], w["L1_ffn_k_scale"]
    rall = np.concatenate([w["L1_ffn_ln_g"], w["L1_ffn_ln_b"], w["L1_ffn_b1"], w["L1_ffn_b2"], qs, swap(qs), ks, swap(ks)], 1)
    def rows(x, k=128):
        y = np.zeros((k, x.shape[1]), np.float32)
        y[:x.shape[0]] = x
        return y

    f, t = np.arange(128.0)[:, None], np.arange(128.0)[None, :]
    ang = 2 * np.pi * f * t / 256
    Fc, Fs, Gc, Gs = np.cos(ang).T.copy(), -np.sin(ang).T.copy(), np.cos(ang) / 128, -np.sin(ang) / 128
    sign = (-1.0) ** np.arange(128)
    Fs[:, 0], Gc[0], Gs[0] = sign, 1 / 256, sign / 256
    twice = lambda m: np.concatenate([m.T, m.T], 0)
    hm = lambda h: np.repeat(np.eye(h), 128 // h, 0)
    l0 = lambda k: w["L0_xattn_" + k]
    l1 = lambda k: w["L1_xattn_" + k]
    parts = {
        "Wq": l0("Wq"), "film": np.concatenate([l0("W_film_in"), l0("W_film_out")], 1), "W1": l0("W1"),
        "W2": l0("W2").reshape(4, 128, D).transpose(1, 0, 2).reshape(128, 4 * D), "Wr": w["L0_ffn_Wr"], "wq1": l1("wq"), "wo1": l1("wo"),
        "k0": rows(l0("Wk")), "v0": rows(l0("Wv")), "k1": rows(np.concatenate([l1("wk"), l1("bk")[None]], 0)),
        "v1": rows(np.concatenate([l1("wv"), l1("bv")[None]], 0)), "Fc": Fc, "Fs": Fs, "Gc": Gc, "Gs": Gs,
        "are": twice(l0("A_re")), "aim": twice(l0("A_im")), "cre": twice(l0("C_re")), "cim": twice(l0("C_im")), "hm0": hm(H0), "hm1": hm(H1),
        "j": np.tile(np.arange(NJ), (128, 1)), "i": np.tile(np.arange(NI) * NJ, (128, 1)),
    }
    w0 = np.concatenate([parts[k].astype(np.float32) for k in W0_AT], 1)
    parts = {
        "g_in": l0("g_norm_in"), "b_in": l0("b_norm_in"), "g_ffn": l0("g_ffn"), "b_ffn": l0("b_ffn"), "g_out": l0("g_norm_out"),
        "b_out": l0("b_norm_out"), "b2": l0("b2"), "film": np.concatenate([l0("b_film_in"), l0("b_film_out")]), "br": w["L0_ffn_br"], "bo": l1("bo"),
        "gates": np.stack([w["g_xattn"][0], w["g_ffn"][0], w["g_xattn"][1], w["g_ffn"][1]]), "mod": l0("mod_gate").reshape(1),
        "log_dt": l0("log_dt"), "dskip": l0("D_skip"), "experts": np.arange(NE),
    }
    r0 = np.concatenate([parts[k].astype(np.float32) for k in R0_AT])
    m0 = (np.arange(128) < NS).astype(np.float32)[:, None]
    z = (np.arange(128) == 0).astype(np.float32)[:, None]
    parts = {"b1": l0("b1").reshape(4, 128).T, "bq": l1("bq")[:, None], "mb1": w["L0_ffn_b1"].reshape(4 * NE, 128).T,
             "m0": m0, "m1": 1 - m0, "-m0": -m0, "-m1": m0 - 1, "off": 0.25 * m0, "nz": 1 - z, "z": z}
    cols = np.concatenate([parts[k].astype(np.float32) for k in C_AT], 1)
    ctx = np.ones((DC + 1, B * S2), np.float32)
    ctx[:DC] = w["ctx_768"].transpose(2, 0, 1).reshape(DC, B * S2)
    return {"w_l1": wall, "r_l1": rall, "w0": w0, "r0": r0, "cols": cols, "ctx": ctx, "b2m": w["L0_ffn_b2"],
            "mw1": w["L0_ffn_W1"].transpose(1, 0, 2).reshape(128, NE * FE),
            "mw2": w["L0_ffn_W2"].reshape(NE, 4, 128, D).transpose(2, 0, 1, 3).reshape(128, NE * 4 * D),
            "tmask": w["mask_BxS_bf1"].T.view(np.uint8), "vmask": w["mask_BxS2_bf1"].reshape(1, B * S2).view(np.uint8),
            "x": w["x"]}


def kernel(**inputs):
    import concourse.bacc as _bacc
    from concourse.bass_utils import run_bass_kernel_spmd

    arrays = dict(constants(), **layout(inputs))
    arrays = {name: np.ascontiguousarray(x) for name, x in arrays.items()}
    nc = _bacc.Bacc("TRN2", target_bir_lowering=False, num_devices=1)
    a = {name: nc.dram_tensor(name, x.shape, mybir.dt.from_np(x.dtype), kind="ExternalInput").ap() for name, x in arrays.items()}
    out = nc.dram_tensor("out", (B, T, D), F32, kind="ExternalOutput").ap()
    flamingo(nc, a, out)
    r = run_bass_kernel_spmd(nc, [arrays], core_ids=[0])
    return r.results[0]["out"]
```

```python
from contextlib import ExitStack

import numpy as np

import concourse.bass as bass
from concourse import mybir

F32 = mybir.dt.float32
I32 = mybir.dt.int32
U8 = mybir.dt.uint8
BF16 = mybir.dt.bfloat16
ALU = mybir.AluOpType
ACT = mybir.ActivationFunctionType
AX = mybir.AxisListType

B = 16
T = 128
D = 128
S2 = 77
DC = 96
EPS = 1e-5
BIG = 1.0e30
BIG16 = -(2.0 ** 100)
GONE = -3.0e38

H0, DH0 = 4, 32
TOPK = 32
HID = 4 * D
NS = 64
NJ, NI = 16, 8
TURN = 6.283185
ROUND = 1.5 * 2.0 ** 23
NE, FE = 8, 512
GB = 4
NG = B // GB
H1, DH1 = 16, 8
SCALE1 = float(1.0 / np.sqrt(DH1))
SPANS = [(0, 5), (5, 5), (10, 6)]

DEPTH = 6
NH = 16
E = 64
WINDOW = 32
INNER = NH * E
FF = int(D * 4 * 2 / 3)
QK_SCALE = 8.0
FC = 3
W_QKV, W_O, W_1, W_2 = 0, 3 * INNER, 3 * INNER + INNER, 3 * INNER + INNER + 2 * FF
W_ALL = W_2 + FC * D
R_G, R_B, R_B1, R_B2, R_QS, R_KS = 0, D, 2 * D, 2 * D + 2 * FF, 3 * D + 2 * FF, 3 * D + 2 * FF + 2 * E
R_ALL = R_KS + 2 * E
UNITS = B * DEPTH
STAGES = 8

def offsets(*sizes):
    at, o = {}, 0
    for name, n in sizes:
        at[name] = (o, n)
        o += n
    return at, o


N_CONST = 10 + DEPTH
R0_AT, R0_ALL = offsets(("g_in", D), ("b_in", D), ("g_ffn", D), ("b_ffn", D), ("g_out", D), ("b_out", D), ("b2", D), ("film", 4 * D),
                        ("br", NE), ("bo", D), ("gates", 4), ("mod", 1), ("log_dt", D), ("dskip", D), ("experts", NE))
W0_AT, W0_ALL = offsets(("Wq", 128), ("film", 512), ("W1", HID), ("W2", HID), ("Wr", NE), ("wq1", 128), ("wo1", 128), ("k0", 128), ("v0", 128),
                        ("k1", 128), ("v1", 128), ("Fc", 128), ("Fs", 128), ("Gc", 128), ("Gs", 128), ("are", 128), ("aim", 128), ("cre", 128),
                        ("cim", 128), ("hm0", H0), ("hm1", H1), ("j", NJ), ("i", NI))
C_AT, C_ALL = offsets(("b1", 4), ("bq", 1), ("mb1", 4 * NE), ("m0", 1), ("m1", 1), ("-m0", 1), ("-m1", 1), ("off", 1), ("nz", 1), ("z", 1))

RSQRT_MAGIC = float(0x5F3759DF)
RSQRT_STEPS = 3
RSQRT = ["shift", "guess"] + [f"{s}{i}" for i in range(RSQRT_STEPS) for s in ("square", "half", "newton")]
SETUP = [
    "identb", "band",
    "dta_re", "dta_im", "turns", "cos_turns", "cos_whole", "cos_frac", "sin_turns", "sin_whole", "sin_frac", "e_re", "e_im",
    "e_re_less_1", "c_e_rr", "c_e_ii", "num_re", "c_e_ri", "c_e_ir", "num_im", "a_rr", "a_ii", "a_abs2", "a_inv", "scale", "n_a_rr",
    "n_a_ii", "dc_re_num", "dc_re", "n_a_ir", "n_a_ri", "dc_im_num", "dc_im", "row_cos_0", "row_cos", "row_sin_0", "row_sin",
    "sin_i_turns", "cos_i_turns", "cos_i_whole", "cos_i_frac", "sin_i_whole", "sin_i_frac", "wave_j_turns", "wave_j_off",
    "wave_j_whole", "wave_j_frac", "arg_i", "arg_j", "cos_i_mag", "sin_i_mag", "row_i_cos", "row_i_sin", "row_i", "power_j", "rows",
    "f_cos", "f_sin", "f_half", "f_flip", "text_mask", "context_mask",
]


class Steps:

    def __init__(self, sem, names, lead=1):
        self.sem, self.names, self.lead, self.turn = sem, names, lead, 0

    def start(self):
        return self.lead * len(self.names)

    def at(self, name, n):
        return n * len(self.names) + (self.start() + self.names.index(name) + 1)

    def step(self, name):
        assert self.names[self.turn % len(self.names)] == name, (name, self.names[self.turn % len(self.names)])
        self.turn += 1
        return 1


def pipeline(eng, body, depth, count, base):
    for t in range(depth - 1):
        body([(t - s, base + (t - s)) if s <= t else None for s in range(depth)])
    with eng.Fori(depth - 1, count) as i:
        body([(i - s, i - s + base) if s else (i, i + base) for s in range(depth)])
    for t in range(count, count + depth - 1):
        body([(t - s, base + (t - s)) if t - s < count else None for s in range(depth)])


def rsqrt(dve, S, n, pre, y, h, v):
    yi, vi = y.bitcast(I32), v.bitcast(I32)
    dve.tensor_scalar(yi, vi, 1, None, ALU.logical_shift_right).then_inc(S.sem, S.step(pre + "shift"))
    dve.wait_ge(S.sem, S.at(pre + "shift", n))
    dve.tensor_scalar(yi, yi, -1.0, RSQRT_MAGIC, ALU.mult, ALU.add).then_inc(S.sem, S.step(pre + "guess"))
    last = "guess"
    for i in range(RSQRT_STEPS):
        dve.wait_ge(S.sem, S.at(pre + last, n))
        dve.tensor_tensor(h, y, y, ALU.mult).then_inc(S.sem, S.step(pre + f"square{i}"))
        dve.wait_ge(S.sem, S.at(pre + f"square{i}", n))
        dve.scalar_tensor_tensor(h, h, -0.5, v, ALU.mult, ALU.mult).then_inc(S.sem, S.step(pre + f"half{i}"))
        dve.wait_ge(S.sem, S.at(pre + f"half{i}", n))
        dve.scalar_tensor_tensor(y, h, 1.5, y, ALU.add, ALU.mult).then_inc(S.sem, S.step(pre + f"newton{i}"))
        last = f"newton{i}"


NORM = ["stats", "aggr", "eps", "xn"]


def normalise(dve, S, G, n, out, x, N, s_pass):
    moments(dve, S, G, n, x, N, s_pass)
    centre(dve, S, G, n, out, x, N)


def moments(dve, S, G, n, x, N, s_pass):
    stats, mv, vv = N[:, 0:6], N[:, 6:8], N[:, 8:9]
    dve.sem_inc(s_pass, 1)
    dve.bn_stats(stats, x).then_inc(S.sem, S.step("stats"))
    dve.wait_ge(S.sem, S.at("stats", n))
    dve.sem_inc(s_pass, 1)
    dve.bn_aggr(mv, stats).then_inc(S.sem, S.step("aggr"))
    dve.wait_ge(S.sem, S.at("aggr", n))
    dve.wait_ge(G.sem, G.at("root", n - 1))
    dve.tensor_scalar(vv, mv[:, 1:2], EPS, None, ALU.add).then_inc(S.sem, S.step("eps"))


def root(pool, S, G, n, N, half):
    pool.wait_ge(S.sem, S.at("eps", n))
    pool.wait_ge(S.sem, S.at("xn", n - 1))
    pool.tensor_tensor(N[:, 9:10], N[:, 8:9], half, ALU.pow).then_inc(G.sem, G.step("root"))


def centre(dve, S, G, n, out, x, N):
    dve.wait_ge(G.sem, G.at("root", n))
    dve.tensor_scalar(out, x, N[:, 6:7], N[:, 9:10], ALU.subtract, ALU.mult).then_inc(S.sem, S.step("xn"))


def flamingo(nc, a, out):
    with ExitStack() as ctx:
        def sb(name, shape, dt=F32):
            return ctx.enter_context(nc.sbuf_tensor(name, shape, dt))

        def sem(name):
            return ctx.enter_context(nc.semaphore(name))

        def steps(name, names, lead=1):
            return Steps(sem(name), names, lead)

        X = sb("X", [T, B, D])
        XD = sb("XD", [T, B, D])
        XS = sb("XS", [T, B, D])
        ident = sb("ident_sb", [128, 128])
        zeros = sb("zeros", [128, 128])
        half = sb("minus_half", [128, 1])
        identb = sb("identb_sb", [128, 128], BF16)

        band = sb("band_sb", [128, 4, 128], BF16)
        rope = sb("rope_sb", [128, 4, E])
        arena = sb("arena", [128, 18 * 1024])
        taken = [0]

        def part(*shape, at=None):
            n = int(np.prod(shape))
            o = taken[0] if at is None else at
            taken[0] = o + n
            assert taken[0] <= 18 * 1024
            ap = arena[:, o:o + n]
            if len(shape) == 2:
                return ap.rearrange("p (a b) -> p a b", a=shape[0])
            if len(shape) == 3:
                return ap.rearrange("p (a b c) -> p a b c", a=shape[0], b=shape[1])
            return ap

        WL = sb("WL", [128, 2, W_ALL])
        RL = sb("RL", [128, 2, R_ALL])
        RT = sb("RT", [128, DEPTH + 1, 4 * E])
        xc = sb("xc", [T, D])
        xsT = sb("xsT", [D, T])
        WLf = WL[:].rearrange("p a n -> p (a n)")
        RLf = RL[:].rearrange("p a n -> p (a n)")
        RTf = RT[:].rearrange("p a n -> p (a n)")
        sq = part(2, INNER)
        ss = sb("ss", [T, 2, NH])
        rn = sb("rn", [T, 2, NH])
        rh = sb("rh", [T, 2, NH])
        qn = part(2, INNER)
        rc = part(2, INNER)
        rs = part(2, INNER)
        qT = part(8, T)
        kbd = part(8, 2, T)
        v = part(INNER)
        mx = sb("mx", [T, NH])
        sc = sb("sc", [T, NH])
        warm = sb("warm", [128, 2])
        nm = sb("nm", [T, NH])
        prob = part(NH, T)
        psums = sb("psums", [T, NH])
        rsum = sb("rsum", [T, NH])
        probT = part(NH, T)
        vn = part(INNER)
        oT = part(8, T)

        R0 = sb("R0", [128, R0_ALL])
        W0 = sb("W0", [128, W0_ALL])
        CO = sb("CO", [128, C_ALL])
        CX = sb("CX", [DC + 1, B, S2])
        b2m = sb("b2m_sb", [NE, D])
        tm8 = sb("tm8", [T, B], U8)
        vm8 = sb("vm8", [1, B * S2], U8)
        tm = sb("tm", [T, B])
        vm = sb("vm", [1, B, S2])
        ones = sb("ones", [1, 128])
        tg = sb("tg", [128, 4])
        KF = sb("KF", [128, 3, 128])
        CB = sb("CB", [T, B, NE])
        N1 = sb("N1", [T, 11])
        N2 = sb("N2", [T, 11])

        def w0(name, n=None, k=128):
            o, m = W0_AT[name]
            return W0[0:k, o:o + (n or m)]

        def r0(name):
            o, m = R0_AT[name]
            return R0[:, o:o + m]

        def co(name, i=0):
            o, m = C_AT[name]
            return CO[:, o + i:o + i + 1]

        MW1 = part(NE, FE, at=0)
        MW2 = part(NE, 4, 128, at=4096)
        FO = part(B, 2 * D, at=8192)
        U = part(B, D, at=12288)
        f0 = 14336
        sP, sT1, sT2 = part(128, NJ, at=f0), part(128, NJ, at=f0 + 2048), part(128, NJ, at=8192)
        sQ, sQ2, sQ3, sQc = part(128, NI, at=8192 + 2048), part(128, NI, at=8192 + 3072), part(128, NI, at=12288), part(128, NI, at=12288 + 1024)
        sS = XS[:].rearrange("p b d -> p (b d)")
        KS = XD[:].rearrange("p b d -> p (b d)")[:, 0:1024].rearrange("p (i d) -> p i d", i=NI)
        KT = sS[:, 15 * 128:16 * 128]
        ax, axT, aqT = part(D, at=f0), part(T, at=f0 + 128), part(T, at=f0 + 256)
        akb, work, esub, eexp = (part(H0, S2, at=f0 + 384 + 308 * i) for i in range(4))
        esel = part(H0, S2, at=f0 + 384 + 308 * 4)
        o = f0 + 384 + 308 * 5
        m8 = part(H0, 8, at=o)
        m8r = part(2, H0, 8, at=o + 700 + 140)
        es = part(H0, at=o + 32)
        ew = part(H0, at=o + 36)
        at_ = part(S2, at=o + 40)
        aT, avT = part(T, at=o + 120), part(S2, at=o + 248)
        avf = part(512, at=o + 328)
        fm = sb("film_m", [T, 256])
        t1, t2, t3, t4 = (part(512, at=f0 + 512 * i) for i in range(4))
        Yr, Yi = part(512, at=f0 + 2048), part(512, at=f0 + 2560)
        chT = part(T, at=f0)
        cgT = part(4, T, at=f0 + 128)
        cy, cx, cx2 = part(D, at=f0 + 640), part(D, at=f0 + 768), part(D, at=f0 + 896)
        ACC = XD
        XTA = part(B, T, at=8192)
        gT = [part(4, 512, at=8192 + 2048), part(4, 512, at=12288)]
        mxT = part(T, at=f0 + 512)
        l8, e8, i8f, c0, c1, c2 = (part(NE, at=f0 + 128 + 8 * i) for i in range(6))
        i8 = part(NE, at=f0 + 200)
        ed = part(4, at=f0 + 208)
        cT = part(T, at=f0 + 256)
        dx, dxT, dqT, dk, dcx = part(D, at=0), part(T, at=128), part(T, at=256), part(S2, at=384), part(S2, at=512)
        dkb, dsub, dpr = part(H1, S2, at=1024), part(H1, S2, at=3072), part(H1, S2, at=5120)
        dpT = part(H1, T, at=7168)
        dv, do_, doT, dyb = part(D, at=9216), part(D, at=9344), part(T, at=9472), part(D, at=9600)
        dmx, dsum, dinv = part(H1, at=9728), part(H1, at=9744), part(H1, at=9760)

        pA = ctx.enter_context(nc.psum_tensor("pA", [128, 2, 512], F32))
        pB = ctx.enter_context(nc.psum_tensor("pB", [128, 2, 512], F32))
        pC = ctx.enter_context(nc.psum_tensor("pC", [128, 2, 512], F32))
        pD = ctx.enter_context(nc.psum_tensor("pD", [128, 2, 512], F32))

        def heads(p):
            return p[:].rearrange("p b (h e) -> p (b h) e", e=E)

        def blocks(p):
            return p[:].rearrange("p b (c t) -> p (b c) t", t=128)

        def flat(p):
            return p[:].rearrange("p b n -> p (b n)")

        ld = sem("ld")
        ldc = sem("ldc")
        s_w = [sem("w_even"), sem("w_odd")]
        s_zero = sem("zeroed")
        s_xd = sem("xd_ready")
        s_sh = sem("shift_attn")
        s_shf = sem("shift_ffn")
        s_out = sem("s_out")
        s_layer = sem("layer_loaded")
        s_pass = sem("wait_passed")

        def stack_steps(name, names):
            return steps(name, names, lead=STAGES)

        AP1 = stack_steps("attn_proj_pe", ["xT", "q", "k", "v", "qT", "kT"])
        AP2 = stack_steps("attn_score_pe", ["S0", "S1"])
        AP3 = stack_steps("attn_value_pe", ["PT0", "PT1", "O", "y"])
        AA1 = stack_steps("attn_proj_act", ["xsT", "q_out", "k_out", "k_sq", "v_out", "qT_out", "kT_out"])
        AA2 = stack_steps("attn_score_act", ["exp0", "exp1"])
        AA3 = stack_steps("attn_value_act", ["pT0", "oT_out"])
        AW = stack_steps("tables_warm", ["exp", "gelu"])
        AV1 = stack_steps("attn_proj_dve", ["q_s", "k_s", "k_ss", "q_r", "q_ss", "floor"] + RSQRT + ["k_r", "k_n", "kT_out"])
        AV2 = stack_steps("attn_score_dve", ["max0", "scale", "neg0", "max1", "neg1", "rsum0", "rsum1"])
        AV3 = stack_steps("attn_value_dve", ["pT1", "x_out"])
        AG0 = stack_steps("attn_in_pool", ["xc"])
        AG1 = stack_steps("attn_proj_pool", ["q_c", "k_c", "q_sq"])
        AG2 = stack_steps("attn_score_pool", ["v", "p0", "p1"])
        AG3 = stack_steps("attn_value_pool", ["xs"])
        GT = steps("tables_pool", ["table"], lead=0)

        NF = sb("NF", [T, 11])
        xn = sb("xn", [T, D])
        xg = sb("xg", [T, D])
        xb = sb("xb", [T, D])
        xnT = sb("xnT", [D, T])
        hb = sb("hb", [T, 2, FF])
        gg = sb("gg", [T, FF])
        mg = sb("mg", [T, FC * 128])
        mT = sb("mT", [128, FC, T])
        yb = sb("yb", [T, D])
        a2, ag, ay, u1 = xn, xnT, xsT, yb
        fb = hb[:].rearrange("p a f -> p (a f)")[:, 0:4 * D]
        FV1 = stack_steps("ffn_norm_dve", NORM)
        FG0 = stack_steps("ffn_root_pool", ["root"])
        FG1 = stack_steps("ffn_norm_pool", ["g", "b"])
        FP2 = stack_steps("ffn_up_pe", ["xT", "h"])
        FA2 = stack_steps("ffn_up_act", ["xT_out"])
        FV2 = stack_steps("ffn_up_dve", ["bias"])
        FV3 = stack_steps("ffn_gate_dve", ["gated"])
        FA3 = stack_steps("ffn_gate_act", ["gelu"])
        FP4 = stack_steps("ffn_down_pe", ["mT", "y"])
        FA4 = stack_steps("ffn_down_act", ["mT_out"])
        FV4 = stack_steps("ffn_down_dve", ["yb", "x_out"])
        FG4 = steps("ffn_down_pool", ["xs"], lead=B)

        s_mw, s_kt, s_set, s_x = sem("expert_weights"), sem("kernel_turned"), sem("front_set"), sem("x_loaded")
        s_clear, s_shx = sem("cleared"), sem("shift_x1")
        s_sp, s_ks = sem("setup_pe"), sem("kernel_rows")
        V1a = steps("x0_norm_dve", NORM + ["keep"])
        P1b = steps("x0_score_pe", ["xT", "k", "Q", "S"])
        A1b = steps("x0_score_act", ["xT_out", "Q_out"])
        V1b = steps("x0_score_dve", ["kbd"])
        A1c = steps("x0_topk_act", ["work", "exp"])
        V1c = steps("x0_topk_dve", [f"{x}{r}" for r in range(TOPK // 8) for x in ("max", "rep")] + ["sub", "sel", "sum", "inv", "tm", "wt", "mean"])
        P1d = steps("x0_film_pe", ["vT", "aT", "vf", "film"])
        A1d = steps("x0_film_act", ["vT_out", "aT_out", "vf_out"])
        V1d = steps("x0_film_dve", NORM + ["fb", "u1", "u"])
        G1d = steps("x0_film_pool", ["g", "b", "fm", "fo"])
        P2a = steps("conv_pe", ["F"])
        V2a = steps("conv_dve", ["t1", "t2", "Yr", "t3", "t4", "Yi"])
        P2b = steps("conv_back_pe", ["G"])
        A2b = steps("conv_back_act", ["cv"])
        V3a = steps("f0_norm_dve", ["z1", "z", "xt"] + NORM)
        G3a = steps("f0_norm_pool", ["g", "b"])
        P3b = steps("f0_up_pe", ["hT", "h"])
        A3b = steps("f0_up_act", ["hT_out", "gelu"])
        P3c = steps("f0_down_pe", ["y"])
        V3c = steps("f0_down_dve", ["yb", "xt"] + NORM)
        G3c = steps("f0_down_pool", ["g", "b"])
        V3d = steps("f0_out_dve", ["x_out"])
        V4a = steps("moe_norm_dve", NORM)
        P4b = steps("moe_route_pe", ["xT", "lg"])
        A4b = steps("moe_route_act", ["xT_out"])
        G4b = steps("moe_route_pool", ["keep"])
        V4c = steps("moe_top_dve", ["lb", "max", "idx", "idxf", "gap", "den", "w0", "w1", "c0", "c1", "cb", "keep"])
        A4c = steps("moe_top_act", ["exp"])
        P4d = steps("moe_bias_pe", ["cT", "bb"])
        A4d = steps("moe_bias_act", ["cT_out"])
        V4d = steps("moe_bias_dve", ["acc"])
        pe_experts = [f"h{e}{c}" for c in range(4) for e in [0]]
        for e in range(1, NE + 1):
            pe_experts += ([f"h{e}{c}" for c in range(4)] if e < NE else []) + [f"y{e - 1}"]
        P4e = steps("expert_pe", pe_experts)
        A4e = steps("expert_act", [f"g{e}{c}" for e in range(NE) for c in range(4)])
        V4e = steps("expert_dve", [f"acc{e}" for e in range(NE)])
        V5a = steps("x1_norm_dve", ["x_in"] + NORM)
        P5b = steps("x1_score_pe", ["xT", "q", "k", "S"])
        A5b = steps("x1_score_act", ["xT_out", "q_out", "k_out"])
        G5b = steps("x1_score_pool", ["kbd"])
        V5c = steps("x1_soft_dve", ["max", "sub", "sum", "inv"])
        A5c = steps("x1_soft_act", ["exp"])
        G5d = steps("x1_out_pool", ["cx"])
        P5d = steps("x1_out_pe", ["v", "PT0", "PT1", "O", "oT", "y"])
        A5d = steps("x1_out_act", ["v_out", "pT0", "oT_out"])
        V5d = steps("x1_out_dve", ["pT1", "o_n", "yb", "x_out"])
        V5e = steps("x1_next_dve", NORM)
        G5e = steps("x1_next_pool", ["xs"])
        VF = steps("final_dve", ["x"])
        N1a, N1d, N3a, N3c, N4a, N5a, N5e = (steps(f"{x}_root", ["root"]) for x in ("x0_in", "x0_norm", "f0_in", "f0_norm", "moe", "x1", "x1_next"))
        front = (V1a, P1b, A1b, V1b, A1c, V1c, P1d, A1d, V1d, G1d, P2a, V2a, P2b, A2b, V3a, G3a, P3b, A3b, P3c, V3c, G3c,
                 V3d, V4a, P4b, A4b, G4b, V4c, A4c, P4d, A4d, V4d, P4e, A4e, V4e, V5a, P5b, A5b, G5b, V5c, A5c, G5d, P5d, A5d, V5d, V5e, G5e, VF,
                 N1a, N1d, N3a, N3c, N4a, N5a, N5e)

        def after(eng, last, *done):
            for S in done:
                eng.wait_ge(S.sem, S.at(S.names[-1], last))

        q = [sS[:, 128 * i:128 * i + 128] for i in range(15)]
        (dt, dta_re, dta_im, turns, cos, sin, e_re, e_im, mag, num_re, num_im, scale, dc_re, dc_im, spare) = q
        are, aim, cre, cim = w0("are"), w0("aim"), w0("cre"), w0("cim")
        SV = steps("setup_dve", SETUP, lead=0)
        SA = steps("setup_act", ["dt", "gates", "cos", "sin", "mag", "cos_i", "sin_i", "wave_j", "mag_i", "mag_j"], lead=0)

        block = ctx.enter_context(nc.Block())

        def value(eng, x):
            return x if isinstance(x, int) else eng.snap(x)

        def of_unit(eng, n):
            return value(eng, n & (B - 1)), (n >> 4) & 1

        assert B == 16

        def shifted(sp, b):
            return XS[1:T, b, D // 2:D], XD[0:T - 1, b, D // 2:D]

        @block.sync
        def _(sp):
            sp.dma_start(ident[:], a["ident"]).then_inc(ldc, 16)
            sp.dma_start(xg[:], a["band"]).then_inc(ldc, 16)
            for l in range(DEPTH):
                sp.dma_start(RT[:, l, :], a["r_l1"][l, R_QS:R_ALL].partition_broadcast(128)).then_inc(ldc, 16)
            sp.dma_start(rope[:], a["rope"].rearrange("p (a b) -> p a b", a=4)).then_inc(ldc, 16)
            sp.dma_start(W0[:], a["w0"]).then_inc(ldc, 16)
            sp.dma_start(R0[:], a["r0"].partition_broadcast(128)).then_inc(ldc, 16)
            sp.dma_start(CO[:], a["cols"]).then_inc(ldc, 16)
            sp.dma_start(CX[:], a["ctx"].rearrange("p (b s) -> p b s", b=B)).then_inc(ldc, 16)
            sp.dma_start(b2m[:], a["b2m"]).then_inc(ldc, 16)
            sp.dma_start(tm8[:], a["tmask"]).then_inc(ldc, 16)
            sp.dma_start(vm8[:], a["vmask"]).then_inc(ldc, 16)
            sp.dma_start(X[:], a["x"].rearrange("b t d -> t b d")).then_inc(s_x, 16)
            sp.dma_start(MW1[:], a["mw1"].rearrange("p (e f) -> p e f", e=NE)).then_inc(s_mw, 16)
            sp.dma_start(MW2[:], a["mw2"].rearrange("p (e c d) -> p e c d", e=NE, c=4)).then_inc(s_mw, 16)
            sp.wait_ge(s_ks, 1)
            for i in range(NI):
                sp.dma_start(KT[NJ * i:NJ * i + NJ, :], KS[0:NJ, i, :]).then_inc(s_kt, 16)
            for l in range(2):
                sp.dma_start(WL[:, l, :], a["w_l1"][l]).then_inc(s_w[l], 16)
                sp.dma_start(RL[:, l, :], a["r_l1"][l].partition_broadcast(128)).then_inc(s_w[l], 16)

            def x1(u):
                if u[4]:
                    b, n = u[4]
                    sp.wait_ge(V5e.sem, V5e.at("xn", n))
                    sp.sem_inc(s_pass, 1)
                    sp.wait_ge(s_shx, n * 16 + 16)
                    dst, src = shifted(sp, b)
                    sp.sem_inc(s_pass, 1)
                    sp.dma_start(dst, src).then_inc(s_shx, 16)

            pipeline(sp, x1, 5, B, 0)

            for l in range(2):
                sp.wait_ge(s_w[l], 32)
                sp.sem_inc(s_layer, 1)

            def attn_shift(b, n):
                sp.wait_ge(AV3.sem, AV3.at("x_out", n))
                sp.sem_inc(s_pass, 1)
                dst, src = shifted(sp, b)
                sp.wait_ge(s_sh, n * 16 + 16)
                sp.sem_inc(s_pass, 1)
                sp.dma_start(dst, src).then_inc(s_sh, 16)

            def ffn_shift(b, n):
                sp.wait_ge(FV4.sem, FV4.at("x_out", n))
                sp.sem_inc(s_pass, 1)
                dst, src = shifted(sp, b)
                sp.wait_ge(s_shf, n * 16 + 16 * B)
                sp.sem_inc(s_pass, 1)
                sp.dma_start(dst, src).then_inc(s_shf, 16)

            AHEAD = 4
            for n in range(AHEAD):
                attn_shift(n, n)

            def shifts(base, first, last):
                with sp.Fori(first, last) as b:
                    attn_shift(sp.snap((b + AHEAD) & (B - 1)), b + (base + AHEAD))
                    ffn_shift(b, b + base)

            with sp.Fori(0, DEPTH // 2 - 1) as lp:
                for l in range(2):
                    base = sp.snap(lp * (2 * B) + l * B)
                    shifts(base, 0, B)
                    sp.wait_ge(FP4.sem, FP4.at("y", base + (B - 1)))
                    sp.sem_inc(s_pass, 1)
                    sp.dma_start(WL[:, l, :], a["w_l1"][lp * 2 + (l + 2)]).then_inc(s_w[l], 16)
                    sp.dma_start(RL[:, l, :], a["r_l1"][lp * 2 + (l + 2)].partition_broadcast(128)).then_inc(s_w[l], 16)
                    sp.wait_ge(s_w[l], lp * 32 + 64)
                    sp.sem_inc(s_layer, 1)
            shifts((DEPTH - 2) * B, 0, B)
            shifts((DEPTH - 1) * B, 0, B - AHEAD)
            n = UNITS - 1
            for m in range(UNITS - AHEAD, UNITS):
                ffn_shift(m & (B - 1), m)
            for g in range(NG):
                sp.wait_ge(VF.sem, VF.at("x", g))
                sp.dma_start(out.rearrange("b t d -> t b d")[:, GB * g:GB * g + GB, :], X[:, GB * g:GB * g + GB, :]).then_inc(s_out, 16)
            sp.wait_ge(s_out, 16 * NG)
            sp.wait_ge(s_shx, 16 * (B + 1))
            sp.wait_ge(s_sh, 16 * (n + 2))
            sp.wait_ge(s_shf, 16 * (n + 1 + B))
            for l in range(2):
                sp.wait_ge(s_w[l], 32 * (DEPTH // 2))

        @block.gpsimd
        def _(pool):
            for c in (AP1, AP2, AP3, AA1, AA2, AA3, AW, AV1, AV2, AV3, AG0, AG1, AG2, AG3, FV1, FG0, FG1, FP2, FA2, FV2, FV3, FA3, FP4, FA4, FV4, FG4):
                pool.sem_inc(c.sem, c.start())
            pool.sem_inc(s_shf, 16 * B)
            pool.sem_inc(s_sh, 16)
            pool.sem_inc(s_shx, 16)
            for c in front:
                pool.sem_inc(c.sem, c.start())
            pool.memset(ones[:], 1.0).then_inc(s_zero, 1)
            pool.memset(zeros[:], 0.0).then_inc(s_zero, 1)
            pool.memset(mg[:], 0.0).then_inc(s_zero, 1)
            pool.memset(half[:], -0.5).then_inc(s_zero, 1)
            pool.wait_ge(s_zero, 4)
            pool.wait_ge(ldc, 16 * N_CONST)
            pool.wait_ge(s_set, 1)
            pool.memset(XS[0:1, :, D // 2:D], 0.0).then_inc(s_clear, 1)

            def x0(u):
                if u[3]:
                    b, n = u[3]
                    root(pool, V1d, N1d, n, N2, half[:])
                    pool.wait_ge(V1d.sem, V1d.at("xn", n))
                    pool.wait_ge(G1d.sem, G1d.at("b", n - 1))
                    pool.tensor_tensor(ag[:], a2[:], r0("g_in"), ALU.mult).then_inc(G1d.sem, G1d.step("g"))
                    pool.wait_ge(G1d.sem, G1d.at("g", n))
                    pool.wait_ge(V1d.sem, V1d.at("u1", n - 1))
                    pool.tensor_tensor(ay[:], ag[:], r0("b_in"), ALU.add).then_inc(G1d.sem, G1d.step("b"))
                    pool.wait_ge(V1d.sem, V1d.at("fb", n))
                    pool.wait_ge(V1d.sem, V1d.at("u", n - 1))
                    mod = r0("mod").to_broadcast([T, 2 * D])
                    pool.tensor_tensor(fm[:], fb[:, 0:2 * D], mod, ALU.mult).then_inc(G1d.sem, G1d.step("fm"))
                    pool.tensor_tensor(FO[:, b, :], fb[:, 2 * D:4 * D], mod, ALU.mult).then_inc(G1d.sem, G1d.step("fo"))
                if u[0]:
                    b, n = u[0]
                    root(pool, V1a, N1a, n, N1, half[:])

            def f0(u):
                if u[2]:
                    b, n = u[2]
                    root(pool, V3c, N3c, n, N2, half[:])
                    pool.wait_ge(V3c.sem, V3c.at("xn", n))
                    pool.wait_ge(G3c.sem, G3c.at("b", n - 1))
                    pool.tensor_tensor(ag[:], a2[:], r0("g_out"), ALU.mult).then_inc(G3c.sem, G3c.step("g"))
                    pool.wait_ge(G3c.sem, G3c.at("g", n))
                    pool.wait_ge(V3d.sem, V3d.at("x_out", n - 1))
                    pool.tensor_tensor(ay[:], ag[:], r0("b_out"), ALU.add).then_inc(G3c.sem, G3c.step("b"))
                if u[0]:
                    b, n = u[0]
                    root(pool, V3a, N3a, n, N1, half[:])
                    pool.wait_ge(V3a.sem, V3a.at("xn", n))
                    pool.wait_ge(G3a.sem, G3a.at("b", n - 1))
                    pool.tensor_tensor(cx2[:], cx[:], r0("g_ffn"), ALU.mult).then_inc(G3a.sem, G3a.step("g"))
                    pool.wait_ge(G3a.sem, G3a.at("g", n))
                    pool.wait_ge(P3b.sem, P3b.at("hT", n - 1))
                    pool.tensor_tensor(cy[:], cx2[:], r0("b_ffn"), ALU.add).then_inc(G3a.sem, G3a.step("b"))

            def route(u):
                if u[1]:
                    b, n = u[1]
                    pool.wait_ge(A4b.sem, A4b.at("xT_out", n))
                    pool.tensor_tensor(XTA[:, b, :], mxT[:], zeros[:], ALU.add).then_inc(G4b.sem, G4b.step("keep"))
                if u[0]:
                    b, n = u[0]
                    root(pool, V4a, N4a, n, N1, half[:])

            def x1(u):
                if u[4]:
                    b, n = u[4]
                    root(pool, V5e, N5e, n, N2, half[:])
                    pool.wait_ge(V5e.sem, V5e.at("xn", n))
                    pool.tensor_tensor(XS[:, b, 0:D // 2], XD[:, b, 0:D // 2], zeros[:, 0:D // 2], ALU.add).then_inc(G5e.sem, G5e.step("xs"))
                if u[3]:
                    b, n = u[3]
                    pool.wait_ge(P5d.sem, P5d.at("v", n - 1))
                    pool.tensor_tensor(dcx[0:DC + 1, :], CX[:, b, :], zeros[0:DC + 1, 0:S2], ALU.add).then_inc(G5d.sem, G5d.step("cx"))
                if u[1]:
                    b, n = u[1]
                    pool.wait_ge(A5b.sem, A5b.at("k_out", n))
                    pool.wait_ge(P5b.sem, P5b.at("S", n - 1))
                    pool.tensor_tensor(dkb[:], dk[:].unsqueeze(1).to_broadcast([128, H1, S2]), w0("hm1").unsqueeze(2).to_broadcast([128, H1, S2]),
                                       ALU.mult).then_inc(G5b.sem, G5b.step("kbd"))
                if u[0]:
                    b, n = u[0]
                    root(pool, V5a, N5a, n, N1, half[:])

            pipeline(pool, x0, 4, B, 0)
            after(pool, NG - 1, A2b)
            pipeline(pool, f0, 4, B, 0)
            after(pool, B - 1, V3d)
            pipeline(pool, route, 4, B, 0)
            after(pool, NG - 1, V4e)
            pipeline(pool, x1, 5, B, 0)
            after(pool, B - 1, V5e)
            pool.memset(kbd[:], 0.0).then_inc(s_clear, 1)
            pool.wait_ge(s_shx, 16 * (B + 1))
            pool.sem_inc(s_clear, 1)
            pool.wait_ge(s_clear, 3)

            for l in range(DEPTH):
                pool.tensor_tensor(RT[:, l, :], rope[:].rearrange("p a e -> p (a e)"), RT[:, l, :], ALU.mult).then_inc(GT.sem, GT.step("table"))

            def stack(u):
                if u[4]:
                    n = u[4][1]
                    parity = value(pool, of_unit(pool, n)[1] * R_ALL)
                    root(pool, FV1, FG0, n, NF, half[:])
                    pool.wait_ge(FG1.sem, FG1.at("b", n - 1))
                    pool.wait_ge(FV1.sem, FV1.at("xn", n))
                    pool.tensor_tensor(xg[:], xn[:], RLf[:, bass.ds(parity + R_G, D)], ALU.mult).then_inc(FG1.sem, FG1.step("g"))
                    pool.wait_ge(FG1.sem, FG1.at("g", n))
                    pool.wait_ge(FP2.sem, FP2.at("xT", n - 1))
                    pool.tensor_tensor(xb[:], xg[:], RLf[:, bass.ds(parity + R_B, D)], ALU.add).then_inc(FG1.sem, FG1.step("b"))
                if u[1]:
                    n = u[1][1]
                    table = value(pool, (n >> 4) * (4 * E))
                    for j, (name, qk) in enumerate([("q_c", "q"), ("k_c", "k")]):
                        pool.wait_ge(AA1.sem, AA1.at(f"{qk}_out", n))
                        pool.wait_ge(AP1.sem, AP1.at(f"{qk}T", n - 1))
                        r3 = rc[:, j, :].rearrange("p (h e) -> p h e", e=E)
                        q3 = qn[:, j, :].rearrange("p (h e) -> p h e", e=E)
                        cs = RTf[:, bass.ds(table + 2 * j * E, E)].unsqueeze(1).to_broadcast([T, NH, E])
                        pool.tensor_tensor(r3, q3, cs, ALU.mult).then_inc(AG1.sem, AG1.step(name))
                    pool.wait_ge(AV1.sem, AV1.at("q_ss", n - 1))
                    pool.tensor_tensor(sq[:, 0, :], qn[:, 0, :], qn[:, 0, :], ALU.mult).then_inc(AG1.sem, AG1.step("q_sq"))
                if u[2]:
                    n = u[2][1]
                    pool.wait_ge(AP3.sem, AP3.at("O", n - 1))
                    pool.wait_ge(AA1.sem, AA1.at("v_out", n))
                    pool.tensor_tensor(v[:], vn[:], zeros[:, 0:1].to_broadcast([T, INNER]), ALU.add).then_inc(AG2.sem, AG2.step("v"))
                    for g in range(2):
                        at = slice(8 * g, 8 * g + 8)
                        pool.wait_ge(AV2.sem, AV2.at(f"rsum{g}", n))
                        pool.tensor_tensor(prob[:, at, :], prob[:, at, :], rsum[:, at].unsqueeze(2).to_broadcast([T, 8, T]), ALU.mult).then_inc(AG2.sem, AG2.step(f"p{g}"))
                if u[0]:
                    n = u[0][1]
                    b, _ = of_unit(pool, n)
                    pool.wait_ge(AP1.sem, AP1.at("xT", n - 1))
                    pool.wait_ge(s_shf, n * 16 + 16)
                    pool.wait_ge(FG4.sem, FG4.at("xs", n - B))
                    pool.tensor_tensor(xc[:], XS[:, b, :], zeros[:], ALU.add).then_inc(AG0.sem, AG0.step("xc"))
                for stage, V, G in ((7, FV4, FG4), (3, AV3, AG3)):
                    if u[stage]:
                        n = u[stage][1]
                        b, _ = of_unit(pool, n)
                        pool.wait_ge(V.sem, V.at("x_out", n))
                        pool.tensor_tensor(XS[:, b, 0:D // 2], XD[:, b, 0:D // 2], zeros[:, 0:D // 2], ALU.add).then_inc(G.sem, G.step("xs"))

            pipeline(pool, stack, STAGES, UNITS, 0)

        @block.tensor
        def _(pe):
            pe.wait_ge(s_zero, 4)
            pe.wait_ge(ldc, 16 * N_CONST)
            pe.wait_ge(SV.sem, SV.at("power_j", 0))
            for d in range(128):
                ins = pe.matmul(pA[0:NJ, d // 64, (d % 64) * NI:(d % 64) * NI + NI], sP[:, d, :], sQc[:, d, :], start=True, stop=True)
            ins.then_inc(s_sp, 1)
            pe.wait_ge(s_kt, 16 * NI)
            pe.matmul(pB[:, 0, 0:128], w0("Fc"), KT, start=True, stop=True)
            pe.matmul(pB[:, 0, 128:256], w0("Fs"), KT, start=True, stop=True).then_inc(s_sp, 1)
            pe.wait_ge(s_set, 1)

            def x0(u):
                if u[3]:
                    b, n = u[3]
                    pe.wait_ge(A1d.sem, A1d.at("vT_out", n - 1))
                    pe.wait_ge(A1d.sem, A1d.at("aT_out", n - 1))
                    pe.matmul(pC[:, 0, 0:S2], w0("v0", k=DC), CX[0:DC, b, :], start=True, stop=True).then_inc(P1d.sem, P1d.step("vT"))
                    pe.wait_ge(V1c.sem, V1c.at("mean", n))
                    pe.wait_ge(A1d.sem, A1d.at("vT_out", n))
                    pe.transpose(pC[0:S2, 0, 128:256], at_, ident[:]).then_inc(P1d.sem, P1d.step("aT"))
                    pe.wait_ge(A1d.sem, A1d.at("vf_out", n - 1))
                    pe.matmul(pC[0:S2, 1, :], avT, w0("film"), start=True, stop=True).then_inc(P1d.sem, P1d.step("vf"))
                    pe.wait_ge(A1d.sem, A1d.at("vf_out", n))
                    pe.wait_ge(V1d.sem, V1d.at("fb", n - 1))
                    pe.matmul(pD[:, 0, :], aT[0:S2, :], avf[0:S2, :], start=True, stop=True).then_inc(P1d.sem, P1d.step("film"))
                if u[1]:
                    b, n = u[1]
                    pe.wait_ge(V1a.sem, V1a.at("xn", n))
                    pe.wait_ge(A1b.sem, A1b.at("xT_out", n - 1))
                    pe.transpose(pA[:, 0, 0:T], ax, ident[:]).then_inc(P1b.sem, P1b.step("xT"))
                    pe.wait_ge(V1b.sem, V1b.at("kbd", n - 1))
                    pe.matmul(pB[:, 0, 0:S2], w0("k0", k=DC), CX[0:DC, b, :], start=True, stop=True).then_inc(P1b.sem, P1b.step("k"))
                    pe.wait_ge(A1b.sem, A1b.at("xT_out", n))
                    pe.wait_ge(A1b.sem, A1b.at("Q_out", n - 1))
                    pe.matmul(pA[:, 1, 0:T], w0("Wq"), axT, start=True, stop=True).then_inc(P1b.sem, P1b.step("Q"))
                    pe.wait_ge(V1c.sem, V1c.at("sub", n - 1))
                    pe.wait_ge(A1c.sem, A1c.at("work", n - 1))
                    pe.matmul(pB[:, 1, 0:H0 * S2], ones[:], vm[:, b, :].unsqueeze(1).to_broadcast([1, H0, S2]), start=True, stop=False)
                    pe.wait_ge(A1b.sem, A1b.at("Q_out", n))
                    pe.wait_ge(V1b.sem, V1b.at("kbd", n))
                    pe.matmul(pB[:, 1, 0:H0 * S2], aqT, akb.rearrange("p h s -> p (h s)"), start=False, stop=True).then_inc(P1b.sem, P1b.step("S"))

            def conv(u):
                if u[1]:
                    c, n = u[1]
                    pe.wait_ge(V2a.sem, V2a.at("Yi", n))
                    pe.wait_ge(A2b.sem, A2b.at("cv", n - 1))
                    pe.matmul(pB[:, 0, :], w0("Gc"), Yr, start=True, stop=False)
                    pe.matmul(pB[:, 0, :], w0("Gs"), Yi, start=False, stop=True).then_inc(P2b.sem, P2b.step("G"))
                if u[0]:
                    c, n = u[0]
                    uc = U[:, bass.ts(c, GB), :].rearrange("p b d -> p (b d)")
                    pe.wait_ge(V2a.sem, V2a.at("t4", n - 1))
                    pe.matmul(pA[:, 0, :], w0("Fc"), uc, start=True, stop=True)
                    pe.matmul(pA[:, 1, :], w0("Fs"), uc, start=True, stop=True).then_inc(P2a.sem, P2a.step("F"))

            def f0(u):
                if u[2]:
                    b, n = u[2]
                    pe.wait_ge(A3b.sem, A3b.at("gelu", n))
                    pe.wait_ge(V3c.sem, V3c.at("yb", n - 1))
                    for c in range(4):
                        ins = pe.matmul(pC[:, 0, 0:D], cgT[:, c, :], w0("W2")[:, 128 * c:128 * c + 128], start=(c == 0), stop=(c == 3))
                    ins.then_inc(P3c.sem, P3c.step("y"))
                if u[1]:
                    b, n = u[1]
                    pe.wait_ge(G3a.sem, G3a.at("b", n))
                    pe.wait_ge(A3b.sem, A3b.at("hT_out", n - 1))
                    pe.transpose(pA[:, 0, 0:T], cy, ident[:]).then_inc(P3b.sem, P3b.step("hT"))
                    pe.wait_ge(A3b.sem, A3b.at("hT_out", n))
                    pe.wait_ge(A3b.sem, A3b.at("gelu", n - 1))
                    for c in range(4):
                        ins = pe.matmul(pB[:, 0, 128 * c:128 * c + 128], w0("W1")[:, 128 * c:128 * c + 128], chT, start=True, stop=True)
                    ins.then_inc(P3b.sem, P3b.step("h"))

            def route(u):
                if u[3]:
                    b, n = u[3]
                    pe.wait_ge(V4c.sem, V4c.at("cb", n))
                    pe.wait_ge(A4d.sem, A4d.at("cT_out", n - 1))
                    pe.transpose(pC[0:NE, 0, 0:128], c2, ident[:]).then_inc(P4d.sem, P4d.step("cT"))
                    pe.wait_ge(A4d.sem, A4d.at("cT_out", n))
                    pe.wait_ge(V4d.sem, V4d.at("acc", n - 1))
                    pe.matmul(pC[:, 1, 0:D], cT[0:NE, :], b2m[:], start=True, stop=True).then_inc(P4d.sem, P4d.step("bb"))
                if u[1]:
                    b, n = u[1]
                    pe.wait_ge(V4a.sem, V4a.at("xn", n))
                    pe.wait_ge(A4b.sem, A4b.at("xT_out", n - 1))
                    pe.transpose(pA[:, 0, 0:T], ax, ident[:]).then_inc(P4b.sem, P4b.step("xT"))
                    pe.wait_ge(A4b.sem, A4b.at("xT_out", n))
                    pe.wait_ge(V4c.sem, V4c.at("lb", n - 1))
                    pe.matmul(pA[:, 1, 0:NE], mxT, w0("Wr"), start=True, stop=True).then_inc(P4b.sem, P4b.step("lg"))

            def up(g, n, e):
                xt = XTA[:, bass.ts(g, GB), :].rearrange("p b t -> p (b t)")
                for c in range(4):
                    pe.wait_ge(A4e.sem, A4e.at(f"g{(e - 1) % NE}{c}", n - (e == 0)))
                    pe.matmul((pA, pB)[c // 2][:, c % 2, :], MW1[:, e, 128 * c:128 * c + 128], xt, start=True, stop=True).then_inc(P4e.sem, P4e.step(f"h{e}{c}"))

            def down(g, n, e):
                pe.wait_ge(A4e.sem, A4e.at(f"g{e}3", n))
                pe.wait_ge(V4e.sem, V4e.at(f"acc{(e - 2) % NE}", n - (e < 2)))
                for t in range(GB):
                    for c in range(4):
                        ins = pe.matmul(pC[:, e % 2, 128 * t:128 * t + 128], gT[e % 2][:, c, 128 * t:128 * t + 128], MW2[:, e, c, :],
                                        start=(c == 0), stop=(c == 3))
                ins.then_inc(P4e.sem, P4e.step(f"y{e}"))

            def x1(u):
                if u[3]:
                    b, n = u[3]
                    pe.wait_ge(G5d.sem, G5d.at("cx", n))
                    pe.wait_ge(V5d.sem, V5d.at("yb", n - 1))
                    pe.matmul(pD[0:S2, 1, 0:128], dcx[0:DC + 1, :], w0("v1", k=DC + 1), start=True, stop=True).then_inc(P5d.sem, P5d.step("v"))
                    for g in range(2):
                        if g == 0:
                            pe.wait_ge(A5c.sem, A5c.at("exp", n))
                            pe.wait_ge(V5d.sem, V5d.at("pT1", n - 1))
                        else:
                            pe.wait_ge(A5d.sem, A5d.at("pT0", n))
                        for c in range(8):
                            ins = pe.transpose(blocks(pB)[0:S2, c, :], dpr[:, 8 * g + c, :], ident[:])
                        ins.then_inc(P5d.sem, P5d.step(f"PT{g}"))
                    pe.wait_ge(A5d.sem, A5d.at("v_out", n))
                    pe.wait_ge(V5d.sem, V5d.at("pT1", n))
                    for h in range(H1):
                        ins = pe.matmul(pD[:, 1, DH1 * h:DH1 * h + DH1], dpT[0:S2, h, :], dv[0:S2, DH1 * h:DH1 * h + DH1], start=True, stop=True)
                    ins.then_inc(P5d.sem, P5d.step("O"))
                    pe.wait_ge(V5d.sem, V5d.at("o_n", n))
                    pe.transpose(pD[:, 1, 128:256], do_, ident[:]).then_inc(P5d.sem, P5d.step("oT"))
                    pe.wait_ge(A5d.sem, A5d.at("oT_out", n))
                    pe.matmul(pD[:, 1, 256:384], doT, w0("wo1"), start=True, stop=True).then_inc(P5d.sem, P5d.step("y"))
                if u[1]:
                    b, n = u[1]
                    pe.wait_ge(V5a.sem, V5a.at("xn", n))
                    pe.wait_ge(A5b.sem, A5b.at("xT_out", n - 1))
                    pe.transpose(pA[:, 0, 0:T], dx, ident[:]).then_inc(P5b.sem, P5b.step("xT"))
                    pe.wait_ge(A5b.sem, A5b.at("xT_out", n))
                    pe.wait_ge(A5b.sem, A5b.at("k_out", n - 1))
                    pe.matmul(pA[:, 1, 0:128], w0("wq1"), dxT, start=True, stop=True).then_inc(P5b.sem, P5b.step("q"))
                    pe.wait_ge(A5b.sem, A5b.at("q_out", n))
                    pe.matmul(pA[:, 1, 128:128 + S2], w0("k1", k=DC + 1), CX[:, b, :], start=True, stop=True).then_inc(P5b.sem, P5b.step("k"))
                    pe.wait_ge(G5b.sem, G5b.at("kbd", n))
                    pe.wait_ge(V5c.sem, V5c.at("sub", n - 1))
                    for (h, m), p in zip(SPANS, (pC[:, 0, :], pC[:, 1, :], pD[:, 0, :])):
                        ins = pe.matmul(p[:, 0:m * S2], dqT, dkb[:, h:h + m, :].rearrange("p h s -> p (h s)"), start=True, stop=True)
                    ins.then_inc(P5b.sem, P5b.step("S"))

            pipeline(pe, x0, 4, B, 0)
            after(pe, B - 1, V1d)
            pipeline(pe, conv, 2, NG, 0)
            after(pe, NG - 1, A2b)
            pipeline(pe, f0, 4, B, 0)
            after(pe, B - 1, V3d)
            pipeline(pe, route, 4, B, 0)
            after(pe, B - 1, V4d, G4b)
            pe.wait_ge(s_mw, 32)
            with pe.Fori(0, NG) as g:
                up(g, g, 0)
                for e in range(1, NE + 1):
                    if e < NE:
                        up(g, g, e)
                    down(g, g, e - 1)
            after(pe, NG - 1, V4e)
            pipeline(pe, x1, 5, B, 0)
            after(pe, B - 1, V5e)
            pe.wait_ge(s_clear, 3)

            def turn(p, src):
                for c in range(8):
                    ins = pe.transpose(blocks(p)[:, c, :], src(c), ident[:])
                return ins

            def scores(n, g, p):
                for c in range(2):
                    pe.matmul(p[:, c, :], identb[:], band[:].rearrange("p a b -> p (a b)"), start=True, stop=False, skip_group_check=True)
                    for j in range(2):
                        h2 = 4 * g + 2 * c + j
                        ins = pe.matmul(p[:, c, 256 * j:256 * j + 256], qT[:, h2, :],
                                        kbd[:, h2, :, :].rearrange("p a t -> p (a t)"), start=False, stop=(j == 1), skip_group_check=True)
                ins.then_inc(AP2.sem, AP2.step(f"S{g}"))

            def last(u, stage, n, lag):
                return n + lag if u[stage] else UNITS - 1

            def stack(u):
                if u[3]:
                    n = u[3][1]
                    pe.wait_ge(AG2.sem, AG2.at("p0", n))
                    pe.wait_ge(AA1.sem, AA1.at("qT_out", last(u, 2, n, 1)))
                    turn(pA, lambda c: prob[:, c, :]).then_inc(AP3.sem, AP3.step("PT0"))
                    pe.wait_ge(AG2.sem, AG2.at("p1", n))
                    turn(pC, lambda c: prob[:, 8 + c, :]).then_inc(AP3.sem, AP3.step("PT1"))
                if u[2]:
                    n = u[2][1]
                    pe.wait_ge(AA1.sem, AA1.at("kT_out", n))
                    pe.wait_ge(AV1.sem, AV1.at("kT_out", n))
                if u[1]:
                    n = u[1][1]
                    pe.wait_ge(AG0.sem, AG0.at("xc", n))
                    pe.transpose(pD[:, 0, 0:T], xc[:], ident[:]).then_inc(AP1.sem, AP1.step("xT"))
                if u[5]:
                    n = u[5][1]
                    pe.wait_ge(FG1.sem, FG1.at("b", n))
                    pe.wait_ge(FA2.sem, FA2.at("xT_out", n - 1))
                    pe.transpose(pD[:, 1, 3 * T:4 * T], xb[:], ident[:]).then_inc(FP2.sem, FP2.step("xT"))
                if u[7]:
                    n = u[7][1]
                    pe.wait_ge(FV3.sem, FV3.at("gated", n))
                    pe.wait_ge(FA4.sem, FA4.at("mT_out", n - 1))
                    for c in range(FC):
                        ins = pe.transpose(pD[:, 1, 128 * c:128 * c + 128], mg[:, 128 * c:128 * c + 128], ident[:])
                    ins.then_inc(FP4.sem, FP4.step("mT"))
                if u[1]:
                    n = u[1][1]
                    qkv = value(pe, of_unit(pe, n)[1] * W_ALL)
                    pe.wait_ge(s_layer, (n >> 4) + 1)
                    pe.wait_ge(AA1.sem, AA1.at("xsT", n))
                    pe.wait_ge(FV2.sem, FV2.at("bias", n - 5))
                    pe.wait_ge(FV4.sem, FV4.at("yb", n - 7))
                    pe.wait_ge(AV3.sem, AV3.at("x_out", n - 3))
                    for name, p, which in (("q", pB, 0), ("k", pD, 1)):
                        if name == "k":
                            pe.wait_ge(FA2.sem, FA2.at("xT_out", n - 4))
                            pe.wait_ge(FA4.sem, FA4.at("mT_out", n - 6))
                        for c in range(2):
                            ins = pe.matmul(p[:, c, :], xsT[:], WLf[:, bass.ds(qkv + (W_QKV + which * INNER + 512 * c), 512)], start=True, stop=True)
                        ins.then_inc(AP1.sem, AP1.step(name))
                if u[3]:
                    n = u[3][1]
                    pe.wait_ge(AA3.sem, AA3.at("pT0", n))
                    pe.wait_ge(AV3.sem, AV3.at("pT1", n))
                    pe.wait_ge(AG2.sem, AG2.at("v", n))
                    pe.wait_ge(AA1.sem, AA1.at("q_out", last(u, 1, n, 2)))
                    pe.wait_ge(FV2.sem, FV2.at("bias", n - 3))
                    pe.wait_ge(FV4.sem, FV4.at("yb", n - 5))
                    pe.wait_ge(AV3.sem, AV3.at("x_out", n - 1))
                    for h in range(NH):
                        o = E * (h % 2)
                        ins = pe.matmul(blocks(pB)[o:o + E, h // 2, :], v[:, h * E:(h + 1) * E], probT[:, h, :], start=True, stop=True)
                    ins.then_inc(AP3.sem, AP3.step("O"))
                if u[2]:
                    n = u[2][1]
                    pe.wait_ge(AA3.sem, AA3.at("pT0", n - 1))
                    scores(n, 0, pA)
                if u[2]:
                    n = u[2][1]
                    pe.wait_ge(AV3.sem, AV3.at("pT1", n - 1))
                    scores(n, 1, pC)
                if u[1]:
                    n = u[1][1]
                    pe.wait_ge(AA1.sem, AA1.at("q_out", n))
                    pe.wait_ge(AA3.sem, AA3.at("oT_out", n - 2))
                    for c in range(2):
                        ins = pe.matmul(pB[:, c, :], xsT[:], WLf[:, bass.ds(qkv + (W_QKV + 2 * INNER + 512 * c), 512)], start=True, stop=True)
                    ins.then_inc(AP1.sem, AP1.step("v"))
                    pe.wait_ge(AV1.sem, AV1.at("q_r", n))
                    pe.wait_ge(AA2.sem, AA2.at("exp0", n - 1))
                    turn(pA, lambda c: rc[:, 0, 128 * c:128 * c + 128]).then_inc(AP1.sem, AP1.step("qT"))
                if u[3]:
                    n = u[3][1]
                    back = value(pe, of_unit(pe, n)[1] * W_ALL)
                    pe.wait_ge(AA3.sem, AA3.at("oT_out", n))
                    pe.wait_ge(AA1.sem, AA1.at("v_out", last(u, 1, n, 2)))
                    for c in range(8):
                        ins = pe.matmul(pB[:, 1, FF:FF + D], oT[:, c, :], WLf[:, bass.ds(back + (W_O + D * c), D)], start=(c == 0), stop=(c == 7))
                    ins.then_inc(AP3.sem, AP3.step("y"))
                if u[7]:
                    n = u[7][1]
                    down = value(pe, of_unit(pe, n)[1] * W_ALL)
                    pe.wait_ge(FA4.sem, FA4.at("mT_out", n))
                    pe.wait_ge(AA3.sem, AA3.at("oT_out", last(u, 3, n, 4)))
                    pe.wait_ge(FV4.sem, FV4.at("yb", n - 1))
                    pe.wait_ge(FV2.sem, FV2.at("bias", last(u, 6, n, 1)))
                    for c in range(FC):
                        ins = pe.matmul(pB[:, 0, FF:FF + D], mT[:, c, :], WLf[:, bass.ds(down + (W_2 + D * c), D)], start=(c == 0), stop=(c == FC - 1))
                    ins.then_inc(FP4.sem, FP4.step("y"))
                if u[5]:
                    n = u[5][1]
                    up = value(pe, of_unit(pe, n)[1] * W_ALL)
                    pe.wait_ge(FA2.sem, FA2.at("xT_out", n))
                    pe.wait_ge(FV2.sem, FV2.at("bias", n - 1))
                    pe.wait_ge(AA1.sem, AA1.at("v_out", last(u, 1, n, 4)))
                    pe.wait_ge(AA3.sem, AA3.at("oT_out", last(u, 3, n, 2)))
                    for c in range(2):
                        ins = pe.matmul(pB[:, c, 0:FF], xnT[:], WLf[:, bass.ds(up + (W_1 + FF * c), FF)], start=True, stop=True)
                    ins.then_inc(FP2.sem, FP2.step("h"))
                if u[1]:
                    n = u[1][1]
                    pe.wait_ge(AV1.sem, AV1.at("k_n", n))
                    pe.wait_ge(AA1.sem, AA1.at("k_out", n))
                    turn(pD, lambda c: rc[:, 1, 128 * c:128 * c + 128]).then_inc(AP1.sem, AP1.step("kT"))

            pipeline(pe, stack, STAGES, UNITS, 0)

        @block.scalar
        def _(act):
            def stack(u):
                def head_exp(n, g, p):
                    act.wait_ge(AV2.sem, AV2.at(f"neg{g}", n))
                    act.wait_ge(AP3.sem, AP3.at(f"PT{g}", n - 1))
                    act.wait_ge(AV2.sem, AV2.at(f"rsum{g}", n - 1))
                    for c in range(8):
                        h = 8 * g + c
                        ins = act.activation(prob[:, h, :], blocks(p)[:, c, :], ACT.Exp, bias=nm[:, h:h + 1], scale=sc[:, h:h + 1],
                                             accum_out=psums[:, h:h + 1])
                    ins.then_inc(AA2.sem, AA2.step(f"exp{g}"))

                def table_of(n, name, f, i):
                    act.wait_ge(AW.sem, AW.at(name, n - 1))
                    act.activation(warm[:, i:i + 1], zeros[:, 0:1], f).then_inc(AW.sem, AW.step(name))

                if u[3]:
                    n = u[3][1]
                    act.wait_ge(AP3.sem, AP3.at("PT0", n))
                    act.wait_ge(AP3.sem, AP3.at("O", n - 1))
                    act.copy(probT[:, 0:8, :], blocks(pA)).then_inc(AA3.sem, AA3.step("pT0"))
                if u[1]:
                    n = u[1][1]
                    act.wait_ge(AP1.sem, AP1.at("xT", n))
                    act.wait_ge(AP1.sem, AP1.at("v", n - 1))
                    act.copy(xsT[:], pD[:, 0, 0:T]).then_inc(AA1.sem, AA1.step("xsT"))
                if u[5]:
                    n = u[5][1]
                    act.wait_ge(FP2.sem, FP2.at("xT", n))
                    act.wait_ge(FP2.sem, FP2.at("h", n - 1))
                    act.wait_ge(FP4.sem, FP4.at("mT", n - 2))
                    act.copy(xnT[:], pD[:, 1, 3 * T:4 * T]).then_inc(FA2.sem, FA2.step("xT_out"))
                if u[7]:
                    n = u[7][1]
                    act.wait_ge(FP4.sem, FP4.at("mT", n))
                    act.wait_ge(FP4.sem, FP4.at("y", n - 1))
                    act.copy(mT[:].rearrange("p a b -> p (a b)"), pD[:, 1, 0:FC * 128]).then_inc(FA4.sem, FA4.step("mT_out"))
                if u[6]:
                    n = u[6][1]
                    act.wait_ge(FV2.sem, FV2.at("bias", n))
                    act.wait_ge(FV3.sem, FV3.at("gated", n - 1))
                    act.activation(gg[:], hb[:, 1, :], ACT.Gelu).then_inc(FA3.sem, FA3.step("gelu"))
                if u[1]:
                    n = u[1][1]
                    table_of(n, "exp", ACT.Exp, 0)
                    for j, (name, p) in enumerate((("q", pB), ("k", pD))):
                        act.wait_ge(AP1.sem, AP1.at(name, n))
                        if j == 0:
                            act.wait_ge(AV1.sem, AV1.at("k_s", n - 1))
                            act.wait_ge(AG1.sem, AG1.at("q_sq", n - 1))
                        act.copy(qn[:, j, :], flat(p)).then_inc(AA1.sem, AA1.step(f"{name}_out"))
                    act.wait_ge(AA1.sem, AA1.at("k_out", n))
                    act.wait_ge(AV1.sem, AV1.at("k_ss", n - 1))
                    act.activation(sq[:, 1, :], qn[:, 1, :], ACT.Square).then_inc(AA1.sem, AA1.step("k_sq"))
                if u[3]:
                    n = u[3][1]
                    act.wait_ge(AP3.sem, AP3.at("O", n))
                    act.wait_ge(AP3.sem, AP3.at("y", n - 1))
                    act.copy(oT[:], blocks(pB)).then_inc(AA3.sem, AA3.step("oT_out"))
                if u[2]:
                    head_exp(u[2][1], 0, pA)
                if u[1]:
                    n = u[1][1]
                    act.wait_ge(AP1.sem, AP1.at("v", n))
                    act.wait_ge(AG2.sem, AG2.at("v", n - 1))
                    act.copy(vn[:], flat(pB)).then_inc(AA1.sem, AA1.step("v_out"))
                if u[2]:
                    head_exp(u[2][1], 1, pC)
                if u[1]:
                    n = u[1][1]
                    act.wait_ge(AP1.sem, AP1.at("qT", n))
                    act.copy(qT[:], blocks(pA)).then_inc(AA1.sem, AA1.step("qT_out"))
                    table_of(n, "gelu", ACT.Gelu, 1)
                    act.wait_ge(AP1.sem, AP1.at("kT", n))
                    act.copy(kbd[0:E, :, 0, :], blocks(pD)[0:E]).then_inc(AA1.sem, AA1.step("kT_out"))

            act.wait_ge(s_zero, 4)
            act.wait_ge(s_zero, 4)
            act.wait_ge(ldc, 16 * N_CONST)
            act.activation(dt, r0("log_dt"), ACT.Exp).then_inc(SA.sem, SA.step("dt"))
            act.activation(tg[:], r0("gates"), ACT.Tanh).then_inc(SA.sem, SA.step("gates"))
            act.wait_ge(SV.sem, SV.at("cos_frac", 0))
            act.activation(cos, cos, ACT.Sin, scale=TURN).then_inc(SA.sem, SA.step("cos"))
            act.wait_ge(SV.sem, SV.at("sin_frac", 0))
            act.activation(sin, sin, ACT.Sin, scale=TURN).then_inc(SA.sem, SA.step("sin"))
            act.wait_ge(SV.sem, SV.at("dta_re", 0))
            act.activation(mag, dta_re, ACT.Exp).then_inc(SA.sem, SA.step("mag"))
            act.wait_ge(SV.sem, SV.at("cos_i_frac", 0))
            act.activation(sQ2, sQ2, ACT.Sin, scale=TURN).then_inc(SA.sem, SA.step("cos_i"))
            act.wait_ge(SV.sem, SV.at("sin_i_frac", 0))
            act.activation(sQ, sQ, ACT.Sin, scale=TURN).then_inc(SA.sem, SA.step("sin_i"))
            act.wait_ge(SV.sem, SV.at("wave_j_frac", 0))
            act.activation(sT1, sT1, ACT.Sin, scale=TURN).then_inc(SA.sem, SA.step("wave_j"))
            act.wait_ge(SV.sem, SV.at("arg_i", 0))
            act.activation(sQ3, sQ3, ACT.Exp).then_inc(SA.sem, SA.step("mag_i"))
            act.wait_ge(SV.sem, SV.at("arg_j", 0))
            act.activation(sP, sP, ACT.Exp).then_inc(SA.sem, SA.step("mag_j"))
            act.wait_ge(s_set, 1)

            def x0(u):
                if u[3]:
                    b, n = u[3]
                    act.wait_ge(P1d.sem, P1d.at("vT", n))
                    act.wait_ge(P1d.sem, P1d.at("vf", n - 1))
                    act.copy(avT, pC[:, 0, 0:S2]).then_inc(A1d.sem, A1d.step("vT_out"))
                    act.wait_ge(P1d.sem, P1d.at("aT", n))
                    act.wait_ge(P1d.sem, P1d.at("film", n - 1))
                    act.copy(aT[0:S2, :], pC[0:S2, 0, 128:256]).then_inc(A1d.sem, A1d.step("aT_out"))
                    act.wait_ge(P1d.sem, P1d.at("vf", n))
                    act.copy(avf[0:S2, :], pC[0:S2, 1, :]).then_inc(A1d.sem, A1d.step("vf_out"))
                if u[2]:
                    b, n = u[2]
                    act.wait_ge(P1b.sem, P1b.at("S", n))
                    act.wait_ge(V1c.sem, V1c.at("sel", n - 1))
                    act.copy(work.rearrange("p h s -> p (h s)"), pB[:, 1, 0:H0 * S2]).then_inc(A1c.sem, A1c.step("work"))
                    act.wait_ge(V1c.sem, V1c.at("sub", n))
                    act.activation(eexp, esub, ACT.Exp).then_inc(A1c.sem, A1c.step("exp"))
                if u[1]:
                    b, n = u[1]
                    act.wait_ge(P1b.sem, P1b.at("xT", n))
                    act.wait_ge(P1b.sem, P1b.at("Q", n - 1))
                    act.copy(axT, pA[:, 0, 0:T]).then_inc(A1b.sem, A1b.step("xT_out"))
                    act.wait_ge(P1b.sem, P1b.at("Q", n))
                    act.wait_ge(P1b.sem, P1b.at("S", n - 1))
                    act.mul(aqT, pA[:, 1, 0:T], float(1.0 / np.sqrt(DH0))).then_inc(A1b.sem, A1b.step("Q_out"))

            def conv(u):
                if u[1]:
                    c, n = u[1]
                    act.wait_ge(P2b.sem, P2b.at("G", n))
                    act.copy(U[:, bass.ts(c, GB), :].rearrange("p b d -> p (b d)"), pB[:, 0, :]).then_inc(A2b.sem, A2b.step("cv"))

            def f0(u):
                if u[1]:
                    b, n = u[1]
                    act.wait_ge(P3b.sem, P3b.at("hT", n))
                    act.wait_ge(P3b.sem, P3b.at("h", n - 1))
                    act.copy(chT, pA[:, 0, 0:T]).then_inc(A3b.sem, A3b.step("hT_out"))
                    act.wait_ge(P3b.sem, P3b.at("h", n))
                    act.wait_ge(P3c.sem, P3c.at("y", n - 1))
                    for c in range(4):
                        ins = act.activation(cgT[:, c, :], pB[:, 0, 128 * c:128 * c + 128], ACT.Gelu, bias=co("b1", c))
                    ins.then_inc(A3b.sem, A3b.step("gelu"))

            def route(u):
                if u[3]:
                    b, n = u[3]
                    act.wait_ge(P4d.sem, P4d.at("cT", n))
                    act.wait_ge(P4d.sem, P4d.at("bb", n - 1))
                    act.copy(cT[0:NE, :], pC[0:NE, 0, 0:128]).then_inc(A4d.sem, A4d.step("cT_out"))
                if u[2]:
                    b, n = u[2]
                    act.wait_ge(V4c.sem, V4c.at("gap", n))
                    act.activation(ed[:, 1:2], ed[:, 0:1], ACT.Exp).then_inc(A4c.sem, A4c.step("exp"))
                if u[1]:
                    b, n = u[1]
                    act.wait_ge(P4b.sem, P4b.at("xT", n))
                    act.wait_ge(P4b.sem, P4b.at("lg", n - 1))
                    act.wait_ge(G4b.sem, G4b.at("keep", n - 1))
                    act.copy(mxT, pA[:, 0, 0:T]).then_inc(A4b.sem, A4b.step("xT_out"))

            def experts(g, n):
                for e in range(NE):
                    for c in range(4):
                        act.wait_ge(P4e.sem, P4e.at(f"h{e}{c}", n))
                        if c == 0:
                            act.wait_ge(P4e.sem, P4e.at(f"y{(e - 2) % NE}", n - (e < 2)))
                        act.activation(gT[e % 2][:, c, :], (pA, pB)[c // 2][:, c % 2, :], ACT.Gelu, bias=co("mb1", 4 * e + c)).then_inc(A4e.sem, A4e.step(f"g{e}{c}"))

            def x1(u):
                if u[3]:
                    b, n = u[3]
                    act.wait_ge(P5d.sem, P5d.at("v", n))
                    act.wait_ge(P5d.sem, P5d.at("O", n - 1))
                    act.copy(dv[0:S2, :], pD[0:S2, 1, 0:128]).then_inc(A5d.sem, A5d.step("v_out"))
                    act.wait_ge(P5d.sem, P5d.at("PT0", n))
                    act.copy(dpT[0:S2, 0:8, :], blocks(pB)[0:S2]).then_inc(A5d.sem, A5d.step("pT0"))
                    act.wait_ge(P5d.sem, P5d.at("oT", n))
                    act.wait_ge(P5d.sem, P5d.at("y", n - 1))
                    act.copy(doT, pD[:, 1, 128:256]).then_inc(A5d.sem, A5d.step("oT_out"))
                if u[2]:
                    b, n = u[2]
                    act.wait_ge(V5c.sem, V5c.at("sub", n))
                    act.wait_ge(P5d.sem, P5d.at("PT1", n - 1))
                    act.activation(dpr, dsub, ACT.Exp, scale=SCALE1).then_inc(A5c.sem, A5c.step("exp"))
                if u[1]:
                    b, n = u[1]
                    act.wait_ge(P5b.sem, P5b.at("xT", n))
                    act.wait_ge(P5b.sem, P5b.at("q", n - 1))
                    act.copy(dxT, pA[:, 0, 0:T]).then_inc(A5b.sem, A5b.step("xT_out"))
                    act.wait_ge(P5b.sem, P5b.at("q", n))
                    act.wait_ge(P5b.sem, P5b.at("S", n - 1))
                    act.add(dqT, pA[:, 1, 0:128], co("bq")).then_inc(A5b.sem, A5b.step("q_out"))
                    act.wait_ge(P5b.sem, P5b.at("k", n))
                    act.wait_ge(G5b.sem, G5b.at("kbd", n - 1))
                    act.copy(dk, pA[:, 1, 128:128 + S2]).then_inc(A5b.sem, A5b.step("k_out"))

            pipeline(act, x0, 4, B, 0)
            after(act, B - 1, V1d)
            pipeline(act, conv, 2, NG, 0)
            pipeline(act, f0, 4, B, 0)
            after(act, B - 1, V3d)
            pipeline(act, route, 4, B, 0)
            after(act, B - 1, V4d, G4b)
            with act.Fori(0, NG) as g:
                experts(g, g)
            after(act, NG - 1, V4e)
            pipeline(act, x1, 5, B, 0)
            after(act, B - 1, V5e)
            act.wait_ge(s_clear, 3)
            pipeline(act, stack, STAGES, UNITS, 0)

        @block.vector
        def _(dve):
            def stack(u):
                def head_max(n, g, p):
                    at = slice(8 * g, 8 * g + 8)
                    dve.wait_ge(AP2.sem, AP2.at(f"S{g}", n))
                    dve.tensor_reduce(mx[:, at], blocks(p), AX.X, ALU.max).then_inc(AV2.sem, AV2.step(f"max{g}"))
                    if g == 0:
                        dve.wait_ge(AA2.sem, AA2.at("exp1", n - 1))
                        dve.tensor_scalar(sc[:], rn[:, 0, :], QK_SCALE, None, ALU.mult).then_inc(AV2.sem, AV2.step("scale"))
                    dve.wait_ge(AV2.sem, AV2.at("scale" if g == 0 else "max1", n))
                    dve.scalar_tensor_tensor(nm[:, at], mx[:, at], -1.0, sc[:, at], ALU.mult, ALU.mult).then_inc(AV2.sem, AV2.step(f"neg{g}"))

                def swapped(n, j, name):
                    q4 = qn[:, j, :].rearrange("p (h two e) -> p h two e", two=2, e=E // 2)
                    s4 = rs[:, j, :].rearrange("p (h two e) -> p h two e", two=2, e=E // 2)
                    dve.wait_ge(AA1.sem, AA1.at(f"{name}_out", n))
                    for c in range(2):
                        tab = RTf[:, bass.ds(table + ((2 * j + 1) * E + c * (E // 2)), E // 2)].unsqueeze(1).to_broadcast([T, NH, E // 2])
                        ins = dve.tensor_tensor(s4[:, :, c, :], q4[:, :, 1 - c, :], tab, ALU.mult)
                    ins.then_inc(AV1.sem, AV1.step(f"{name}_s"))

                def turned(n, j, name):
                    dve.wait_ge(AV1.sem, AV1.at("k_s", n))
                    dve.wait_ge(AG1.sem, AG1.at(f"{name}_c", n))
                    dve.tensor_tensor(rc[:, j, :], rc[:, j, :], rs[:, j, :], ALU.add).then_inc(AV1.sem, AV1.step(f"{name}_r"))

                def sums(n, g):
                    dve.wait_ge(AA2.sem, AA2.at(f"exp{g}", n))
                    dve.wait_ge(AG2.sem, AG2.at(f"p{g}", n - 1))
                    dve.reciprocal(rsum[:, 8 * g:8 * g + 8], psums[:, 8 * g:8 * g + 8]).then_inc(AV2.sem, AV2.step(f"rsum{g}"))

                def squares(n, j, name):
                    S = (AG1, AA1)[j]
                    dve.wait_ge(S.sem, S.at(f"{name}_sq", n))
                    dve.tensor_reduce(ss[:, j, :], sq[:, j, :].rearrange("p (h e) -> p h e", e=E), AX.X, ALU.add).then_inc(AV1.sem, AV1.step(f"{name}_ss"))

                if u[3]:
                    n = u[3][1]
                    dve.wait_ge(AP3.sem, AP3.at("PT1", n))
                    dve.wait_ge(AP3.sem, AP3.at("O", n - 1))
                    dve.tensor_copy(probT[:, 8:16, :], blocks(pC)).then_inc(AV3.sem, AV3.step("pT1"))
                if u[4]:
                    n = u[4][1]
                    b4, _ = of_unit(dve, n)
                    dve.wait_ge(s_sh, (n + 2) * 16)
                    dve.wait_ge(AG3.sem, AG3.at("xs", n))
                    moments(dve, FV1, FG0, n, XS[:, b4, :], NF, s_pass)
                if u[6]:
                    n = u[6][1]
                    dve.wait_ge(FA3.sem, FA3.at("gelu", n))
                    dve.wait_ge(FP4.sem, FP4.at("mT", n - 1))
                    dve.tensor_tensor(mg[:, 0:FF], hb[:, 0, :], gg[:], ALU.mult).then_inc(FV3.sem, FV3.step("gated"))
                if u[4]:
                    n = u[4][1]
                    dve.wait_ge(FG1.sem, FG1.at("g", n - 1))
                    centre(dve, FV1, FG0, n, xn[:], XS[:, b4, :], NF)
                if u[1]:
                    n = u[1][1]
                    table = value(dve, (n >> 4) * (4 * E))
                    swapped(n, 0, "q")
                    swapped(n, 1, "k")
                    squares(n, 1, "k")
                if u[2]:
                    head_max(u[2][1], 0, pA)
                if u[1]:
                    n = u[1][1]
                    turned(n, 0, "q")
                if u[2]:
                    head_max(u[2][1], 1, pC)
                if u[1]:
                    n = u[1][1]
                    squares(n, 0, "q")
                if u[1]:
                    n = u[1][1]
                    dve.wait_ge(AV1.sem, AV1.at("q_ss", n))
                    dve.tensor_scalar(ss[:], ss[:], 1e-24, None, ALU.max).then_inc(AV1.sem, AV1.step("floor"))
                    dve.wait_ge(AV1.sem, AV1.at("floor", n))
                    rsqrt(dve, AV1, n, "", rn[:], rh[:], ss[:])
                    turned(n, 1, "k")
                    dve.wait_ge(AV1.sem, AV1.at("k_r", n))
                    k3 = rc[:, 1, :].rearrange("p (h e) -> p h e", e=E)
                    dve.tensor_tensor(k3, k3, rn[:, 1, :].unsqueeze(2).to_broadcast([T, NH, E]), ALU.mult).then_inc(AV1.sem, AV1.step("k_n"))
                if u[2]:
                    sums(u[2][1], 0)
                    sums(u[2][1], 1)
                if u[3]:
                    n = u[3][1]
                    b, _ = of_unit(dve, n)
                    dve.wait_ge(AP3.sem, AP3.at("y", n))
                    if u[5]:
                        dve.wait_ge(FP2.sem, FP2.at("h", n - 2))
                    dve.tensor_tensor(XD[:, b, :], pB[:, 1, FF:FF + D], XD[:, b, :], ALU.add).then_inc(AV3.sem, AV3.step("x_out"))
                if u[7]:
                    n = u[7][1]
                    b, parity = of_unit(dve, n)
                    bias = value(dve, parity * R_ALL)
                    dve.wait_ge(FV4.sem, FV4.at("x_out", n - 1))
                    dve.wait_ge(FP4.sem, FP4.at("y", n))
                    if u[5]:
                        dve.wait_ge(FP2.sem, FP2.at("h", n + 2))
                    dve.tensor_tensor(yb[:], pB[:, 0, FF:FF + D], RLf[:, bass.ds(bias + R_B2, D)], ALU.add).then_inc(FV4.sem, FV4.step("yb"))
                    dve.wait_ge(FV4.sem, FV4.at("yb", n))
                    dve.tensor_tensor(XD[:, b, :], yb[:], XD[:, b, :], ALU.add).then_inc(FV4.sem, FV4.step("x_out"))
                if u[5]:
                    n = u[5][1]
                    bias = value(dve, of_unit(dve, n)[1] * R_ALL)
                    dve.wait_ge(FP2.sem, FP2.at("h", n))
                    dve.wait_ge(FV3.sem, FV3.at("gated", n - 1))
                    dve.tensor_tensor(hb[:], pB[:, :, 0:FF], RLf[:, bass.ds(bias + R_B1, 2 * FF)].rearrange("p (a f) -> p a f", a=2), ALU.add).then_inc(FV2.sem, FV2.step("bias"))
                if u[1]:
                    n = u[1][1]
                    dve.wait_ge(AP1.sem, AP1.at("kT", n))
                    dve.tensor_copy(kbd[E:2 * E, :, 1, :], blocks(pD)[E:2 * E]).then_inc(AV1.sem, AV1.step("kT_out"))

            dve.wait_ge(s_zero, 4)
            def done(name, ins):
                ins.then_inc(SV.sem, SV.step(name))
                dve.wait_ge(SV.sem, SV.at(name, 0))

            def tt(name, out_, x, y, o):
                done(name, dve.tensor_tensor(out_, x, y, o))

            def ts(name, out_, x, s1, s2, o1, o2=None):
                done(name, dve.tensor_scalar(out_, x, s1, s2, o1, o2) if o2 else dve.tensor_scalar(out_, x, s1, s2, o1))

            def over(x, m):
                return x.unsqueeze(2).to_broadcast([128, 128, m])

            def along(x, m):
                return x.unsqueeze(1).to_broadcast([128, 128, m])

            def whole_turns_off(name, x, k):
                ts(name + "_whole", k, x, ROUND, -ROUND, ALU.add, ALU.add)
                tt(name + "_frac", x, x, k, ALU.subtract)

            dve.wait_ge(ldc, 16 * N_CONST)
            done("identb", dve.tensor_copy(identb[:], ident[:]))
            done("band", dve.tensor_copy(band[:], xg[:].unsqueeze(1).to_broadcast([128, 4, 128])))
            dve.wait_ge(SA.sem, SA.at("dt", 0))
            tt("dta_re", dta_re, dt, are, ALU.mult)
            tt("dta_im", dta_im, dt, aim, ALU.mult)
            ts("turns", turns, dta_im, float(1 / (2 * np.pi)), None, ALU.mult)
            ts("cos_turns", cos, turns, 0.25, None, ALU.add)
            whole_turns_off("cos", cos, spare)
            ts("sin_turns", sin, turns, 0.0, None, ALU.add)
            whole_turns_off("sin", sin, spare)
            dve.wait_ge(SA.sem, SA.at("mag", 0))
            tt("e_re", e_re, cos, mag, ALU.mult)
            tt("e_im", e_im, sin, mag, ALU.mult)
            ts("e_re_less_1", e_re, e_re, -1.0, None, ALU.add)
            tt("c_e_rr", num_re, cre, e_re, ALU.mult)
            tt("c_e_ii", spare, cim, e_im, ALU.mult)
            tt("num_re", num_re, num_re, spare, ALU.subtract)
            tt("c_e_ri", num_im, cre, e_im, ALU.mult)
            tt("c_e_ir", spare, cim, e_re, ALU.mult)
            tt("num_im", num_im, num_im, spare, ALU.add)
            tt("a_rr", scale, are, are, ALU.mult)
            tt("a_ii", spare, aim, aim, ALU.mult)
            tt("a_abs2", spare, scale, spare, ALU.add)
            done("a_inv", dve.reciprocal(scale, spare))
            ts("scale", scale, scale, 2.0, None, ALU.mult)
            tt("n_a_rr", dc_re, num_re, are, ALU.mult)
            tt("n_a_ii", spare, num_im, aim, ALU.mult)
            tt("dc_re_num", dc_re, dc_re, spare, ALU.add)
            tt("dc_re", dc_re, dc_re, scale, ALU.mult)
            tt("n_a_ir", dc_im, num_im, are, ALU.mult)
            tt("n_a_ri", spare, num_re, aim, ALU.mult)
            tt("dc_im_num", dc_im, dc_im, spare, ALU.subtract)
            tt("dc_im", dc_im, dc_im, scale, ALU.mult)
            ts("row_cos_0", spare, dc_re, co("m0"), None, ALU.mult)
            done("row_cos", dve.scalar_tensor_tensor(num_re, dc_im, co("-m1"), spare, ALU.mult, ALU.add))
            ts("row_sin_0", spare, dc_im, co("-m0"), None, ALU.mult)
            done("row_sin", dve.scalar_tensor_tensor(num_im, dc_re, co("-m1"), spare, ALU.mult, ALU.add))
            tt("sin_i_turns", sQ, over(turns, NI), along(w0("i"), NI), ALU.mult)
            ts("cos_i_turns", sQ2, sQ, 0.25, None, ALU.add)
            whole_turns_off("cos_i", sQ2, sQ3)
            whole_turns_off("sin_i", sQ, sQ3)
            tt("wave_j_turns", sP, over(turns, NJ), along(w0("j"), NJ), ALU.mult)
            ts("wave_j_off", sT1, sP, co("off"), None, ALU.add)
            whole_turns_off("wave_j", sT1, sT2)
            tt("arg_i", sQ3, over(dta_re, NI), along(w0("i"), NI), ALU.mult)
            tt("arg_j", sP, over(dta_re, NJ), along(w0("j"), NJ), ALU.mult)
            dve.wait_ge(SA.sem, SA.at("mag_i", 0))
            tt("cos_i_mag", sQ2, sQ2, sQ3, ALU.mult)
            tt("sin_i_mag", sQ, sQ, sQ3, ALU.mult)
            tt("row_i_cos", sQc, sQ2, over(num_re, NI), ALU.mult)
            tt("row_i_sin", sQ3, sQ, over(num_im, NI), ALU.mult)
            tt("row_i", sQc, sQc, sQ3, ALU.add)
            dve.wait_ge(SA.sem, SA.at("mag_j", 0))
            tt("power_j", sP, sP, sT1, ALU.mult)
            dve.wait_ge(s_sp, 1)
            done("rows", dve.tensor_copy(KS[0:NJ].rearrange("j i d -> j d i"), pA[0:NJ].rearrange("p b (d i) -> p (b d) i", i=NI)))
            dve.tensor_tensor(KS[0:1, 0, :], KS[0:1, 0, :], r0("dskip")[0:1], ALU.add).then_inc(s_ks, 1)
            dve.wait_ge(s_sp, 2)
            done("f_cos", dve.tensor_copy(KF[:, 0, :], pB[:, 0, 0:128]))
            ts("f_sin", KF[:, 1, :], pB[:, 0, 128:256], co("nz"), None, ALU.mult)
            ts("f_half", KF[:, 2, :], pB[:, 0, 128:256], co("z"), None, ALU.mult)
            done("f_flip", dve.scalar_tensor_tensor(KF[:, 2, :], KF[:, 0, :], co("nz"), KF[:, 2, :], ALU.mult, ALU.add))
            ts("text_mask", tm[:], tm8[:], 1.0 / H0, None, ALU.mult)
            ts("context_mask", vm[:].rearrange("p b s -> p (b s)"), vm8[:], -1.0, BIG, ALU.add, ALU.mult)
            dve.sem_inc(s_set, 1)
            dve.wait_ge(s_x, 16)

            def x0(u):
                if u[3]:
                    b, n = u[3]
                    dve.wait_ge(G1d.sem, G1d.at("g", n - 1))
                    normalise(dve, V1d, N1d, n, a2[:], XD[:, b, :], N2, s_pass)
                    dve.wait_ge(P1d.sem, P1d.at("film", n))
                    dve.wait_ge(G1d.sem, G1d.at("fo", n - 1))
                    dve.tensor_tensor(fb, pD[:, 0, :], r0("film"), ALU.add).then_inc(V1d.sem, V1d.step("fb"))
                    dve.wait_ge(G1d.sem, G1d.at("fm", n))
                    dve.scalar_tensor_tensor(u1[:], fm[:, 0:D], 1.0, ay[:], ALU.add, ALU.mult).then_inc(V1d.sem, V1d.step("u1"))
                    dve.wait_ge(V1d.sem, V1d.at("u1", n))
                    dve.tensor_tensor(U[:, b, :], u1[:], fm[:, D:2 * D], ALU.add).then_inc(V1d.sem, V1d.step("u"))
                if u[2]:
                    b, n = u[2]
                    dve.wait_ge(A1c.sem, A1c.at("work", n))
                    dve.sem_inc(s_pass, 1)
                    for r in range(TOPK // 8):
                        for h in range(H0):
                            ins = dve.max(m8r[:, r % 2, h, :] if r else m8[:, h, :], work[:, h, :])
                        ins.then_inc(V1c.sem, V1c.step(f"max{r}"))
                        dve.wait_ge(V1c.sem, V1c.at(f"max{r}", n))
                        dve.sem_inc(s_pass, 1)
                        for h in range(H0):
                            ins = dve.match_replace(work[:, h, :], m8r[:, r % 2, h, :] if r else m8[:, h, :], work[:, h, :], GONE)
                        ins.then_inc(V1c.sem, V1c.step(f"rep{r}"))
                        dve.wait_ge(V1c.sem, V1c.at(f"rep{r}", n))
                        dve.sem_inc(s_pass, 1)
                    dve.wait_ge(A1c.sem, A1c.at("exp", n - 1))
                    dve.tensor_tensor(esub, pB[:, 1, 0:H0 * S2].rearrange("p (h s) -> p h s", h=H0), m8[:, :, 0:1].to_broadcast([T, H0, S2]),
                                      ALU.subtract).then_inc(V1c.sem, V1c.step("sub"))
                    dve.wait_ge(A1c.sem, A1c.at("exp", n))
                    dve.scalar_tensor_tensor(esel, work, GONE / 2, eexp, ALU.is_le, ALU.mult).then_inc(V1c.sem, V1c.step("sel"))
                    dve.wait_ge(V1c.sem, V1c.at("sel", n))
                    dve.tensor_reduce(es, esel, AX.X, ALU.add).then_inc(V1c.sem, V1c.step("sum"))
                    dve.wait_ge(V1c.sem, V1c.at("sum", n))
                    dve.reciprocal(ew, es).then_inc(V1c.sem, V1c.step("inv"))
                    dve.wait_ge(V1c.sem, V1c.at("inv", n))
                    dve.tensor_tensor(ew, ew, tm[:, bass.ds(b, 1)].to_broadcast([T, H0]), ALU.mult).then_inc(V1c.sem, V1c.step("tm"))
                    dve.wait_ge(V1c.sem, V1c.at("tm", n))
                    dve.tensor_tensor(esel, esel, ew.unsqueeze(2).to_broadcast([T, H0, S2]), ALU.mult).then_inc(V1c.sem, V1c.step("wt"))
                    dve.wait_ge(V1c.sem, V1c.at("wt", n))
                    dve.wait_ge(P1d.sem, P1d.at("aT", n - 1))
                    dve.tensor_reduce(at_, esel.rearrange("p h s -> p s h"), AX.X, ALU.add).then_inc(V1c.sem, V1c.step("mean"))
                if u[1]:
                    b, n = u[1]
                    dve.wait_ge(P1b.sem, P1b.at("k", n))
                    dve.wait_ge(P1b.sem, P1b.at("S", n - 1))
                    dve.tensor_tensor(akb, pB[:, 0, 0:S2].unsqueeze(1).to_broadcast([128, H0, S2]), w0("hm0").unsqueeze(2).to_broadcast([128, H0, S2]),
                                      ALU.mult).then_inc(V1b.sem, V1b.step("kbd"))
                if u[0]:
                    b, n = u[0]
                    dve.wait_ge(P1b.sem, P1b.at("xT", n - 1))
                    normalise(dve, V1a, N1a, n, ax, X[:, b, :], N1, s_pass)
                    dve.wait_ge(V1a.sem, V1a.at("xn", n))
                    dve.tensor_copy(XD[:, b, :], ax).then_inc(V1a.sem, V1a.step("keep"))

            def conv(u):
                if u[0]:
                    c, n = u[0]
                    re, im = pA[:, 0, :].rearrange("p (b d) -> p b d", b=GB), pA[:, 1, :].rearrange("p (b d) -> p b d", b=GB)
                    K = [KF[:, i, :].unsqueeze(1).to_broadcast([128, GB, D]) for i in range(3)]
                    v4 = lambda t: t.rearrange("p (b d) -> p b d", b=GB)
                    dve.wait_ge(P2a.sem, P2a.at("F", n))
                    dve.wait_ge(V2a.sem, V2a.at("Yi", n - 1))
                    dve.tensor_tensor(v4(t1), re, K[0], ALU.mult).then_inc(V2a.sem, V2a.step("t1"))
                    dve.tensor_tensor(v4(t2), im, K[1], ALU.mult).then_inc(V2a.sem, V2a.step("t2"))
                    dve.wait_ge(V2a.sem, V2a.at("t2", n))
                    dve.wait_ge(P2b.sem, P2b.at("G", n - 1))
                    dve.tensor_tensor(Yr, t1, t2, ALU.subtract).then_inc(V2a.sem, V2a.step("Yr"))
                    dve.tensor_tensor(v4(t3), re, K[1], ALU.mult).then_inc(V2a.sem, V2a.step("t3"))
                    dve.tensor_tensor(v4(t4), im, K[2], ALU.mult).then_inc(V2a.sem, V2a.step("t4"))
                    dve.wait_ge(V2a.sem, V2a.at("t4", n))
                    dve.tensor_tensor(Yi, t3, t4, ALU.add).then_inc(V2a.sem, V2a.step("Yi"))

            def f0(u):
                if u[3]:
                    b, n = u[3]
                    dve.wait_ge(G3c.sem, G3c.at("b", n))
                    dve.scalar_tensor_tensor(X[:, b, :], ay[:], tg[:, 0:1], X[:, b, :], ALU.mult, ALU.add).then_inc(V3d.sem, V3d.step("x_out"))
                if u[2]:
                    b, n = u[2]
                    dve.wait_ge(P3c.sem, P3c.at("y", n))
                    dve.wait_ge(V3c.sem, V3c.at("xt", n - 1))
                    dve.tensor_tensor(fb[:, 0:D], pC[:, 0, 0:D], r0("b2"), ALU.add).then_inc(V3c.sem, V3c.step("yb"))
                    dve.wait_ge(V3c.sem, V3c.at("yb", n))
                    dve.wait_ge(V3c.sem, V3c.at("xn", n - 1))
                    dve.tensor_tensor(fb[:, D:2 * D], fb[:, 0:D], U[:, b, :], ALU.add).then_inc(V3c.sem, V3c.step("xt"))
                    dve.wait_ge(V3c.sem, V3c.at("xt", n))
                    dve.wait_ge(G3c.sem, G3c.at("g", n - 1))
                    normalise(dve, V3c, N3c, n, a2[:], fb[:, D:2 * D], N2, s_pass)
                if u[0]:
                    b, n = u[0]
                    dve.wait_ge(V3a.sem, V3a.at("z", n - 1))
                    dve.scalar_tensor_tensor(u1[:], FO[:, b, 0:D], 1.0, U[:, b, :], ALU.add, ALU.mult).then_inc(V3a.sem, V3a.step("z1"))
                    dve.wait_ge(V3a.sem, V3a.at("z1", n))
                    dve.wait_ge(V3a.sem, V3a.at("xt", n - 1))
                    dve.tensor_tensor(fm[:, 0:D], u1[:], FO[:, b, D:2 * D], ALU.add).then_inc(V3a.sem, V3a.step("z"))
                    dve.wait_ge(V3a.sem, V3a.at("z", n))
                    dve.tensor_tensor(U[:, b, :], fm[:, 0:D], XD[:, b, :], ALU.add).then_inc(V3a.sem, V3a.step("xt"))
                    dve.wait_ge(V3a.sem, V3a.at("xt", n))
                    dve.wait_ge(G3a.sem, G3a.at("g", n - 1))
                    normalise(dve, V3a, N3a, n, cx, U[:, b, :], N1, s_pass)

            def route(u):
                if u[3]:
                    b, n = u[3]
                    dve.wait_ge(P4d.sem, P4d.at("bb", n))
                    dve.tensor_copy(ACC[:, b, :], pC[:, 1, 0:D]).then_inc(V4d.sem, V4d.step("acc"))
                if u[2]:
                    b, n = u[2]
                    S = V4c
                    dve.wait_ge(P4b.sem, P4b.at("lg", n))
                    dve.wait_ge(S.sem, S.at("keep", n - 1))
                    dve.tensor_tensor(l8, pA[:, 1, 0:NE], r0("br"), ALU.add).then_inc(S.sem, S.step("lb"))
                    dve.wait_ge(S.sem, S.at("lb", n))
                    dve.sem_inc(s_pass, 1)
                    dve.max(e8, l8).then_inc(S.sem, S.step("max"))
                    dve.wait_ge(S.sem, S.at("max", n))
                    dve.sem_inc(s_pass, 1)
                    dve.max_index(i8.bitcast(mybir.dt.uint32), e8, l8).then_inc(S.sem, S.step("idx"))
                    dve.wait_ge(S.sem, S.at("idx", n))
                    dve.tensor_copy(i8f, i8.bitcast(mybir.dt.uint32)).then_inc(S.sem, S.step("idxf"))
                    dve.tensor_tensor(ed[:, 0:1], e8[:, 1:2], e8[:, 0:1], ALU.subtract).then_inc(S.sem, S.step("gap"))
                    dve.wait_ge(A4c.sem, A4c.at("exp", n))
                    dve.tensor_scalar(ed[:, 2:3], ed[:, 1:2], 1.0, None, ALU.add).then_inc(S.sem, S.step("den"))
                    dve.wait_ge(S.sem, S.at("den", n))
                    dve.reciprocal(ed[:, 3:4], ed[:, 2:3]).then_inc(S.sem, S.step("w0"))
                    dve.wait_ge(S.sem, S.at("w0", n))
                    dve.tensor_tensor(ed[:, 2:3], ed[:, 3:4], ed[:, 1:2], ALU.mult).then_inc(S.sem, S.step("w1"))
                    dve.wait_ge(S.sem, S.at("w1", n))
                    dve.tensor_scalar(c0, r0("experts"), i8f[:, 0:1], ed[:, 3:4], ALU.is_equal, ALU.mult).then_inc(S.sem, S.step("c0"))
                    dve.tensor_scalar(c1, r0("experts"), i8f[:, 1:2], ed[:, 2:3], ALU.is_equal, ALU.mult).then_inc(S.sem, S.step("c1"))
                    dve.wait_ge(S.sem, S.at("c1", n))
                    dve.wait_ge(P4d.sem, P4d.at("cT", n - 1))
                    dve.tensor_tensor(c2, c0, c1, ALU.add).then_inc(S.sem, S.step("cb"))
                    dve.tensor_tensor(CB[:, b, :], c0, c1, ALU.add).then_inc(S.sem, S.step("keep"))
                if u[0]:
                    b, n = u[0]
                    dve.wait_ge(P4b.sem, P4b.at("xT", n - 1))
                    normalise(dve, V4a, N4a, n, ax, X[:, b, :], N1, s_pass)

            def experts(g, n):
                for e in range(NE):
                    dve.wait_ge(P4e.sem, P4e.at(f"y{e}", n))
                    dve.wait_ge(V4e.sem, V4e.at(f"acc{(e - 1) % NE}", n - (e == 0)))
                    for t in range(GB):
                        b = g * GB + t
                        ins = dve.scalar_tensor_tensor(ACC[:, b, :], pC[:, e % 2, 128 * t:128 * t + 128], CB[:, b, e:e + 1], ACC[:, b, :],
                                                       ALU.mult, ALU.add)
                    ins.then_inc(V4e.sem, V4e.step(f"acc{e}"))

            def x1(u):
                if u[4]:
                    b, n = u[4]
                    dve.wait_ge(V5d.sem, V5d.at("x_out", n))
                    normalise(dve, V5e, N5e, n, XD[:, b, :], X[:, b, :], N2, s_pass)
                if u[3]:
                    b, n = u[3]
                    dve.wait_ge(P5d.sem, P5d.at("PT1", n))
                    dve.tensor_copy(dpT[0:S2, 8:16, :], blocks(pB)[0:S2]).then_inc(V5d.sem, V5d.step("pT1"))
                    dve.wait_ge(P5d.sem, P5d.at("O", n))
                    dve.tensor_tensor(do_.rearrange("p (h e) -> p h e", e=DH1), pD[:, 1, 0:D].rearrange("p (h e) -> p h e", e=DH1),
                                      dinv.unsqueeze(2).to_broadcast([T, H1, DH1]), ALU.mult).then_inc(V5d.sem, V5d.step("o_n"))
                    dve.wait_ge(P5d.sem, P5d.at("y", n))
                    dve.wait_ge(V5d.sem, V5d.at("x_out", n - 1))
                    dve.tensor_tensor(dyb, pD[:, 1, 256:384], r0("bo"), ALU.add).then_inc(V5d.sem, V5d.step("yb"))
                    dve.wait_ge(V5d.sem, V5d.at("yb", n))
                    dve.scalar_tensor_tensor(X[:, b, :], dyb, tg[:, 2:3], X[:, b, :], ALU.mult, ALU.add).then_inc(V5d.sem, V5d.step("x_out"))
                if u[2]:
                    b, n = u[2]
                    dve.wait_ge(P5b.sem, P5b.at("S", n))
                    dve.wait_ge(V5c.sem, V5c.at("sub", n - 1))
                    for (h, m), p in zip(SPANS, (pC[:, 0, :], pC[:, 1, :], pD[:, 0, :])):
                        ins = dve.tensor_reduce(dmx[:, h:h + m], p[:, 0:m * S2].rearrange("p (h s) -> p h s", s=S2), AX.X, ALU.max)
                    ins.then_inc(V5c.sem, V5c.step("max"))
                    dve.wait_ge(V5c.sem, V5c.at("max", n))
                    dve.wait_ge(A5c.sem, A5c.at("exp", n - 1))
                    for (h, m), p in zip(SPANS, (pC[:, 0, :], pC[:, 1, :], pD[:, 0, :])):
                        ins = dve.tensor_tensor(dsub[:, h:h + m, :], p[:, 0:m * S2].rearrange("p (h s) -> p h s", s=S2),
                                                dmx[:, h:h + m].unsqueeze(2).to_broadcast([T, m, S2]), ALU.subtract)
                    ins.then_inc(V5c.sem, V5c.step("sub"))
                    dve.wait_ge(A5c.sem, A5c.at("exp", n))
                    dve.tensor_reduce(dsum, dpr, AX.X, ALU.add).then_inc(V5c.sem, V5c.step("sum"))
                    dve.wait_ge(V5c.sem, V5c.at("sum", n))
                    dve.wait_ge(V5d.sem, V5d.at("o_n", n - 1))
                    dve.reciprocal(dinv, dsum).then_inc(V5c.sem, V5c.step("inv"))
                if u[0]:
                    b, n = u[0]
                    dve.scalar_tensor_tensor(X[:, b, :], ACC[:, b, :], tg[:, 1:2], X[:, b, :], ALU.mult, ALU.add).then_inc(V5a.sem, V5a.step("x_in"))
                    dve.wait_ge(V5a.sem, V5a.at("x_in", n))
                    dve.wait_ge(P5b.sem, P5b.at("xT", n - 1))
                    normalise(dve, V5a, N5a, n, dx, X[:, b, :], N1, s_pass)

            pipeline(dve, x0, 4, B, 0)
            pipeline(dve, conv, 2, NG, 0)
            after(dve, NG - 1, A2b)
            pipeline(dve, f0, 4, B, 0)
            after(dve, B - 1, V3d)
            pipeline(dve, route, 4, B, 0)
            after(dve, B - 1, V4d)
            with dve.Fori(0, NG) as g:
                experts(g, g)
            after(dve, NG - 1, V4e)
            pipeline(dve, x1, 5, B, 0)
            after(dve, B - 1, V5e)
            dve.wait_ge(s_clear, 3)
            dve.wait_ge(GT.sem, GT.at("table", DEPTH - 1))
            pipeline(dve, stack, STAGES, UNITS, 0)
            after(dve, B * DEPTH - 1, FV4)
            for g in range(NG):
                at = slice(GB * g, GB * g + GB)
                dve.scalar_tensor_tensor(X[:, at, :], XD[:, at, :], tg[:, 3:4], X[:, at, :], ALU.mult, ALU.add).then_inc(VF.sem, VF.step("x"))


def rope_tables():
    half = np.arange(0, E, 2, dtype=np.float32)
    inv_freq = (1.0 / 10000.0 ** (half / E)).astype(np.float32)
    t = np.arange(T, dtype=np.float32)
    f = t[:, None] * inv_freq[None, :]
    f = np.concatenate([f, f], -1).astype(np.float32)
    base = (half + 0.4 * E) / (1.4 * E)
    power = (t - T // 2) / (WINDOW // 2)
    s = base[None, :] ** power[:, None]
    s = np.concatenate([s, s], -1)
    sign = np.concatenate([-np.ones(E // 2), np.ones(E // 2)])
    c, sn = np.cos(f), np.sin(f) * sign
    return np.stack([c * s, sn * s, c / s, sn / s], 1).reshape(T, 4 * E).astype(np.float32)


def constants():
    i, j = np.arange(T)[:, None], np.arange(T)[None, :]
    band = np.where((j <= i) & (j >= i - WINDOW), 0.0, BIG16).astype(np.float32)
    return {
        "ident": np.eye(128, dtype=np.float32),
        "band": band,
        "rope": rope_tables(),
    }


def layout(inputs):
    w = {k: np.asarray(x) for k, x in inputs.items()}
    wall = np.zeros((DEPTH, 128, W_ALL), np.float32)
    wall[:, :, W_QKV:W_O] = w["L1_ffn_Wqkv"]
    wall[:, :, W_O:W_1] = w["L1_ffn_Wo"].reshape(DEPTH, 8, 128, D).transpose(0, 2, 1, 3).reshape(DEPTH, 128, 8 * D)
    wall[:, :, W_1:W_2] = w["L1_ffn_W1"]
    w2 = np.zeros((DEPTH, FC * 128, D), np.float32)
    w2[:, :FF] = w["L1_ffn_W2"]
    wall[:, :, W_2:] = w2.reshape(DEPTH, FC, 128, D).transpose(0, 2, 1, 3).reshape(DEPTH, 128, FC * D)
    swap = lambda s: np.concatenate([s[:, E // 2:], s[:, :E // 2]], 1)
    qs, ks = w["L1_ffn_q_scale"], w["L1_ffn_k_scale"]
    rall = np.concatenate([w["L1_ffn_ln_g"], w["L1_ffn_ln_b"], w["L1_ffn_b1"], w["L1_ffn_b2"], qs, swap(qs), ks, swap(ks)], 1)
    def rows(x, k=128):
        y = np.zeros((k, x.shape[1]), np.float32)
        y[:x.shape[0]] = x
        return y

    f, t = np.arange(128.0)[:, None], np.arange(128.0)[None, :]
    ang = 2 * np.pi * f * t / 256
    Fc, Fs, Gc, Gs = np.cos(ang).T.copy(), -np.sin(ang).T.copy(), np.cos(ang) / 128, -np.sin(ang) / 128
    sign = (-1.0) ** np.arange(128)
    Fs[:, 0], Gc[0], Gs[0] = sign, 1 / 256, sign / 256
    twice = lambda m: np.concatenate([m.T, m.T], 0)
    hm = lambda h: np.repeat(np.eye(h), 128 // h, 0)
    l0 = lambda k: w["L0_xattn_" + k]
    l1 = lambda k: w["L1_xattn_" + k]
    parts = {
        "Wq": l0("Wq"), "film": np.concatenate([l0("W_film_in"), l0("W_film_out")], 1), "W1": l0("W1"),
        "W2": l0("W2").reshape(4, 128, D).transpose(1, 0, 2).reshape(128, 4 * D), "Wr": w["L0_ffn_Wr"], "wq1": l1("wq"), "wo1": l1("wo"),
        "k0": rows(l0("Wk")), "v0": rows(l0("Wv")), "k1": rows(np.concatenate([l1("wk"), l1("bk")[None]], 0)),
        "v1": rows(np.concatenate([l1("wv"), l1("bv")[None]], 0)), "Fc": Fc, "Fs": Fs, "Gc": Gc, "Gs": Gs,
        "are": twice(l0("A_re")), "aim": twice(l0("A_im")), "cre": twice(l0("C_re")), "cim": twice(l0("C_im")), "hm0": hm(H0), "hm1": hm(H1),
        "j": np.tile(np.arange(NJ), (128, 1)), "i": np.tile(np.arange(NI) * NJ, (128, 1)),
    }
    w0 = np.concatenate([parts[k].astype(np.float32) for k in W0_AT], 1)
    parts = {
        "g_in": l0("g_norm_in"), "b_in": l0("b_norm_in"), "g_ffn": l0("g_ffn"), "b_ffn": l0("b_ffn"), "g_out": l0("g_norm_out"),
        "b_out": l0("b_norm_out"), "b2": l0("b2"), "film": np.concatenate([l0("b_film_in"), l0("b_film_out")]), "br": w["L0_ffn_br"], "bo": l1("bo"),
        "gates": np.stack([w["g_xattn"][0], w["g_ffn"][0], w["g_xattn"][1], w["g_ffn"][1]]), "mod": l0("mod_gate").reshape(1),
        "log_dt": l0("log_dt"), "dskip": l0("D_skip"), "experts": np.arange(NE),
    }
    r0 = np.concatenate([parts[k].astype(np.float32) for k in R0_AT])
    m0 = (np.arange(128) < NS).astype(np.float32)[:, None]
    z = (np.arange(128) == 0).astype(np.float32)[:, None]
    parts = {"b1": l0("b1").reshape(4, 128).T, "bq": l1("bq")[:, None], "mb1": w["L0_ffn_b1"].reshape(4 * NE, 128).T,
             "m0": m0, "m1": 1 - m0, "-m0": -m0, "-m1": m0 - 1, "off": 0.25 * m0, "nz": 1 - z, "z": z}
    cols = np.concatenate([parts[k].astype(np.float32) for k in C_AT], 1)
    ctx = np.ones((DC + 1, B * S2), np.float32)
    ctx[:DC] = w["ctx_768"].transpose(2, 0, 1).reshape(DC, B * S2)
    return {"w_l1": wall, "r_l1": rall, "w0": w0, "r0": r0, "cols": cols, "ctx": ctx, "b2m": w["L0_ffn_b2"],
            "mw1": w["L0_ffn_W1"].transpose(1, 0, 2).reshape(128, NE * FE),
            "mw2": w["L0_ffn_W2"].reshape(NE, 4, 128, D).transpose(2, 0, 1, 3).reshape(128, NE * 4 * D),
            "tmask": w["mask_BxS_bf1"].T.view(np.uint8), "vmask": w["mask_BxS2_bf1"].reshape(1, B * S2).view(np.uint8),
            "x": w["x"]}


def kernel(**inputs):
    import concourse.bacc as _bacc
    from concourse.bass_utils import run_bass_kernel_spmd

    arrays = dict(constants(), **layout(inputs))
    arrays = {name: np.ascontiguousarray(x) for name, x in arrays.items()}
    nc = _bacc.Bacc("TRN2", target_bir_lowering=False, num_devices=1)
    a = {name: nc.dram_tensor(name, x.shape, mybir.dt.from_np(x.dtype), kind="ExternalInput").ap() for name, x in arrays.items()}
    out = nc.dram_tensor("out", (B, T, D), F32, kind="ExternalOutput").ap()
    flamingo(nc, a, out)
    r = run_bass_kernel_spmd(nc, [arrays], core_ids=[0])
    return r.results[0]["out"]
```

```python
from contextlib import ExitStack

import numpy as np

import concourse.bass as bass
from concourse import mybir

F32 = mybir.dt.float32
I32 = mybir.dt.int32
U8 = mybir.dt.uint8
BF16 = mybir.dt.bfloat16
ALU = mybir.AluOpType
ACT = mybir.ActivationFunctionType
AX = mybir.AxisListType

B = 16
T = 128
D = 128
S2 = 77
DC = 96
EPS = 1e-5
BIG = 1.0e30
BIG16 = -(2.0 ** 100)
GONE = -3.0e38

H0, DH0 = 4, 32
TOPK = 32
HID = 4 * D
NS = 64
NJ, NI = 16, 8
TURN = 6.283185
ROUND = 1.5 * 2.0 ** 23
NE, FE = 8, 512
GB = 4
NG = B // GB
H1, DH1 = 16, 8
SCALE1 = float(1.0 / np.sqrt(DH1))
SPANS = [(0, 5), (5, 5), (10, 6)]

DEPTH = 6
NH = 16
E = 64
WINDOW = 32
INNER = NH * E
FF = int(D * 4 * 2 / 3)
QK_SCALE = 8.0
FC = 3
W_QKV, W_O, W_1, W_2 = 0, 3 * INNER, 3 * INNER + INNER, 3 * INNER + INNER + 2 * FF
W_ALL = W_2 + FC * D
R_G, R_B, R_B1, R_B2, R_QS, R_KS = 0, D, 2 * D, 2 * D + 2 * FF, 3 * D + 2 * FF, 3 * D + 2 * FF + 2 * E
R_ALL = R_KS + 2 * E
UNITS = B * DEPTH
LAYER_BITS = B.bit_length() - 1
LOAD, PROJ, SCORE, VALUE, CENTRE, UP, GATE, DOWN = range(8)
STAGES = 8
AHEAD = DOWN - VALUE

def offsets(*sizes):
    at, o = {}, 0
    for name, n in sizes:
        at[name] = (o, n)
        o += n
    return at, o


N_CONST = 10 + DEPTH
R0_AT, R0_ALL = offsets(("g_in", D), ("b_in", D), ("g_ffn", D), ("b_ffn", D), ("g_out", D), ("b_out", D), ("b2", D), ("film", 4 * D),
                        ("br", NE), ("bo", D), ("gates", 4), ("mod", 1), ("log_dt", D), ("dskip", D), ("experts", NE))
W0_AT, W0_ALL = offsets(("Wq", 128), ("film", 512), ("W1", HID), ("W2", HID), ("Wr", NE), ("wq1", 128), ("wo1", 128), ("k0", 128), ("v0", 128),
                        ("k1", 128), ("v1", 128), ("Fc", 128), ("Fs", 128), ("Gc", 128), ("Gs", 128), ("are", 128), ("aim", 128), ("cre", 128),
                        ("cim", 128), ("hm0", H0), ("hm1", H1), ("j", NJ), ("i", NI), ("lanes", 128))
C_AT, C_ALL = offsets(("b1", 4), ("bq", 1), ("mb1", 4 * NE), ("m0", 1), ("m1", 1), ("-m0", 1), ("-m1", 1), ("off", 1), ("nz", 1), ("z", 1))

RSQRT_MAGIC = float(0x5F3759DF)
RSQRT_STEPS = 3
RSQRT = ["shift", "guess"] + [f"{s}{i}" for i in range(RSQRT_STEPS) for s in ("square", "half", "newton")]
SETUP = [
    "identb", "band",
    "dta_re", "dta_im", "turns", "cos_turns", "cos_whole", "cos_frac", "sin_turns", "sin_whole", "sin_frac", "e_re", "e_im",
    "e_re_less_1", "c_e_rr", "c_e_ii", "num_re", "c_e_ri", "c_e_ir", "num_im", "a_rr", "a_ii", "a_abs2", "a_inv", "scale", "n_a_rr",
    "n_a_ii", "dc_re_num", "dc_re", "n_a_ir", "n_a_ri", "dc_im_num", "dc_im", "row_cos_0", "row_cos", "row_sin_0", "row_sin",
    "sin_i_turns", "cos_i_turns", "cos_i_whole", "cos_i_frac", "sin_i_whole", "sin_i_frac", "wave_j_turns", "wave_j_off",
    "wave_j_whole", "wave_j_frac", "arg_i", "arg_j", "cos_i_mag", "sin_i_mag", "row_i_cos", "row_i_sin", "row_i", "power_j", "rows",
    "f_cos", "f_sin", "f_half", "f_flip", "text_mask", "context_mask",
]


class Steps:

    def __init__(self, sem, names, lead=1):
        self.sem, self.names, self.lead, self.turn = sem, names, lead, 0

    def start(self):
        return self.lead * len(self.names)

    def at(self, name, n):
        return n * len(self.names) + (self.start() + self.names.index(name) + 1)

    def step(self, name):
        assert self.names[self.turn % len(self.names)] == name, (name, self.names[self.turn % len(self.names)])
        self.turn += 1
        return 1


def pipeline(eng, body, depth, count, base):
    for t in range(depth - 1):
        body([(t - s, base + (t - s)) if s <= t else None for s in range(depth)])
    with eng.Fori(depth - 1, count) as i:
        body([(i - s, i - s + base) if s else (i, i + base) for s in range(depth)])
    for t in range(count, count + depth - 1):
        body([(t - s, base + (t - s)) if t - s < count else None for s in range(depth)])


def rsqrt(dve, S, n, pre, y, h, v):
    yi, vi = y.bitcast(I32), v.bitcast(I32)
    dve.tensor_scalar(yi, vi, 1, None, ALU.logical_shift_right).then_inc(S.sem, S.step(pre + "shift"))
    dve.wait_ge(S.sem, S.at(pre + "shift", n))
    dve.tensor_scalar(yi, yi, -1.0, RSQRT_MAGIC, ALU.mult, ALU.add).then_inc(S.sem, S.step(pre + "guess"))
    last = "guess"
    for i in range(RSQRT_STEPS):
        dve.wait_ge(S.sem, S.at(pre + last, n))
        dve.tensor_tensor(h, y, y, ALU.mult).then_inc(S.sem, S.step(pre + f"square{i}"))
        dve.wait_ge(S.sem, S.at(pre + f"square{i}", n))
        dve.scalar_tensor_tensor(h, h, -0.5, v, ALU.mult, ALU.mult).then_inc(S.sem, S.step(pre + f"half{i}"))
        dve.wait_ge(S.sem, S.at(pre + f"half{i}", n))
        dve.scalar_tensor_tensor(y, h, 1.5, y, ALU.add, ALU.mult).then_inc(S.sem, S.step(pre + f"newton{i}"))
        last = f"newton{i}"


NORM = ["stats", "aggr", "eps", "xn"]


def normalise(dve, S, G, n, out, x, N, s_pass):
    moments(dve, S, G, n, x, N, s_pass)
    centre(dve, S, G, n, out, x, N)


def moments(dve, S, G, n, x, N, s_pass):
    stats, mv, vv = N[:, 0:6], N[:, 6:8], N[:, 8:9]
    dve.sem_inc(s_pass, 1)
    dve.bn_stats(stats, x).then_inc(S.sem, S.step("stats"))
    dve.wait_ge(S.sem, S.at("stats", n))
    dve.sem_inc(s_pass, 1)
    dve.bn_aggr(mv, stats).then_inc(S.sem, S.step("aggr"))
    dve.wait_ge(S.sem, S.at("aggr", n))
    dve.wait_ge(G.sem, G.at("root", n - 1))
    dve.tensor_scalar(vv, mv[:, 1:2], EPS, None, ALU.add).then_inc(S.sem, S.step("eps"))


def root(pool, S, G, n, N, half):
    pool.wait_ge(S.sem, S.at("eps", n))
    pool.wait_ge(S.sem, S.at("xn", n - 1))
    pool.tensor_tensor(N[:, 9:10], N[:, 8:9], half, ALU.pow).then_inc(G.sem, G.step("root"))


def centre(dve, S, G, n, out, x, N):
    dve.wait_ge(G.sem, G.at("root", n))
    dve.tensor_scalar(out, x, N[:, 6:7], N[:, 9:10], ALU.subtract, ALU.mult).then_inc(S.sem, S.step("xn"))


def flamingo(nc, a, out):
    with ExitStack() as ctx:
        def sb(name, shape, dt=F32):
            return ctx.enter_context(nc.sbuf_tensor(name, shape, dt))

        def sem(name):
            return ctx.enter_context(nc.semaphore(name))

        def steps(name, names, lead=1):
            return Steps(sem(name), names, lead)

        X = sb("X", [T, B, D])
        XD = sb("XD", [T, B, D])
        XS = sb("XS", [T, B, D])
        ident = sb("ident_sb", [128, 128])
        zeros = sb("zeros", [128, 128])
        half = sb("minus_half", [128, 1])
        identb = sb("identb_sb", [128, 128], BF16)

        band = sb("band_sb", [128, 4, 128], BF16)
        rope = sb("rope_sb", [128, 4, E])
        arena = sb("arena", [128, 18 * 1024])
        taken = [0]

        def part(*shape, at=None):
            n = int(np.prod(shape))
            o = taken[0] if at is None else at
            taken[0] = o + n
            assert taken[0] <= 18 * 1024
            ap = arena[:, o:o + n]
            if len(shape) == 2:
                return ap.rearrange("p (a b) -> p a b", a=shape[0])
            if len(shape) == 3:
                return ap.rearrange("p (a b c) -> p a b c", a=shape[0], b=shape[1])
            return ap

        WL = sb("WL", [128, 2, W_ALL])
        RL = sb("RL", [128, 2, R_ALL])
        RT = sb("RT", [128, DEPTH + 1, 4 * E])
        xc = sb("xc", [T, D])
        xsT = sb("xsT", [D, T])
        WLf = WL[:].rearrange("p a n -> p (a n)")
        RLf = RL[:].rearrange("p a n -> p (a n)")
        RTf = RT[:].rearrange("p a n -> p (a n)")
        sq = part(2, INNER)
        ss = sb("ss", [T, 2, NH])
        rn = sb("rn", [T, 2, NH])
        rh = sb("rh", [T, 2, NH])
        qn = part(2, INNER)
        rc = part(2, INNER)
        rs = part(2, INNER)
        qT = part(8, T)
        kbd = part(8, 2, T)
        v = part(INNER)
        mx = sb("mx", [T, NH])
        sc = sb("sc", [T, NH])
        warm = sb("warm", [128, 2])
        nm = sb("nm", [T, NH])
        prob = part(NH, T)
        psums = sb("psums", [T, NH])
        rsum = sb("rsum", [T, NH])
        probT = part(NH, T)
        vn = part(INNER)
        oT = part(8, T)

        R0 = sb("R0", [128, R0_ALL])
        W0 = sb("W0", [128, W0_ALL])
        CO = sb("CO", [128, C_ALL])
        CX = sb("CX", [DC + 1, B, S2])
        b2m = sb("b2m_sb", [NE, D])
        tm8 = sb("tm8", [T, B], U8)
        vm8 = sb("vm8", [1, B * S2], U8)
        tm = sb("tm", [T, B])
        vm = sb("vm", [1, B, S2])
        ones = sb("ones", [1, 128])
        tg = sb("tg", [128, 4])
        KF = sb("KF", [128, 3, 128])
        CB = sb("CB", [T, B, NE])
        N1 = sb("N1", [T, 11])
        N2 = sb("N2", [T, 11])

        def w0(name, n=None, k=128):
            o, m = W0_AT[name]
            return W0[0:k, o:o + (n or m)]

        def r0(name):
            o, m = R0_AT[name]
            return R0[:, o:o + m]

        def co(name, i=0):
            o, m = C_AT[name]
            return CO[:, o + i:o + i + 1]

        MW1 = part(NE, FE, at=0)
        MW2 = part(NE, 4, 128, at=4096)
        FO = part(B, 2 * D, at=8192)
        U = part(B, D, at=12288)
        f0 = 14336
        sP, sT1, sT2 = part(128, NJ, at=f0), part(128, NJ, at=f0 + 2048), part(128, NJ, at=8192)
        sQ, sQ2, sQ3, sQc = part(128, NI, at=8192 + 2048), part(128, NI, at=8192 + 3072), part(128, NI, at=12288), part(128, NI, at=12288 + 1024)
        sS = XS[:].rearrange("p b d -> p (b d)")
        KS = XD[:].rearrange("p b d -> p (b d)")[:, 0:1024].rearrange("p (i d) -> p i d", i=NI)
        KT = sS[:, 15 * 128:16 * 128]
        ax, axT, aqT = part(D, at=f0), part(T, at=f0 + 128), part(T, at=f0 + 256)
        akb, work, esub, eexp = (part(H0, S2, at=f0 + 384 + 308 * i) for i in range(4))
        esel = part(H0, S2, at=f0 + 384 + 308 * 4)
        o = f0 + 384 + 308 * 5
        m8 = part(H0, 8, at=o)
        m8r = part(2, H0, 8, at=o + 700 + 140)
        es = part(H0, at=o + 32)
        ew = part(H0, at=o + 36)
        at_ = part(S2, at=o + 40)
        aT, avT = part(T, at=o + 120), part(S2, at=o + 248)
        avf = part(512, at=o + 328)
        fm = sb("film_m", [T, 256])
        t1, t2, t3, t4 = (part(512, at=f0 + 512 * i) for i in range(4))
        Yr, Yi = part(512, at=f0 + 2048), part(512, at=f0 + 2560)
        chT = part(T, at=f0)
        cgT = part(4, T, at=f0 + 128)
        cy, cx, cx2 = part(D, at=f0 + 640), part(D, at=f0 + 768), part(D, at=f0 + 896)
        ACC = XD
        XTA = part(B, T, at=8192)
        gT = [part(4, 512, at=8192 + 2048), part(4, 512, at=12288)]
        mxT = part(T, at=f0 + 512)
        l8, e8, i8f, c0, c1, c2 = (part(NE, at=f0 + 128 + 8 * i) for i in range(6))
        i8 = part(NE, at=f0 + 200)
        ed = part(4, at=f0 + 208)
        cT = part(T, at=f0 + 256)
        dx, dxT, dqT, dk, dcx = part(D, at=0), part(T, at=128), part(T, at=256), part(S2, at=384), part(S2, at=512)
        dkb, dsub, dpr = part(H1, S2, at=1024), part(H1, S2, at=3072), part(H1, S2, at=5120)
        dpT = part(H1, T, at=7168)
        dv, doT, dyb = part(D, at=9216), part(T, at=9472), part(D, at=9600)
        dvm = part(4, 4, 32, at=9792)
        dmx, dsum, dinv = part(H1, at=9728), part(H1, at=9744), part(H1, at=9760)

        pA = ctx.enter_context(nc.psum_tensor("pA", [128, 2, 512], F32))
        pB = ctx.enter_context(nc.psum_tensor("pB", [128, 2, 512], F32))
        pC = ctx.enter_context(nc.psum_tensor("pC", [128, 2, 512], F32))
        pD = ctx.enter_context(nc.psum_tensor("pD", [128, 2, 512], F32))

        def heads(p):
            return p[:].rearrange("p b (h e) -> p (b h) e", e=E)

        def blocks(p):
            return p[:].rearrange("p b (c t) -> p (b c) t", t=128)

        def flat(p):
            return p[:].rearrange("p b n -> p (b n)")

        ldc = sem("constants_loaded")
        s_w = [sem("w_even"), sem("w_odd")]
        s_zero = sem("zeroed")
        s_sh = sem("shift_attn")
        s_shf = sem("shift_ffn")
        s_out = sem("s_out")
        s_layer = sem("layer_loaded")
        s_pass = sem("wait_passed")

        def stack_steps(name, names):
            return steps(name, names, lead=STAGES)

        AP1 = stack_steps("attn_proj_pe", ["xT", "q", "k", "v", "qT", "kT"])
        AP2 = stack_steps("attn_score_pe", ["S0", "S1"])
        AP3 = stack_steps("attn_value_pe", ["PT0", "PT1", "O", "y"])
        AA1 = stack_steps("attn_proj_act", ["xsT", "q_out", "k_out", "k_sq", "q_sq", "v_out", "qT_out", "kT_out"])
        AA2 = stack_steps("attn_score_act", ["exp0", "exp1"])
        AA3 = stack_steps("attn_value_act", ["pT0", "oT_out"])
        AW = stack_steps("tables_warm", ["exp", "gelu"])
        AV1 = stack_steps("attn_proj_dve", ["q_s", "k_s", "k_ss", "q_ss", "floor"] + RSQRT + ["k_n", "kT_out"])
        AV2 = stack_steps("attn_score_dve", ["max0", "scale", "neg0", "max1", "neg1", "rsum0", "rsum1"])
        AV3 = stack_steps("attn_value_dve", ["pT1", "x_out"])
        AG0 = stack_steps("attn_in_pool", ["xc"])
        AG1 = stack_steps("attn_proj_pool", ["q_c", "k_c", "q_r", "k_r"])
        AG2 = stack_steps("attn_score_pool", ["v", "p0", "p1"])
        AG3 = stack_steps("attn_value_pool", ["xs"])
        GT = steps("tables_pool", ["table"], lead=0)

        NF = sb("NF", [T, 11])
        xn = sb("xn", [T, D])
        xg = sb("xg", [T, D])
        xb = sb("xb", [T, D])
        xnT = sb("xnT", [D, T])
        hb = sb("hb", [T, 2, FF])
        gg = sb("gg", [T, FF])
        mg = sb("mg", [T, FC * 128])
        mT = sb("mT", [128, FC, T])
        yb = sb("yb", [T, D])
        a2, ag, ay, u1 = xn, xnT, xsT, yb
        fb = hb[:].rearrange("p a f -> p (a f)")[:, 0:4 * D]
        FV1 = stack_steps("ffn_norm_dve", NORM)
        FG0 = stack_steps("ffn_root_pool", ["root"])
        FG1 = stack_steps("ffn_norm_pool", ["g", "b"])
        FP2 = stack_steps("ffn_up_pe", ["xT", "h"])
        FA2 = stack_steps("ffn_up_act", ["xT_out"])
        FV2 = stack_steps("ffn_up_dve", ["bias"])
        FV3 = stack_steps("ffn_gate_dve", ["gated"])
        FA3 = stack_steps("ffn_gate_act", ["gelu"])
        FP4 = stack_steps("ffn_down_pe", ["mT", "y"])
        FA4 = stack_steps("ffn_down_act", ["mT_out"])
        FV4 = stack_steps("ffn_down_dve", ["yb", "x_out"])
        FG4 = steps("ffn_down_pool", ["xs"], lead=B)

        s_mw, s_kt, s_set, s_x = sem("expert_weights"), sem("kernel_turned"), sem("front_set"), sem("x_loaded")
        s_clear, s_shx = sem("cleared"), sem("shift_x1")
        s_sp, s_ks = sem("setup_pe"), sem("kernel_rows")
        V1a = steps("x0_norm_dve", NORM + ["keep"])
        P1b = steps("x0_score_pe", ["xT", "k", "Q", "S"])
        A1b = steps("x0_score_act", ["xT_out", "Q_out"])
        V1b = steps("x0_score_dve", ["kbd"])
        A1c = steps("x0_topk_act", ["work", "exp"])
        V1c = steps("x0_topk_dve", [f"{x}{r}" for r in range(TOPK // 8) for x in ("max", "rep")] + ["sub", "sel", "sum", "inv", "tm", "wt", "mean"])
        P1d = steps("x0_film_pe", ["vT", "aT", "vf", "film"])
        A1d = steps("x0_film_act", ["vT_out", "aT_out", "vf_out"])
        V1d = steps("x0_film_dve", NORM + ["fb", "u1", "u"])
        G1d = steps("x0_film_pool", ["g", "b", "fm", "fo"])
        P2a = steps("conv_pe", ["F"])
        V2a = steps("conv_dve", ["t1", "t2", "Yr", "t3", "t4", "Yi"])
        P2b = steps("conv_back_pe", ["G"])
        A2b = steps("conv_back_act", ["cv"])
        V3a = steps("f0_norm_dve", ["z1", "z", "xt"] + NORM)
        G3a = steps("f0_norm_pool", ["g", "b"])
        P3b = steps("f0_up_pe", ["hT", "h"])
        A3b = steps("f0_up_act", ["hT_out", "gelu"])
        P3c = steps("f0_down_pe", ["y"])
        V3c = steps("f0_down_dve", ["yb", "xt"] + NORM)
        G3c = steps("f0_down_pool", ["g", "b"])
        V3d = steps("f0_out_dve", ["x_out"])
        V4a = steps("moe_norm_dve", NORM)
        P4b = steps("moe_route_pe", ["xT", "lg"])
        A4b = steps("moe_route_act", ["xT_out"])
        G4b = steps("moe_route_pool", ["keep"])
        V4c = steps("moe_top_dve", ["lb", "max", "idx", "idxf", "gap", "den", "w0", "w1", "c0", "c1", "cb", "keep"])
        A4c = steps("moe_top_act", ["exp"])
        P4d = steps("moe_bias_pe", ["cT", "bb"])
        A4d = steps("moe_bias_act", ["cT_out"])
        V4d = steps("moe_bias_dve", ["acc"])
        pe_experts = [f"h{e}{c}" for c in range(4) for e in [0]]
        for e in range(1, NE + 1):
            pe_experts += ([f"h{e}{c}" for c in range(4)] if e < NE else []) + [f"y{e - 1}"]
        P4e = steps("expert_pe", pe_experts)
        A4e = steps("expert_act", [f"g{e}{c}" for e in range(NE) for c in range(4)])
        V4e = steps("expert_dve", [f"acc{e}" for e in range(NE)])
        V5a = steps("x1_norm_dve", ["x_in"] + NORM)
        P5b = steps("x1_score_pe", ["xT", "k", "q", "S"])
        A5b = steps("x1_score_act", ["xT_out", "k_out", "q_out"])
        G5b = steps("x1_score_pool", ["kbd"])
        V5c = steps("x1_soft_dve", ["max", "sub", "sum", "inv"])
        A5c = steps("x1_soft_act", ["exp"])
        G5d = steps("x1_out_pool", ["cx", "vm"])
        G5c = steps("x1_soft_pool", ["p"])
        P5d = steps("x1_out_pe", ["v", "PT0", "PT1", "O", "y"])
        A5d = steps("x1_out_act", ["v_out", "pT0", "oT_out"])
        V5d = steps("x1_out_dve", ["pT1", "yb", "x_out"])
        V5e = steps("x1_next_dve", NORM)
        G5e = steps("x1_next_pool", ["xs"])
        VF = steps("final_dve", ["x"])
        N1a, N1d, N3a, N3c, N4a, N5a, N5e = (steps(f"{x}_root", ["root"]) for x in ("x0_in", "x0_norm", "f0_in", "f0_norm", "moe", "x1", "x1_next"))
        front = (V1a, P1b, A1b, V1b, A1c, V1c, P1d, A1d, V1d, G1d, P2a, V2a, P2b, A2b, V3a, G3a, P3b, A3b, P3c, V3c, G3c,
                 V3d, V4a, P4b, A4b, G4b, V4c, A4c, P4d, A4d, V4d, P4e, A4e, V4e, V5a, P5b, A5b, G5b, V5c, A5c, G5d, P5d, A5d, V5d, V5e, G5e, VF,
                 N1a, N1d, N3a, N3c, N4a, N5a, N5e, G5c)

        def after(eng, last, *done):
            for S in done:
                eng.wait_ge(S.sem, S.at(S.names[-1], last))

        q = [sS[:, 128 * i:128 * i + 128] for i in range(15)]
        (dt, dta_re, dta_im, turns, cos, sin, e_re, e_im, mag, num_re, num_im, scale, dc_re, dc_im, spare) = q
        are, aim, cre, cim = w0("are"), w0("aim"), w0("cre"), w0("cim")
        SV = steps("setup_dve", SETUP, lead=0)
        SA = steps("setup_act", ["dt", "gates", "cos", "sin", "mag", "cos_i", "sin_i", "wave_j", "mag_i", "mag_j"], lead=0)

        block = ctx.enter_context(nc.Block())

        def value(eng, x):
            return x if isinstance(x, int) else eng.snap(x)

        def of_unit(eng, n):
            return n & (B - 1), (n >> LAYER_BITS) & 1

        def shifted(sp, b):
            return XS[1:T, b, D // 2:D], XD[0:T - 1, b, D // 2:D]

        @block.sync
        def _(sp):
            sp.dma_start(ident[:], a["ident"]).then_inc(ldc, 16)
            sp.dma_start(xg[:], a["band"]).then_inc(ldc, 16)
            for l in range(DEPTH):
                sp.dma_start(RT[:, l, :], a["r_l1"][l, R_QS:R_ALL].partition_broadcast(128)).then_inc(ldc, 16)
            sp.dma_start(rope[:], a["rope"].rearrange("p (a b) -> p a b", a=4)).then_inc(ldc, 16)
            sp.dma_start(W0[:], a["w0"]).then_inc(ldc, 16)
            sp.dma_start(R0[:], a["r0"].partition_broadcast(128)).then_inc(ldc, 16)
            sp.dma_start(CO[:], a["cols"]).then_inc(ldc, 16)
            sp.dma_start(CX[:], a["ctx"].rearrange("p (b s) -> p b s", b=B)).then_inc(ldc, 16)
            sp.dma_start(b2m[:], a["b2m"]).then_inc(ldc, 16)
            sp.dma_start(tm8[:], a["tmask"]).then_inc(ldc, 16)
            sp.dma_start(vm8[:], a["vmask"]).then_inc(ldc, 16)
            sp.dma_start(X[:], a["x"].rearrange("b t d -> t b d")).then_inc(s_x, 16)
            sp.dma_start(MW1[:], a["mw1"].rearrange("p (e f) -> p e f", e=NE)).then_inc(s_mw, 16)
            sp.dma_start(MW2[:], a["mw2"].rearrange("p (e c d) -> p e c d", e=NE, c=4)).then_inc(s_mw, 16)
            sp.wait_ge(s_ks, 1)
            for i in range(NI):
                sp.dma_start(KT[NJ * i:NJ * i + NJ, :], KS[0:NJ, i, :]).then_inc(s_kt, 16)
            for l in range(2):
                sp.dma_start(WL[:, l, :], a["w_l1"][l]).then_inc(s_w[l], 16)
                sp.dma_start(RL[:, l, :], a["r_l1"][l].partition_broadcast(128)).then_inc(s_w[l], 16)

            def x1(u):
                if u[4]:
                    b, n = u[4]
                    sp.wait_ge(V5e.sem, V5e.at("xn", n))
                    sp.sem_inc(s_pass, 1)
                    sp.wait_ge(s_shx, n * 16 + 16)
                    dst, src = shifted(sp, b)
                    sp.sem_inc(s_pass, 1)
                    sp.dma_start(dst, src).then_inc(s_shx, 16)

            pipeline(sp, x1, 5, B, 0)

            for l in range(2):
                sp.wait_ge(s_w[l], 32)
                sp.sem_inc(s_layer, 1)

            def attn_shift(b, n):
                sp.wait_ge(AV3.sem, AV3.at("x_out", n))
                sp.sem_inc(s_pass, 1)
                dst, src = shifted(sp, b)
                sp.wait_ge(s_sh, n * 16 + 16)
                sp.sem_inc(s_pass, 1)
                sp.dma_start(dst, src).then_inc(s_sh, 16)

            def ffn_shift(b, n):
                sp.wait_ge(FV4.sem, FV4.at("x_out", n))
                sp.sem_inc(s_pass, 1)
                dst, src = shifted(sp, b)
                sp.wait_ge(s_shf, n * 16 + 16 * B)
                sp.sem_inc(s_pass, 1)
                sp.dma_start(dst, src).then_inc(s_shf, 16)

            for n in range(AHEAD):
                attn_shift(n, n)

            def shifts(base, first, last):
                with sp.Fori(first, last) as b:
                    attn_shift(sp.snap((b + AHEAD) & (B - 1)), b + (base + AHEAD))
                    ffn_shift(b, b + base)

            with sp.Fori(0, DEPTH // 2 - 1) as lp:
                for l in range(2):
                    base = sp.snap(lp * (2 * B) + l * B)
                    shifts(base, 0, B)
                    sp.wait_ge(FP4.sem, FP4.at("y", base + (B - 1)))
                    sp.sem_inc(s_pass, 1)
                    sp.dma_start(WL[:, l, :], a["w_l1"][lp * 2 + (l + 2)]).then_inc(s_w[l], 16)
                    sp.dma_start(RL[:, l, :], a["r_l1"][lp * 2 + (l + 2)].partition_broadcast(128)).then_inc(s_w[l], 16)
                    sp.wait_ge(s_w[l], lp * 32 + 64)
                    sp.sem_inc(s_layer, 1)
            shifts((DEPTH - 2) * B, 0, B)
            shifts((DEPTH - 1) * B, 0, B - AHEAD)
            n = UNITS - 1
            for m in range(UNITS - AHEAD, UNITS):
                ffn_shift(m & (B - 1), m)
            for g in range(NG):
                sp.wait_ge(VF.sem, VF.at("x", g))
                sp.dma_start(out.rearrange("b t d -> t b d")[:, GB * g:GB * g + GB, :], X[:, GB * g:GB * g + GB, :]).then_inc(s_out, 16)
            sp.wait_ge(s_out, 16 * NG)
            sp.wait_ge(s_shx, 16 * (B + 1))
            sp.wait_ge(s_sh, 16 * (n + 2))
            sp.wait_ge(s_shf, 16 * (n + 1 + B))
            for l in range(2):
                sp.wait_ge(s_w[l], 32 * (DEPTH // 2))

        @block.gpsimd
        def _(pool):
            for c in (AP1, AP2, AP3, AA1, AA2, AA3, AW, AV1, AV2, AV3, AG0, AG1, AG2, AG3, FV1, FG0, FG1, FP2, FA2, FV2, FV3, FA3, FP4, FA4, FV4, FG4):
                pool.sem_inc(c.sem, c.start())
            pool.sem_inc(s_shf, 16 * B)
            pool.sem_inc(s_sh, 16)
            pool.sem_inc(s_shx, 16)
            for c in front:
                pool.sem_inc(c.sem, c.start())
            pool.memset(ones[:], 1.0).then_inc(s_zero, 1)
            pool.memset(zeros[:], 0.0).then_inc(s_zero, 1)
            pool.memset(mg[:], 0.0).then_inc(s_zero, 1)
            pool.memset(half[:], -0.5).then_inc(s_zero, 1)
            pool.wait_ge(s_zero, 4)
            pool.wait_ge(ldc, 16 * N_CONST)
            pool.wait_ge(s_set, 1)
            pool.memset(XS[0:1, :, D // 2:D], 0.0).then_inc(s_clear, 1)

            def x0(u):
                if u[3]:
                    b, n = u[3]
                    root(pool, V1d, N1d, n, N2, half[:])
                    pool.wait_ge(V1d.sem, V1d.at("xn", n))
                    pool.wait_ge(G1d.sem, G1d.at("b", n - 1))
                    pool.tensor_tensor(ag[:], a2[:], r0("g_in"), ALU.mult).then_inc(G1d.sem, G1d.step("g"))
                    pool.wait_ge(G1d.sem, G1d.at("g", n))
                    pool.wait_ge(V1d.sem, V1d.at("u1", n - 1))
                    pool.tensor_tensor(ay[:], ag[:], r0("b_in"), ALU.add).then_inc(G1d.sem, G1d.step("b"))
                    pool.wait_ge(V1d.sem, V1d.at("fb", n))
                    pool.wait_ge(V1d.sem, V1d.at("u", n - 1))
                    mod = r0("mod").to_broadcast([T, 2 * D])
                    pool.tensor_tensor(fm[:], fb[:, 0:2 * D], mod, ALU.mult).then_inc(G1d.sem, G1d.step("fm"))
                    pool.tensor_tensor(FO[:, b, :], fb[:, 2 * D:4 * D], mod, ALU.mult).then_inc(G1d.sem, G1d.step("fo"))
                if u[0]:
                    b, n = u[0]
                    root(pool, V1a, N1a, n, N1, half[:])

            def f0(u):
                if u[2]:
                    b, n = u[2]
                    root(pool, V3c, N3c, n, N2, half[:])
                    pool.wait_ge(V3c.sem, V3c.at("xn", n))
                    pool.wait_ge(G3c.sem, G3c.at("b", n - 1))
                    pool.tensor_tensor(ag[:], a2[:], r0("g_out"), ALU.mult).then_inc(G3c.sem, G3c.step("g"))
                    pool.wait_ge(G3c.sem, G3c.at("g", n))
                    pool.wait_ge(V3d.sem, V3d.at("x_out", n - 1))
                    pool.tensor_tensor(ay[:], ag[:], r0("b_out"), ALU.add).then_inc(G3c.sem, G3c.step("b"))
                if u[0]:
                    b, n = u[0]
                    root(pool, V3a, N3a, n, N1, half[:])
                    pool.wait_ge(V3a.sem, V3a.at("xn", n))
                    pool.wait_ge(G3a.sem, G3a.at("b", n - 1))
                    pool.tensor_tensor(cx2[:], cx[:], r0("g_ffn"), ALU.mult).then_inc(G3a.sem, G3a.step("g"))
                    pool.wait_ge(G3a.sem, G3a.at("g", n))
                    pool.wait_ge(P3b.sem, P3b.at("hT", n - 1))
                    pool.tensor_tensor(cy[:], cx2[:], r0("b_ffn"), ALU.add).then_inc(G3a.sem, G3a.step("b"))

            def route(u):
                if u[1]:
                    b, n = u[1]
                    pool.wait_ge(A4b.sem, A4b.at("xT_out", n))
                    pool.tensor_tensor(XTA[:, b, :], mxT[:], zeros[:], ALU.add).then_inc(G4b.sem, G4b.step("keep"))
                if u[0]:
                    b, n = u[0]
                    root(pool, V4a, N4a, n, N1, half[:])

            def x1(u):
                if u[3]:
                    b, n = u[3]
                    pool.wait_ge(P5d.sem, P5d.at("v", n - 1))
                    pool.tensor_tensor(dcx[0:DC + 1, :], CX[:, b, :], zeros[0:DC + 1, 0:S2], ALU.add).then_inc(G5d.sem, G5d.step("cx"))
                if u[3]:
                    b, n = u[3]
                    pool.wait_ge(A5d.sem, A5d.at("v_out", n))
                    pool.wait_ge(P5d.sem, P5d.at("O", n - 1))
                    pool.tensor_tensor(dvm[0:S2], dv[0:S2, :].rearrange("p (g c) -> p g c", g=4).unsqueeze(2).to_broadcast([S2, 4, 4, 32]),
                                       w0("lanes", k=S2).rearrange("p (k c) -> p k c", k=4).unsqueeze(1).to_broadcast([S2, 4, 4, 32]),
                                       ALU.mult).then_inc(G5d.sem, G5d.step("vm"))
                if u[1]:
                    b, n = u[1]
                    pool.wait_ge(A5b.sem, A5b.at("k_out", n))
                    pool.wait_ge(P5b.sem, P5b.at("S", n - 1))
                    pool.tensor_tensor(dkb[:], dk[:].unsqueeze(1).to_broadcast([128, H1, S2]), w0("hm1").unsqueeze(2).to_broadcast([128, H1, S2]),
                                       ALU.mult).then_inc(G5b.sem, G5b.step("kbd"))
                if u[4]:
                    b, n = u[4]
                    root(pool, V5e, N5e, n, N2, half[:])
                if u[0]:
                    b, n = u[0]
                    root(pool, V5a, N5a, n, N1, half[:])
                if u[4]:
                    b, n = u[4]
                    pool.wait_ge(V5e.sem, V5e.at("xn", n))
                    pool.tensor_tensor(XS[:, b, 0:D // 2], XD[:, b, 0:D // 2], zeros[:, 0:D // 2], ALU.add).then_inc(G5e.sem, G5e.step("xs"))
                if u[2]:
                    b, n = u[2]
                    pool.wait_ge(V5c.sem, V5c.at("inv", n))
                    pool.tensor_tensor(dpr, dpr, dinv.unsqueeze(2).to_broadcast([T, H1, S2]), ALU.mult).then_inc(G5c.sem, G5c.step("p"))

            pipeline(pool, x0, 4, B, 0)
            after(pool, NG - 1, A2b)
            pipeline(pool, f0, 4, B, 0)
            after(pool, B - 1, V3d)
            pipeline(pool, route, 4, B, 0)
            after(pool, NG - 1, V4e)
            pipeline(pool, x1, 5, B, 0)
            after(pool, B - 1, V5e)
            pool.memset(kbd[:], 0.0).then_inc(s_clear, 1)
            pool.wait_ge(s_shx, 16 * (B + 1))
            pool.sem_inc(s_clear, 1)
            pool.wait_ge(s_clear, 3)

            for l in range(DEPTH):
                pool.tensor_tensor(RT[:, l, :], rope[:].rearrange("p a e -> p (a e)"), RT[:, l, :], ALU.mult).then_inc(GT.sem, GT.step("table"))

            def stack(u):
                if u[CENTRE]:
                    n = u[CENTRE][1]
                    parity = value(pool, of_unit(pool, n)[1] * R_ALL)
                    root(pool, FV1, FG0, n, NF, half[:])
                    pool.wait_ge(FG1.sem, FG1.at("b", n - 1))
                    pool.wait_ge(FV1.sem, FV1.at("xn", n))
                    pool.tensor_tensor(xg[:], xn[:], RLf[:, bass.ds(parity + R_G, D)], ALU.mult).then_inc(FG1.sem, FG1.step("g"))
                    pool.wait_ge(FG1.sem, FG1.at("g", n))
                    pool.wait_ge(FP2.sem, FP2.at("xT", n - 1))
                    pool.tensor_tensor(xb[:], xg[:], RLf[:, bass.ds(parity + R_B, D)], ALU.add).then_inc(FG1.sem, FG1.step("b"))
                if u[PROJ]:
                    n = u[PROJ][1]
                    table = value(pool, (n >> LAYER_BITS) * (4 * E))
                    for j, (name, qk) in enumerate([("q_c", "q"), ("k_c", "k")]):
                        pool.wait_ge(AA1.sem, AA1.at(f"{qk}_out", n))
                        pool.wait_ge(AP1.sem, AP1.at(f"{qk}T", n - 1))
                        r3 = rc[:, j, :].rearrange("p (h e) -> p h e", e=E)
                        q3 = qn[:, j, :].rearrange("p (h e) -> p h e", e=E)
                        cs = RTf[:, bass.ds(table + 2 * j * E, E)].unsqueeze(1).to_broadcast([T, NH, E])
                        pool.tensor_tensor(r3, q3, cs, ALU.mult).then_inc(AG1.sem, AG1.step(name))
                    for j, qk in enumerate("qk"):
                        pool.wait_ge(AV1.sem, AV1.at(f"{qk}_s", n))
                        pool.wait_ge(AG1.sem, AG1.at(f"{qk}_c", n))
                        pool.tensor_tensor(rc[:, j, :], rc[:, j, :], rs[:, j, :], ALU.add).then_inc(AG1.sem, AG1.step(f"{qk}_r"))
                if u[SCORE]:
                    n = u[SCORE][1]
                    pool.wait_ge(AP3.sem, AP3.at("O", n - 1))
                    pool.wait_ge(AA1.sem, AA1.at("v_out", n))
                    pool.tensor_tensor(v[:], vn[:], zeros[:, 0:1].to_broadcast([T, INNER]), ALU.add).then_inc(AG2.sem, AG2.step("v"))
                    for g in range(2):
                        at = slice(8 * g, 8 * g + 8)
                        pool.wait_ge(AV2.sem, AV2.at(f"rsum{g}", n))
                        pool.tensor_tensor(prob[:, at, :], prob[:, at, :], rsum[:, at].unsqueeze(2).to_broadcast([T, 8, T]), ALU.mult).then_inc(AG2.sem, AG2.step(f"p{g}"))
                if u[LOAD]:
                    n = u[LOAD][1]
                    b = value(pool, of_unit(pool, n)[0])
                    pool.wait_ge(AP1.sem, AP1.at("xT", n - 1))
                    pool.wait_ge(s_shf, n * 16 + 16)
                    pool.wait_ge(FG4.sem, FG4.at("xs", n - B))
                    pool.tensor_tensor(xc[:], XS[:, b, :], zeros[:], ALU.add).then_inc(AG0.sem, AG0.step("xc"))
                for stage, V, G in ((DOWN, FV4, FG4), (VALUE, AV3, AG3)):
                    if u[stage]:
                        n = u[stage][1]
                        b = value(pool, of_unit(pool, n)[0])
                        pool.wait_ge(V.sem, V.at("x_out", n))
                        pool.tensor_tensor(XS[:, b, 0:D // 2], XD[:, b, 0:D // 2], zeros[:, 0:D // 2], ALU.add).then_inc(G.sem, G.step("xs"))

            pipeline(pool, stack, STAGES, UNITS, 0)

        @block.tensor
        def _(pe):
            pe.wait_ge(s_zero, 4)
            pe.wait_ge(ldc, 16 * N_CONST)
            pe.wait_ge(SV.sem, SV.at("power_j", 0))
            for d in range(128):
                ins = pe.matmul(pA[0:NJ, d // 64, (d % 64) * NI:(d % 64) * NI + NI], sP[:, d, :], sQc[:, d, :], start=True, stop=True)
            ins.then_inc(s_sp, 1)
            pe.wait_ge(s_kt, 16 * NI)
            pe.matmul(pB[:, 0, 0:128], w0("Fc"), KT, start=True, stop=True)
            pe.matmul(pB[:, 0, 128:256], w0("Fs"), KT, start=True, stop=True).then_inc(s_sp, 1)
            pe.wait_ge(s_set, 1)

            def x0(u):
                if u[3]:
                    b, n = u[3]
                    pe.wait_ge(A1d.sem, A1d.at("vT_out", n - 1))
                    pe.wait_ge(A1d.sem, A1d.at("aT_out", n - 1))
                    pe.matmul(pC[:, 0, 0:S2], w0("v0", k=DC), CX[0:DC, b, :], start=True, stop=True).then_inc(P1d.sem, P1d.step("vT"))
                    pe.wait_ge(V1c.sem, V1c.at("mean", n))
                    pe.wait_ge(A1d.sem, A1d.at("vT_out", n))
                    pe.transpose(pC[0:S2, 0, 128:256], at_, ident[:]).then_inc(P1d.sem, P1d.step("aT"))
                    pe.wait_ge(A1d.sem, A1d.at("vf_out", n - 1))
                    pe.matmul(pC[0:S2, 1, :], avT, w0("film"), start=True, stop=True).then_inc(P1d.sem, P1d.step("vf"))
                    pe.wait_ge(A1d.sem, A1d.at("vf_out", n))
                    pe.wait_ge(V1d.sem, V1d.at("fb", n - 1))
                    pe.matmul(pD[:, 0, :], aT[0:S2, :], avf[0:S2, :], start=True, stop=True).then_inc(P1d.sem, P1d.step("film"))
                if u[1]:
                    b, n = u[1]
                    pe.wait_ge(V1a.sem, V1a.at("xn", n))
                    pe.wait_ge(A1b.sem, A1b.at("xT_out", n - 1))
                    pe.transpose(pA[:, 0, 0:T], ax, ident[:]).then_inc(P1b.sem, P1b.step("xT"))
                    pe.wait_ge(V1b.sem, V1b.at("kbd", n - 1))
                    pe.matmul(pB[:, 0, 0:S2], w0("k0", k=DC), CX[0:DC, b, :], start=True, stop=True).then_inc(P1b.sem, P1b.step("k"))
                    pe.wait_ge(A1b.sem, A1b.at("xT_out", n))
                    pe.wait_ge(A1b.sem, A1b.at("Q_out", n - 1))
                    pe.matmul(pA[:, 1, 0:T], w0("Wq"), axT, start=True, stop=True).then_inc(P1b.sem, P1b.step("Q"))
                    pe.wait_ge(V1c.sem, V1c.at("sub", n - 1))
                    pe.wait_ge(A1c.sem, A1c.at("work", n - 1))
                    pe.matmul(pB[:, 1, 0:H0 * S2], ones[:], vm[:, b, :].unsqueeze(1).to_broadcast([1, H0, S2]), start=True, stop=False)
                    pe.wait_ge(A1b.sem, A1b.at("Q_out", n))
                    pe.wait_ge(V1b.sem, V1b.at("kbd", n))
                    pe.matmul(pB[:, 1, 0:H0 * S2], aqT, akb.rearrange("p h s -> p (h s)"), start=False, stop=True).then_inc(P1b.sem, P1b.step("S"))

            def conv(u):
                if u[1]:
                    c, n = u[1]
                    pe.wait_ge(V2a.sem, V2a.at("Yi", n))
                    pe.wait_ge(A2b.sem, A2b.at("cv", n - 1))
                    pe.matmul(pB[:, 0, :], w0("Gc"), Yr, start=True, stop=False)
                    pe.matmul(pB[:, 0, :], w0("Gs"), Yi, start=False, stop=True).then_inc(P2b.sem, P2b.step("G"))
                if u[0]:
                    c, n = u[0]
                    uc = U[:, bass.ts(c, GB), :].rearrange("p b d -> p (b d)")
                    pe.wait_ge(V2a.sem, V2a.at("t4", n - 1))
                    pe.matmul(pA[:, 0, :], w0("Fc"), uc, start=True, stop=True)
                    pe.matmul(pA[:, 1, :], w0("Fs"), uc, start=True, stop=True).then_inc(P2a.sem, P2a.step("F"))

            def f0(u):
                if u[2]:
                    b, n = u[2]
                    pe.wait_ge(A3b.sem, A3b.at("gelu", n))
                    pe.wait_ge(V3c.sem, V3c.at("yb", n - 1))
                    for c in range(4):
                        ins = pe.matmul(pC[:, 0, 0:D], cgT[:, c, :], w0("W2")[:, 128 * c:128 * c + 128], start=(c == 0), stop=(c == 3))
                    ins.then_inc(P3c.sem, P3c.step("y"))
                if u[1]:
                    b, n = u[1]
                    pe.wait_ge(G3a.sem, G3a.at("b", n))
                    pe.wait_ge(A3b.sem, A3b.at("hT_out", n - 1))
                    pe.transpose(pA[:, 0, 0:T], cy, ident[:]).then_inc(P3b.sem, P3b.step("hT"))
                    pe.wait_ge(A3b.sem, A3b.at("hT_out", n))
                    pe.wait_ge(A3b.sem, A3b.at("gelu", n - 1))
                    for c in range(4):
                        ins = pe.matmul(pB[:, 0, 128 * c:128 * c + 128], w0("W1")[:, 128 * c:128 * c + 128], chT, start=True, stop=True)
                    ins.then_inc(P3b.sem, P3b.step("h"))

            def route(u):
                if u[3]:
                    b, n = u[3]
                    pe.wait_ge(V4c.sem, V4c.at("cb", n))
                    pe.wait_ge(A4d.sem, A4d.at("cT_out", n - 1))
                    pe.transpose(pC[0:NE, 0, 0:128], c2, ident[:]).then_inc(P4d.sem, P4d.step("cT"))
                    pe.wait_ge(A4d.sem, A4d.at("cT_out", n))
                    pe.wait_ge(V4d.sem, V4d.at("acc", n - 1))
                    pe.matmul(pC[:, 1, 0:D], cT[0:NE, :], b2m[:], start=True, stop=True).then_inc(P4d.sem, P4d.step("bb"))
                if u[1]:
                    b, n = u[1]
                    pe.wait_ge(V4a.sem, V4a.at("xn", n))
                    pe.wait_ge(A4b.sem, A4b.at("xT_out", n - 1))
                    pe.transpose(pA[:, 0, 0:T], ax, ident[:]).then_inc(P4b.sem, P4b.step("xT"))
                    pe.wait_ge(A4b.sem, A4b.at("xT_out", n))
                    pe.wait_ge(V4c.sem, V4c.at("lb", n - 1))
                    pe.matmul(pA[:, 1, 0:NE], mxT, w0("Wr"), start=True, stop=True).then_inc(P4b.sem, P4b.step("lg"))

            def up(g, n, e):
                xt = XTA[:, bass.ts(g, GB), :].rearrange("p b t -> p (b t)")
                for c in range(4):
                    pe.wait_ge(A4e.sem, A4e.at(f"g{(e - 1) % NE}{c}", n - (e == 0)))
                    pe.matmul((pA, pB)[c // 2][:, c % 2, :], MW1[:, e, 128 * c:128 * c + 128], xt, start=True, stop=True).then_inc(P4e.sem, P4e.step(f"h{e}{c}"))

            def down(g, n, e):
                pe.wait_ge(A4e.sem, A4e.at(f"g{e}3", n))
                pe.wait_ge(V4e.sem, V4e.at(f"acc{(e - 2) % NE}", n - (e < 2)))
                for t in range(GB):
                    for c in range(4):
                        ins = pe.matmul(pC[:, e % 2, 128 * t:128 * t + 128], gT[e % 2][:, c, 128 * t:128 * t + 128], MW2[:, e, c, :],
                                        start=(c == 0), stop=(c == 3))
                ins.then_inc(P4e.sem, P4e.step(f"y{e}"))

            def x1(u):
                if u[3]:
                    b, n = u[3]
                    pe.wait_ge(G5d.sem, G5d.at("cx", n))
                    pe.wait_ge(V5d.sem, V5d.at("yb", n - 1))
                    pe.matmul(pD[0:S2, 1, 0:128], dcx[0:DC + 1, :], w0("v1", k=DC + 1), start=True, stop=True).then_inc(P5d.sem, P5d.step("v"))
                    for g in range(2):
                        if g == 0:
                            pe.wait_ge(G5c.sem, G5c.at("p", n))
                            pe.wait_ge(V5d.sem, V5d.at("pT1", n - 1))
                        else:
                            pe.wait_ge(A5d.sem, A5d.at("pT0", n))
                        for c in range(8):
                            ins = pe.transpose(blocks(pB)[0:S2, c, :], dpr[:, 8 * g + c, :], ident[:])
                        ins.then_inc(P5d.sem, P5d.step(f"PT{g}"))
                if u[1]:
                    b, n = u[1]
                    pe.wait_ge(V5a.sem, V5a.at("xn", n))
                    pe.wait_ge(A5b.sem, A5b.at("xT_out", n - 1))
                    pe.transpose(pA[:, 0, 0:T], dx, ident[:]).then_inc(P5b.sem, P5b.step("xT"))
                    pe.wait_ge(A5b.sem, A5b.at("q_out", n - 1))
                    pe.matmul(pA[:, 1, 128:128 + S2], w0("k1", k=DC + 1), CX[:, b, :], start=True, stop=True).then_inc(P5b.sem, P5b.step("k"))
                    pe.wait_ge(A5b.sem, A5b.at("xT_out", n))
                    pe.wait_ge(A5b.sem, A5b.at("k_out", n))
                    pe.matmul(pA[:, 1, 0:128], w0("wq1"), dxT, start=True, stop=True).then_inc(P5b.sem, P5b.step("q"))
                if u[3]:
                    b, n = u[3]
                    pe.wait_ge(A5d.sem, A5d.at("v_out", n))
                    pe.wait_ge(V5d.sem, V5d.at("pT1", n))
                    pe.wait_ge(G5d.sem, G5d.at("vm", n))
                    for i in range(4):
                        for g in range(4):
                            ins = pe.matmul(pD[32 * g:32 * g + 32, 1, 0:T], dvm[0:S2, g, i, :], dpT[0:S2, 4 * g + i, :], start=(i == 0), stop=(i == 3),
                                            skip_group_check=True)
                    ins.then_inc(P5d.sem, P5d.step("O"))
                if u[1]:
                    b, n = u[1]
                    pe.wait_ge(A5b.sem, A5b.at("q_out", n))
                    pe.wait_ge(G5b.sem, G5b.at("kbd", n))
                    pe.wait_ge(V5c.sem, V5c.at("sub", n - 1))
                    for (h, m), p in zip(SPANS, (pC[:, 0, :], pC[:, 1, :], pD[:, 0, :])):
                        ins = pe.matmul(p[:, 0:m * S2], dqT, dkb[:, h:h + m, :].rearrange("p h s -> p (h s)"), start=True, stop=True)
                    ins.then_inc(P5b.sem, P5b.step("S"))
                if u[3]:
                    b, n = u[3]
                    pe.wait_ge(A5d.sem, A5d.at("oT_out", n))
                    pe.matmul(pD[:, 1, 256:384], doT, w0("wo1"), start=True, stop=True).then_inc(P5d.sem, P5d.step("y"))

            pipeline(pe, x0, 4, B, 0)
            after(pe, B - 1, V1d)
            pipeline(pe, conv, 2, NG, 0)
            after(pe, NG - 1, A2b)
            pipeline(pe, f0, 4, B, 0)
            after(pe, B - 1, V3d)
            pipeline(pe, route, 4, B, 0)
            after(pe, B - 1, V4d, G4b)
            pe.wait_ge(s_mw, 32)
            with pe.Fori(0, NG) as g:
                up(g, g, 0)
                for e in range(1, NE + 1):
                    if e < NE:
                        up(g, g, e)
                    down(g, g, e - 1)
            after(pe, NG - 1, V4e)
            pipeline(pe, x1, 5, B, 0)
            after(pe, B - 1, V5e)
            pe.wait_ge(s_clear, 3)

            def turn(p, src):
                for c in range(8):
                    ins = pe.transpose(blocks(p)[:, c, :], src(c), ident[:])
                return ins

            def scores(n, g, p):
                for c in range(2):
                    pe.matmul(p[:, c, :], identb[:], band[:].rearrange("p a b -> p (a b)"), start=True, stop=False, skip_group_check=True)
                    for j in range(2):
                        h2 = 4 * g + 2 * c + j
                        ins = pe.matmul(p[:, c, 256 * j:256 * j + 256], qT[:, h2, :],
                                        kbd[:, h2, :, :].rearrange("p a t -> p (a t)"), start=False, stop=(j == 1), skip_group_check=True)
                ins.then_inc(AP2.sem, AP2.step(f"S{g}"))

            def last(u, stage, n, lag):
                return n + lag if u[stage] else UNITS - 1

            def stack(u):
                qkv, back, up, down = (value(pe, of_unit(pe, u[k][1])[1] * W_ALL) if u[k] else None for k in (PROJ, VALUE, UP, DOWN))
                if u[VALUE]:
                    n = u[VALUE][1]
                    pe.wait_ge(AG2.sem, AG2.at("p0", n))
                    pe.wait_ge(AA1.sem, AA1.at("qT_out", last(u, SCORE, n, 1)))
                    turn(pA, lambda c: prob[:, c, :]).then_inc(AP3.sem, AP3.step("PT0"))
                    pe.wait_ge(AG2.sem, AG2.at("p1", n))
                    turn(pC, lambda c: prob[:, 8 + c, :]).then_inc(AP3.sem, AP3.step("PT1"))
                if u[SCORE]:
                    n = u[SCORE][1]
                    pe.wait_ge(AA1.sem, AA1.at("kT_out", n))
                    pe.wait_ge(AV1.sem, AV1.at("kT_out", n))
                if u[PROJ]:
                    n = u[PROJ][1]
                    pe.wait_ge(AG0.sem, AG0.at("xc", n))
                    pe.transpose(pD[:, 0, 0:T], xc[:], ident[:]).then_inc(AP1.sem, AP1.step("xT"))
                if u[UP]:
                    n = u[UP][1]
                    pe.wait_ge(FG1.sem, FG1.at("b", n))
                    pe.wait_ge(FA2.sem, FA2.at("xT_out", n - 1))
                    pe.transpose(pD[:, 1, 3 * T:4 * T], xb[:], ident[:]).then_inc(FP2.sem, FP2.step("xT"))
                if u[DOWN]:
                    n = u[DOWN][1]
                    pe.wait_ge(FV3.sem, FV3.at("gated", n))
                    pe.wait_ge(FA4.sem, FA4.at("mT_out", n - 1))
                    for c in range(FC):
                        ins = pe.transpose(pD[:, 1, 128 * c:128 * c + 128], mg[:, 128 * c:128 * c + 128], ident[:])
                    ins.then_inc(FP4.sem, FP4.step("mT"))
                if u[PROJ]:
                    n = u[PROJ][1]
                    pe.wait_ge(s_layer, (n >> LAYER_BITS) + 1)
                    pe.wait_ge(AA1.sem, AA1.at("xsT", n))
                    pe.wait_ge(FV2.sem, FV2.at("bias", n - 5))
                    pe.wait_ge(FV4.sem, FV4.at("yb", n - 7))
                    pe.wait_ge(AV3.sem, AV3.at("x_out", n - 3))
                    for name, p, which in (("q", pB, 0), ("k", pD, 1)):
                        if name == "k":
                            pe.wait_ge(FA2.sem, FA2.at("xT_out", n - 4))
                            pe.wait_ge(FA4.sem, FA4.at("mT_out", n - 6))
                        for c in range(2):
                            ins = pe.matmul(p[:, c, :], xsT[:], WLf[:, bass.ds(qkv + (W_QKV + which * INNER + 512 * c), 512)], start=True, stop=True)
                        ins.then_inc(AP1.sem, AP1.step(name))
                if u[SCORE]:
                    n = u[SCORE][1]
                    pe.wait_ge(AA3.sem, AA3.at("pT0", n - 1))
                    scores(n, 0, pA)
                if u[VALUE]:
                    n = u[VALUE][1]
                    pe.wait_ge(AA3.sem, AA3.at("pT0", n))
                    pe.wait_ge(AV3.sem, AV3.at("pT1", n))
                    pe.wait_ge(AG2.sem, AG2.at("v", n))
                    pe.wait_ge(AA1.sem, AA1.at("q_out", last(u, PROJ, n, 2)))
                    pe.wait_ge(FV2.sem, FV2.at("bias", n - 3))
                    pe.wait_ge(FV4.sem, FV4.at("yb", n - 5))
                    pe.wait_ge(AV3.sem, AV3.at("x_out", n - 1))
                    for h in range(NH):
                        o = E * (h % 2)
                        ins = pe.matmul(blocks(pB)[o:o + E, h // 2, :], v[:, h * E:(h + 1) * E], probT[:, h, :], start=True, stop=True)
                    ins.then_inc(AP3.sem, AP3.step("O"))
                if u[SCORE]:
                    n = u[SCORE][1]
                    pe.wait_ge(AV3.sem, AV3.at("pT1", n - 1))
                    scores(n, 1, pC)
                if u[PROJ]:
                    n = u[PROJ][1]
                    pe.wait_ge(AA1.sem, AA1.at("k_out", n))
                    for c in range(2):
                        ins = pe.matmul(pD[:, c, :], xsT[:], WLf[:, bass.ds(qkv + (W_QKV + 2 * INNER + 512 * c), 512)], start=True, stop=True)
                    ins.then_inc(AP1.sem, AP1.step("v"))
                    pe.wait_ge(AG1.sem, AG1.at("q_r", n))
                    pe.wait_ge(AA2.sem, AA2.at("exp0", n - 1))
                    turn(pA, lambda c: rc[:, 0, 128 * c:128 * c + 128]).then_inc(AP1.sem, AP1.step("qT"))
                if u[VALUE]:
                    n = u[VALUE][1]
                    pe.wait_ge(AA3.sem, AA3.at("oT_out", n))
                    pe.wait_ge(AA1.sem, AA1.at("q_out", last(u, PROJ, n, 2)))
                    for c in range(8):
                        ins = pe.matmul(pB[:, 1, FF:FF + D], oT[:, c, :], WLf[:, bass.ds(back + (W_O + D * c), D)], start=(c == 0), stop=(c == 7))
                    ins.then_inc(AP3.sem, AP3.step("y"))
                if u[DOWN]:
                    n = u[DOWN][1]
                    pe.wait_ge(FA4.sem, FA4.at("mT_out", n))
                    pe.wait_ge(AA3.sem, AA3.at("oT_out", last(u, VALUE, n, 4)))
                    pe.wait_ge(FV4.sem, FV4.at("yb", n - 1))
                    pe.wait_ge(FV2.sem, FV2.at("bias", last(u, GATE, n, 1)))
                    for c in range(FC):
                        ins = pe.matmul(pB[:, 0, FF:FF + D], mT[:, c, :], WLf[:, bass.ds(down + (W_2 + D * c), D)], start=(c == 0), stop=(c == FC - 1))
                    ins.then_inc(FP4.sem, FP4.step("y"))
                if u[UP]:
                    n = u[UP][1]
                    pe.wait_ge(FA2.sem, FA2.at("xT_out", n))
                    pe.wait_ge(FV2.sem, FV2.at("bias", n - 1))
                    pe.wait_ge(AA1.sem, AA1.at("q_out", last(u, PROJ, n, 4)))
                    pe.wait_ge(AA3.sem, AA3.at("oT_out", last(u, VALUE, n, 2)))
                    for c in range(2):
                        ins = pe.matmul(pB[:, c, 0:FF], xnT[:], WLf[:, bass.ds(up + (W_1 + FF * c), FF)], start=True, stop=True)
                    ins.then_inc(FP2.sem, FP2.step("h"))
                if u[PROJ]:
                    n = u[PROJ][1]
                    pe.wait_ge(AV1.sem, AV1.at("k_n", n))
                    pe.wait_ge(AA1.sem, AA1.at("v_out", n))
                    turn(pD, lambda c: rc[:, 1, 128 * c:128 * c + 128]).then_inc(AP1.sem, AP1.step("kT"))

            pipeline(pe, stack, STAGES, UNITS, 0)

        @block.scalar
        def _(act):
            def stack(u):
                def head_exp(n, g, p):
                    act.wait_ge(AV2.sem, AV2.at(f"neg{g}", n))
                    act.wait_ge(AP3.sem, AP3.at(f"PT{g}", n - 1))
                    act.wait_ge(AV2.sem, AV2.at(f"rsum{g}", n - 1))
                    for c in range(8):
                        h = 8 * g + c
                        ins = act.activation(prob[:, h, :], blocks(p)[:, c, :], ACT.Exp, bias=nm[:, h:h + 1], scale=sc[:, h:h + 1],
                                             accum_out=psums[:, h:h + 1])
                    ins.then_inc(AA2.sem, AA2.step(f"exp{g}"))

                def table_of(n, name, f, i):
                    act.wait_ge(AW.sem, AW.at(name, n - 1))
                    act.activation(warm[:, i:i + 1], zeros[:, 0:1], f).then_inc(AW.sem, AW.step(name))

                if u[PROJ]:
                    n = u[PROJ][1]
                    act.wait_ge(AP1.sem, AP1.at("xT", n))
                    act.wait_ge(AP1.sem, AP1.at("v", n - 1))
                    act.copy(xsT[:], pD[:, 0, 0:T]).then_inc(AA1.sem, AA1.step("xsT"))
                if u[UP]:
                    n = u[UP][1]
                    act.wait_ge(FP2.sem, FP2.at("xT", n))
                    act.wait_ge(FP2.sem, FP2.at("h", n - 1))
                    act.wait_ge(FP4.sem, FP4.at("mT", n - 2))
                    act.copy(xnT[:], pD[:, 1, 3 * T:4 * T]).then_inc(FA2.sem, FA2.step("xT_out"))
                if u[DOWN]:
                    n = u[DOWN][1]
                    act.wait_ge(FP4.sem, FP4.at("mT", n))
                    act.wait_ge(FP4.sem, FP4.at("y", n - 1))
                    act.copy(mT[:].rearrange("p a b -> p (a b)"), pD[:, 1, 0:FC * 128]).then_inc(FA4.sem, FA4.step("mT_out"))
                if u[VALUE]:
                    n = u[VALUE][1]
                    act.wait_ge(AP3.sem, AP3.at("PT0", n))
                    act.wait_ge(AP3.sem, AP3.at("O", n - 1))
                    act.copy(probT[:, 0:8, :], blocks(pA)).then_inc(AA3.sem, AA3.step("pT0"))
                if u[GATE]:
                    n = u[GATE][1]
                    act.wait_ge(FV2.sem, FV2.at("bias", n))
                    act.wait_ge(FV3.sem, FV3.at("gated", n - 1))
                    act.activation(gg[:], hb[:, 1, :], ACT.Gelu).then_inc(FA3.sem, FA3.step("gelu"))
                if u[PROJ]:
                    n = u[PROJ][1]
                    for j, (name, p) in enumerate((("q", pB), ("k", pD))):
                        act.wait_ge(AP1.sem, AP1.at(name, n))
                        if j == 0:
                            act.wait_ge(AV1.sem, AV1.at("k_s", n - 1))
                            act.wait_ge(AG1.sem, AG1.at("k_c", n - 1))
                        act.copy(qn[:, j, :], flat(p)).then_inc(AA1.sem, AA1.step(f"{name}_out"))
                    table_of(n, "exp", ACT.Exp, 0)
                    act.wait_ge(AA1.sem, AA1.at("k_out", n))
                    act.wait_ge(AV1.sem, AV1.at("q_ss", n - 1))
                    for j, name in ((1, "k_sq"), (0, "q_sq")):
                        act.activation(sq[:, j, :], qn[:, j, :], ACT.Square).then_inc(AA1.sem, AA1.step(name))
                if u[SCORE]:
                    head_exp(u[SCORE][1], 0, pA)
                if u[VALUE]:
                    n = u[VALUE][1]
                    act.wait_ge(AP3.sem, AP3.at("O", n))
                    act.wait_ge(AP3.sem, AP3.at("y", n - 1))
                    act.copy(oT[:], blocks(pB)).then_inc(AA3.sem, AA3.step("oT_out"))
                if u[SCORE]:
                    head_exp(u[SCORE][1], 1, pC)
                if u[PROJ]:
                    n = u[PROJ][1]
                    act.wait_ge(AP1.sem, AP1.at("v", n))
                    act.wait_ge(AG2.sem, AG2.at("v", n - 1))
                    act.copy(vn[:], flat(pD)).then_inc(AA1.sem, AA1.step("v_out"))
                    act.wait_ge(AP1.sem, AP1.at("qT", n))
                    act.copy(qT[:], blocks(pA)).then_inc(AA1.sem, AA1.step("qT_out"))
                    act.wait_ge(AP1.sem, AP1.at("kT", n))
                    act.copy(kbd[0:E, :, 0, :], blocks(pD)[0:E]).then_inc(AA1.sem, AA1.step("kT_out"))
                    table_of(n, "gelu", ACT.Gelu, 1)

            act.wait_ge(s_zero, 4)
            act.wait_ge(s_zero, 4)
            act.wait_ge(ldc, 16 * N_CONST)
            act.activation(dt, r0("log_dt"), ACT.Exp).then_inc(SA.sem, SA.step("dt"))
            act.activation(tg[:], r0("gates"), ACT.Tanh).then_inc(SA.sem, SA.step("gates"))
            act.wait_ge(SV.sem, SV.at("cos_frac", 0))
            act.activation(cos, cos, ACT.Sin, scale=TURN).then_inc(SA.sem, SA.step("cos"))
            act.wait_ge(SV.sem, SV.at("sin_frac", 0))
            act.activation(sin, sin, ACT.Sin, scale=TURN).then_inc(SA.sem, SA.step("sin"))
            act.wait_ge(SV.sem, SV.at("dta_re", 0))
            act.activation(mag, dta_re, ACT.Exp).then_inc(SA.sem, SA.step("mag"))
            act.wait_ge(SV.sem, SV.at("cos_i_frac", 0))
            act.activation(sQ2, sQ2, ACT.Sin, scale=TURN).then_inc(SA.sem, SA.step("cos_i"))
            act.wait_ge(SV.sem, SV.at("sin_i_frac", 0))
            act.activation(sQ, sQ, ACT.Sin, scale=TURN).then_inc(SA.sem, SA.step("sin_i"))
            act.wait_ge(SV.sem, SV.at("wave_j_frac", 0))
            act.activation(sT1, sT1, ACT.Sin, scale=TURN).then_inc(SA.sem, SA.step("wave_j"))
            act.wait_ge(SV.sem, SV.at("arg_i", 0))
            act.activation(sQ3, sQ3, ACT.Exp).then_inc(SA.sem, SA.step("mag_i"))
            act.wait_ge(SV.sem, SV.at("arg_j", 0))
            act.activation(sP, sP, ACT.Exp).then_inc(SA.sem, SA.step("mag_j"))
            act.wait_ge(s_set, 1)

            def x0(u):
                if u[2]:
                    b, n = u[2]
                    act.wait_ge(P1b.sem, P1b.at("S", n))
                    act.wait_ge(V1c.sem, V1c.at("sel", n - 1))
                    act.copy(work.rearrange("p h s -> p (h s)"), pB[:, 1, 0:H0 * S2]).then_inc(A1c.sem, A1c.step("work"))
                if u[3]:
                    b, n = u[3]
                    act.wait_ge(P1d.sem, P1d.at("vT", n))
                    act.wait_ge(P1d.sem, P1d.at("vf", n - 1))
                    act.copy(avT, pC[:, 0, 0:S2]).then_inc(A1d.sem, A1d.step("vT_out"))
                    act.wait_ge(P1d.sem, P1d.at("aT", n))
                    act.wait_ge(P1d.sem, P1d.at("film", n - 1))
                    act.copy(aT[0:S2, :], pC[0:S2, 0, 128:256]).then_inc(A1d.sem, A1d.step("aT_out"))
                    act.wait_ge(P1d.sem, P1d.at("vf", n))
                    act.copy(avf[0:S2, :], pC[0:S2, 1, :]).then_inc(A1d.sem, A1d.step("vf_out"))
                if u[2]:
                    b, n = u[2]
                    act.wait_ge(V1c.sem, V1c.at("sub", n))
                    act.activation(eexp, esub, ACT.Exp).then_inc(A1c.sem, A1c.step("exp"))
                if u[1]:
                    b, n = u[1]
                    act.wait_ge(P1b.sem, P1b.at("xT", n))
                    act.wait_ge(P1b.sem, P1b.at("Q", n - 1))
                    act.copy(axT, pA[:, 0, 0:T]).then_inc(A1b.sem, A1b.step("xT_out"))
                    act.wait_ge(P1b.sem, P1b.at("Q", n))
                    act.wait_ge(P1b.sem, P1b.at("S", n - 1))
                    act.mul(aqT, pA[:, 1, 0:T], float(1.0 / np.sqrt(DH0))).then_inc(A1b.sem, A1b.step("Q_out"))

            def conv(u):
                if u[1]:
                    c, n = u[1]
                    act.wait_ge(P2b.sem, P2b.at("G", n))
                    act.copy(U[:, bass.ts(c, GB), :].rearrange("p b d -> p (b d)"), pB[:, 0, :]).then_inc(A2b.sem, A2b.step("cv"))

            def f0(u):
                if u[1]:
                    b, n = u[1]
                    act.wait_ge(P3b.sem, P3b.at("hT", n))
                    act.wait_ge(P3b.sem, P3b.at("h", n - 1))
                    act.copy(chT, pA[:, 0, 0:T]).then_inc(A3b.sem, A3b.step("hT_out"))
                    act.wait_ge(P3b.sem, P3b.at("h", n))
                    act.wait_ge(P3c.sem, P3c.at("y", n - 1))
                    for c in range(4):
                        ins = act.activation(cgT[:, c, :], pB[:, 0, 128 * c:128 * c + 128], ACT.Gelu, bias=co("b1", c))
                    ins.then_inc(A3b.sem, A3b.step("gelu"))

            def route(u):
                if u[3]:
                    b, n = u[3]
                    act.wait_ge(P4d.sem, P4d.at("cT", n))
                    act.wait_ge(P4d.sem, P4d.at("bb", n - 1))
                    act.copy(cT[0:NE, :], pC[0:NE, 0, 0:128]).then_inc(A4d.sem, A4d.step("cT_out"))
                if u[2]:
                    b, n = u[2]
                    act.wait_ge(V4c.sem, V4c.at("gap", n))
                    act.activation(ed[:, 1:2], ed[:, 0:1], ACT.Exp).then_inc(A4c.sem, A4c.step("exp"))
                if u[1]:
                    b, n = u[1]
                    act.wait_ge(P4b.sem, P4b.at("xT", n))
                    act.wait_ge(P4b.sem, P4b.at("lg", n - 1))
                    act.wait_ge(G4b.sem, G4b.at("keep", n - 1))
                    act.copy(mxT, pA[:, 0, 0:T]).then_inc(A4b.sem, A4b.step("xT_out"))

            def experts(g, n):
                for e in range(NE):
                    for c in range(4):
                        act.wait_ge(P4e.sem, P4e.at(f"h{e}{c}", n))
                        if c == 0:
                            act.wait_ge(P4e.sem, P4e.at(f"y{(e - 2) % NE}", n - (e < 2)))
                        act.activation(gT[e % 2][:, c, :], (pA, pB)[c // 2][:, c % 2, :], ACT.Gelu, bias=co("mb1", 4 * e + c)).then_inc(A4e.sem, A4e.step(f"g{e}{c}"))

            def x1(u):
                if u[3]:
                    b, n = u[3]
                    act.wait_ge(P5d.sem, P5d.at("v", n))
                    act.wait_ge(G5d.sem, G5d.at("vm", n - 1))
                    act.copy(dv[0:S2, :], pD[0:S2, 1, 0:128]).then_inc(A5d.sem, A5d.step("v_out"))
                    act.wait_ge(P5d.sem, P5d.at("PT0", n))
                    act.copy(dpT[0:S2, 0:8, :], blocks(pB)[0:S2]).then_inc(A5d.sem, A5d.step("pT0"))
                if u[1]:
                    b, n = u[1]
                    act.wait_ge(P5b.sem, P5b.at("xT", n))
                    act.wait_ge(P5b.sem, P5b.at("q", n - 1))
                    act.copy(dxT, pA[:, 0, 0:T]).then_inc(A5b.sem, A5b.step("xT_out"))
                    act.wait_ge(P5b.sem, P5b.at("k", n))
                    act.wait_ge(G5b.sem, G5b.at("kbd", n - 1))
                    act.copy(dk, pA[:, 1, 128:128 + S2]).then_inc(A5b.sem, A5b.step("k_out"))
                    act.wait_ge(P5b.sem, P5b.at("q", n))
                    act.wait_ge(P5b.sem, P5b.at("S", n - 1))
                    act.add(dqT, pA[:, 1, 0:128], co("bq")).then_inc(A5b.sem, A5b.step("q_out"))
                if u[2]:
                    b, n = u[2]
                    act.wait_ge(V5c.sem, V5c.at("sub", n))
                    act.wait_ge(P5d.sem, P5d.at("PT1", n - 1))
                    act.activation(dpr, dsub, ACT.Exp, scale=SCALE1).then_inc(A5c.sem, A5c.step("exp"))
                if u[3]:
                    b, n = u[3]
                    act.wait_ge(P5d.sem, P5d.at("O", n))
                    act.wait_ge(P5d.sem, P5d.at("y", n - 1))
                    act.copy(doT, pD[:, 1, 0:128]).then_inc(A5d.sem, A5d.step("oT_out"))

            pipeline(act, x0, 4, B, 0)
            after(act, B - 1, V1d)
            pipeline(act, conv, 2, NG, 0)
            pipeline(act, f0, 4, B, 0)
            after(act, B - 1, V3d)
            pipeline(act, route, 4, B, 0)
            after(act, B - 1, V4d, G4b)
            with act.Fori(0, NG) as g:
                experts(g, g)
            after(act, NG - 1, V4e)
            pipeline(act, x1, 5, B, 0)
            after(act, B - 1, V5e)
            act.wait_ge(s_clear, 3)
            pipeline(act, stack, STAGES, UNITS, 0)

        @block.vector
        def _(dve):
            def stack(u):
                def head_max(n, g, p):
                    at = slice(8 * g, 8 * g + 8)
                    dve.wait_ge(AP2.sem, AP2.at(f"S{g}", n))
                    dve.tensor_reduce(mx[:, at], blocks(p), AX.X, ALU.max).then_inc(AV2.sem, AV2.step(f"max{g}"))
                    if g == 0:
                        dve.wait_ge(AA2.sem, AA2.at("exp1", n - 1))
                        dve.tensor_scalar(sc[:], rn[:, 0, :], QK_SCALE, None, ALU.mult).then_inc(AV2.sem, AV2.step("scale"))
                    dve.wait_ge(AV2.sem, AV2.at("scale" if g == 0 else "max1", n))
                    dve.scalar_tensor_tensor(nm[:, at], mx[:, at], -1.0, sc[:, at], ALU.mult, ALU.mult).then_inc(AV2.sem, AV2.step(f"neg{g}"))

                def swapped(n, j, name):
                    q4 = qn[:, j, :].rearrange("p (h two e) -> p h two e", two=2, e=E // 2)
                    s4 = rs[:, j, :].rearrange("p (h two e) -> p h two e", two=2, e=E // 2)
                    dve.wait_ge(AA1.sem, AA1.at(f"{name}_out", n))
                    dve.wait_ge(AG1.sem, AG1.at(f"{name}_r", n - 1))
                    for c in range(2):
                        tab = RTf[:, bass.ds(table + ((2 * j + 1) * E + c * (E // 2)), E // 2)].unsqueeze(1).to_broadcast([T, NH, E // 2])
                        ins = dve.tensor_tensor(s4[:, :, c, :], q4[:, :, 1 - c, :], tab, ALU.mult)
                    ins.then_inc(AV1.sem, AV1.step(f"{name}_s"))

                def sums(n, g):
                    dve.wait_ge(AA2.sem, AA2.at(f"exp{g}", n))
                    dve.wait_ge(AG2.sem, AG2.at(f"p{g}", n - 1))
                    dve.reciprocal(rsum[:, 8 * g:8 * g + 8], psums[:, 8 * g:8 * g + 8]).then_inc(AV2.sem, AV2.step(f"rsum{g}"))

                def squares(n, j, name):
                    dve.wait_ge(AA1.sem, AA1.at(f"{name}_sq", n))
                    dve.tensor_reduce(ss[:, j, :], sq[:, j, :].rearrange("p (h e) -> p h e", e=E), AX.X, ALU.add).then_inc(AV1.sem, AV1.step(f"{name}_ss"))

                b3, b4, b7 = (value(dve, u[k][1] & (B - 1)) if u[k] else None for k in (VALUE, CENTRE, DOWN))
                bias5, bias7 = (value(dve, of_unit(dve, u[k][1])[1] * R_ALL) if u[k] else None for k in (UP, DOWN))
                table = value(dve, (u[PROJ][1] >> LAYER_BITS) * (4 * E)) if u[PROJ] else None
                if u[VALUE]:
                    n = u[VALUE][1]
                    dve.wait_ge(AP3.sem, AP3.at("PT1", n))
                    dve.wait_ge(AP3.sem, AP3.at("O", n - 1))
                    dve.tensor_copy(probT[:, 8:16, :], blocks(pC)).then_inc(AV3.sem, AV3.step("pT1"))
                if u[CENTRE]:
                    n = u[CENTRE][1]
                    dve.wait_ge(s_sh, (n + 2) * 16)
                    dve.wait_ge(AG3.sem, AG3.at("xs", n))
                    moments(dve, FV1, FG0, n, XS[:, b4, :], NF, s_pass)
                if u[GATE]:
                    n = u[GATE][1]
                    dve.wait_ge(FA3.sem, FA3.at("gelu", n))
                    dve.wait_ge(FP4.sem, FP4.at("mT", n - 1))
                    dve.tensor_tensor(mg[:, 0:FF], hb[:, 0, :], gg[:], ALU.mult).then_inc(FV3.sem, FV3.step("gated"))
                if u[CENTRE]:
                    n = u[CENTRE][1]
                    dve.wait_ge(FG1.sem, FG1.at("g", n - 1))
                    centre(dve, FV1, FG0, n, xn[:], XS[:, b4, :], NF)
                if u[PROJ]:
                    n = u[PROJ][1]
                    swapped(n, 0, "q")
                    swapped(n, 1, "k")
                if u[SCORE]:
                    head_max(u[SCORE][1], 0, pA)
                if u[PROJ]:
                    n = u[PROJ][1]
                    squares(n, 1, "k")
                    squares(n, 0, "q")
                if u[SCORE]:
                    head_max(u[SCORE][1], 1, pC)
                if u[PROJ]:
                    n = u[PROJ][1]
                    dve.wait_ge(AV1.sem, AV1.at("q_ss", n))
                    dve.tensor_scalar(ss[:], ss[:], 1e-24, None, ALU.max).then_inc(AV1.sem, AV1.step("floor"))
                    dve.wait_ge(AV1.sem, AV1.at("floor", n))
                    rsqrt(dve, AV1, n, "", rn[:], rh[:], ss[:])
                if u[SCORE]:
                    sums(u[SCORE][1], 0)
                if u[PROJ]:
                    n = u[PROJ][1]
                    dve.wait_ge(AV1.sem, AV1.at(f"newton{RSQRT_STEPS - 1}", n))
                    dve.wait_ge(AG1.sem, AG1.at("k_r", n))
                    k3 = rc[:, 1, :].rearrange("p (h e) -> p h e", e=E)
                    dve.tensor_tensor(k3, k3, rn[:, 1, :].unsqueeze(2).to_broadcast([T, NH, E]), ALU.mult).then_inc(AV1.sem, AV1.step("k_n"))
                if u[SCORE]:
                    sums(u[SCORE][1], 1)
                if u[VALUE]:
                    n = u[VALUE][1]
                    dve.wait_ge(AP3.sem, AP3.at("y", n))
                    if u[UP]:
                        dve.wait_ge(FP2.sem, FP2.at("h", n - 2))
                    dve.tensor_tensor(XD[:, b3, :], pB[:, 1, FF:FF + D], XD[:, b3, :], ALU.add).then_inc(AV3.sem, AV3.step("x_out"))
                if u[DOWN]:
                    n = u[DOWN][1]
                    dve.wait_ge(FV4.sem, FV4.at("x_out", n - 1))
                    dve.wait_ge(FP4.sem, FP4.at("y", n))
                    if u[UP]:
                        dve.wait_ge(FP2.sem, FP2.at("h", n + 2))
                    dve.tensor_tensor(yb[:], pB[:, 0, FF:FF + D], RLf[:, bass.ds(bias7 + R_B2, D)], ALU.add).then_inc(FV4.sem, FV4.step("yb"))
                if u[UP]:
                    n = u[UP][1]
                    dve.wait_ge(FP2.sem, FP2.at("h", n))
                    dve.wait_ge(FV3.sem, FV3.at("gated", n - 1))
                    dve.tensor_tensor(hb[:], pB[:, :, 0:FF], RLf[:, bass.ds(bias5 + R_B1, 2 * FF)].rearrange("p (a f) -> p a f", a=2), ALU.add).then_inc(FV2.sem, FV2.step("bias"))
                if u[DOWN]:
                    n = u[DOWN][1]
                    dve.wait_ge(FV4.sem, FV4.at("yb", n))
                    dve.tensor_tensor(XD[:, b7, :], yb[:], XD[:, b7, :], ALU.add).then_inc(FV4.sem, FV4.step("x_out"))
                if u[PROJ]:
                    n = u[PROJ][1]
                    dve.wait_ge(AP1.sem, AP1.at("kT", n))
                    dve.tensor_copy(kbd[E:2 * E, :, 1, :], blocks(pD)[E:2 * E]).then_inc(AV1.sem, AV1.step("kT_out"))

            dve.wait_ge(s_zero, 4)
            def done(name, ins):
                ins.then_inc(SV.sem, SV.step(name))
                dve.wait_ge(SV.sem, SV.at(name, 0))

            def tt(name, out_, x, y, o):
                done(name, dve.tensor_tensor(out_, x, y, o))

            def ts(name, out_, x, s1, s2, o1, o2=None):
                done(name, dve.tensor_scalar(out_, x, s1, s2, o1, o2) if o2 else dve.tensor_scalar(out_, x, s1, s2, o1))

            def over(x, m):
                return x.unsqueeze(2).to_broadcast([128, 128, m])

            def along(x, m):
                return x.unsqueeze(1).to_broadcast([128, 128, m])

            def whole_turns_off(name, x, k):
                ts(name + "_whole", k, x, ROUND, -ROUND, ALU.add, ALU.add)
                tt(name + "_frac", x, x, k, ALU.subtract)

            dve.wait_ge(ldc, 16 * N_CONST)
            done("identb", dve.tensor_copy(identb[:], ident[:]))
            done("band", dve.tensor_copy(band[:], xg[:].unsqueeze(1).to_broadcast([128, 4, 128])))
            dve.wait_ge(SA.sem, SA.at("dt", 0))
            tt("dta_re", dta_re, dt, are, ALU.mult)
            tt("dta_im", dta_im, dt, aim, ALU.mult)
            ts("turns", turns, dta_im, float(1 / (2 * np.pi)), None, ALU.mult)
            ts("cos_turns", cos, turns, 0.25, None, ALU.add)
            whole_turns_off("cos", cos, spare)
            ts("sin_turns", sin, turns, 0.0, None, ALU.add)
            whole_turns_off("sin", sin, spare)
            dve.wait_ge(SA.sem, SA.at("mag", 0))
            tt("e_re", e_re, cos, mag, ALU.mult)
            tt("e_im", e_im, sin, mag, ALU.mult)
            ts("e_re_less_1", e_re, e_re, -1.0, None, ALU.add)
            tt("c_e_rr", num_re, cre, e_re, ALU.mult)
            tt("c_e_ii", spare, cim, e_im, ALU.mult)
            tt("num_re", num_re, num_re, spare, ALU.subtract)
            tt("c_e_ri", num_im, cre, e_im, ALU.mult)
            tt("c_e_ir", spare, cim, e_re, ALU.mult)
            tt("num_im", num_im, num_im, spare, ALU.add)
            tt("a_rr", scale, are, are, ALU.mult)
            tt("a_ii", spare, aim, aim, ALU.mult)
            tt("a_abs2", spare, scale, spare, ALU.add)
            done("a_inv", dve.reciprocal(scale, spare))
            ts("scale", scale, scale, 2.0, None, ALU.mult)
            tt("n_a_rr", dc_re, num_re, are, ALU.mult)
            tt("n_a_ii", spare, num_im, aim, ALU.mult)
            tt("dc_re_num", dc_re, dc_re, spare, ALU.add)
            tt("dc_re", dc_re, dc_re, scale, ALU.mult)
            tt("n_a_ir", dc_im, num_im, are, ALU.mult)
            tt("n_a_ri", spare, num_re, aim, ALU.mult)
            tt("dc_im_num", dc_im, dc_im, spare, ALU.subtract)
            tt("dc_im", dc_im, dc_im, scale, ALU.mult)
            ts("row_cos_0", spare, dc_re, co("m0"), None, ALU.mult)
            done("row_cos", dve.scalar_tensor_tensor(num_re, dc_im, co("-m1"), spare, ALU.mult, ALU.add))
            ts("row_sin_0", spare, dc_im, co("-m0"), None, ALU.mult)
            done("row_sin", dve.scalar_tensor_tensor(num_im, dc_re, co("-m1"), spare, ALU.mult, ALU.add))
            tt("sin_i_turns", sQ, over(turns, NI), along(w0("i"), NI), ALU.mult)
            ts("cos_i_turns", sQ2, sQ, 0.25, None, ALU.add)
            whole_turns_off("cos_i", sQ2, sQ3)
            whole_turns_off("sin_i", sQ, sQ3)
            tt("wave_j_turns", sP, over(turns, NJ), along(w0("j"), NJ), ALU.mult)
            ts("wave_j_off", sT1, sP, co("off"), None, ALU.add)
            whole_turns_off("wave_j", sT1, sT2)
            tt("arg_i", sQ3, over(dta_re, NI), along(w0("i"), NI), ALU.mult)
            tt("arg_j", sP, over(dta_re, NJ), along(w0("j"), NJ), ALU.mult)
            dve.wait_ge(SA.sem, SA.at("mag_i", 0))
            tt("cos_i_mag", sQ2, sQ2, sQ3, ALU.mult)
            tt("sin_i_mag", sQ, sQ, sQ3, ALU.mult)
            tt("row_i_cos", sQc, sQ2, over(num_re, NI), ALU.mult)
            tt("row_i_sin", sQ3, sQ, over(num_im, NI), ALU.mult)
            tt("row_i", sQc, sQc, sQ3, ALU.add)
            dve.wait_ge(SA.sem, SA.at("mag_j", 0))
            tt("power_j", sP, sP, sT1, ALU.mult)
            dve.wait_ge(s_sp, 1)
            done("rows", dve.tensor_copy(KS[0:NJ].rearrange("j i d -> j d i"), pA[0:NJ].rearrange("p b (d i) -> p (b d) i", i=NI)))
            dve.tensor_tensor(KS[0:1, 0, :], KS[0:1, 0, :], r0("dskip")[0:1], ALU.add).then_inc(s_ks, 1)
            dve.wait_ge(s_sp, 2)
            done("f_cos", dve.tensor_copy(KF[:, 0, :], pB[:, 0, 0:128]))
            ts("f_sin", KF[:, 1, :], pB[:, 0, 128:256], co("nz"), None, ALU.mult)
            ts("f_half", KF[:, 2, :], pB[:, 0, 128:256], co("z"), None, ALU.mult)
            done("f_flip", dve.scalar_tensor_tensor(KF[:, 2, :], KF[:, 0, :], co("nz"), KF[:, 2, :], ALU.mult, ALU.add))
            ts("text_mask", tm[:], tm8[:], 1.0 / H0, None, ALU.mult)
            ts("context_mask", vm[:].rearrange("p b s -> p (b s)"), vm8[:], -1.0, BIG, ALU.add, ALU.mult)
            dve.sem_inc(s_set, 1)
            dve.wait_ge(s_x, 16)

            def x0(u):
                if u[3]:
                    b, n = u[3]
                    dve.wait_ge(G1d.sem, G1d.at("g", n - 1))
                    normalise(dve, V1d, N1d, n, a2[:], XD[:, b, :], N2, s_pass)
                if u[2]:
                    b, n = u[2]
                    dve.wait_ge(A1c.sem, A1c.at("work", n))
                    dve.sem_inc(s_pass, 1)
                    for r in range(TOPK // 8):
                        for h in range(H0):
                            ins = dve.max(m8r[:, r % 2, h, :] if r else m8[:, h, :], work[:, h, :])
                        ins.then_inc(V1c.sem, V1c.step(f"max{r}"))
                        dve.wait_ge(V1c.sem, V1c.at(f"max{r}", n))
                        dve.sem_inc(s_pass, 1)
                        for h in range(H0):
                            ins = dve.match_replace(work[:, h, :], m8r[:, r % 2, h, :] if r else m8[:, h, :], work[:, h, :], GONE)
                        ins.then_inc(V1c.sem, V1c.step(f"rep{r}"))
                        dve.wait_ge(V1c.sem, V1c.at(f"rep{r}", n))
                        dve.sem_inc(s_pass, 1)
                if u[3]:
                    b, n = u[3]
                    dve.wait_ge(P1d.sem, P1d.at("film", n))
                    dve.wait_ge(G1d.sem, G1d.at("fo", n - 1))
                    dve.tensor_tensor(fb, pD[:, 0, :], r0("film"), ALU.add).then_inc(V1d.sem, V1d.step("fb"))
                if u[2]:
                    b, n = u[2]
                    dve.wait_ge(A1c.sem, A1c.at("exp", n - 1))
                    dve.tensor_tensor(esub, pB[:, 1, 0:H0 * S2].rearrange("p (h s) -> p h s", h=H0), m8[:, :, 0:1].to_broadcast([T, H0, S2]),
                                      ALU.subtract).then_inc(V1c.sem, V1c.step("sub"))
                if u[3]:
                    b, n = u[3]
                    dve.wait_ge(G1d.sem, G1d.at("fm", n))
                    dve.scalar_tensor_tensor(u1[:], fm[:, 0:D], 1.0, ay[:], ALU.add, ALU.mult).then_inc(V1d.sem, V1d.step("u1"))
                    dve.wait_ge(V1d.sem, V1d.at("u1", n))
                    dve.tensor_tensor(U[:, b, :], u1[:], fm[:, D:2 * D], ALU.add).then_inc(V1d.sem, V1d.step("u"))
                if u[2]:
                    b, n = u[2]
                    dve.wait_ge(A1c.sem, A1c.at("exp", n))
                    dve.scalar_tensor_tensor(esel, work, GONE / 2, eexp, ALU.is_le, ALU.mult).then_inc(V1c.sem, V1c.step("sel"))
                    dve.wait_ge(V1c.sem, V1c.at("sel", n))
                    dve.tensor_reduce(es, esel, AX.X, ALU.add).then_inc(V1c.sem, V1c.step("sum"))
                    dve.wait_ge(V1c.sem, V1c.at("sum", n))
                    dve.reciprocal(ew, es).then_inc(V1c.sem, V1c.step("inv"))
                    dve.wait_ge(V1c.sem, V1c.at("inv", n))
                    dve.tensor_tensor(ew, ew, tm[:, bass.ds(b, 1)].to_broadcast([T, H0]), ALU.mult).then_inc(V1c.sem, V1c.step("tm"))
                    dve.wait_ge(V1c.sem, V1c.at("tm", n))
                    dve.tensor_tensor(esel, esel, ew.unsqueeze(2).to_broadcast([T, H0, S2]), ALU.mult).then_inc(V1c.sem, V1c.step("wt"))
                    dve.wait_ge(V1c.sem, V1c.at("wt", n))
                    dve.wait_ge(P1d.sem, P1d.at("aT", n - 1))
                    dve.tensor_reduce(at_, esel.rearrange("p h s -> p s h"), AX.X, ALU.add).then_inc(V1c.sem, V1c.step("mean"))
                if u[1]:
                    b, n = u[1]
                    dve.wait_ge(P1b.sem, P1b.at("k", n))
                    dve.wait_ge(P1b.sem, P1b.at("S", n - 1))
                    dve.tensor_tensor(akb, pB[:, 0, 0:S2].unsqueeze(1).to_broadcast([128, H0, S2]), w0("hm0").unsqueeze(2).to_broadcast([128, H0, S2]),
                                      ALU.mult).then_inc(V1b.sem, V1b.step("kbd"))
                if u[0]:
                    b, n = u[0]
                    dve.wait_ge(P1b.sem, P1b.at("xT", n - 1))
                    normalise(dve, V1a, N1a, n, ax, X[:, b, :], N1, s_pass)
                    dve.wait_ge(V1a.sem, V1a.at("xn", n))
                    dve.tensor_copy(XD[:, b, :], ax).then_inc(V1a.sem, V1a.step("keep"))

            def conv(u):
                if u[0]:
                    c, n = u[0]
                    re, im = pA[:, 0, :].rearrange("p (b d) -> p b d", b=GB), pA[:, 1, :].rearrange("p (b d) -> p b d", b=GB)
                    K = [KF[:, i, :].unsqueeze(1).to_broadcast([128, GB, D]) for i in range(3)]
                    v4 = lambda t: t.rearrange("p (b d) -> p b d", b=GB)
                    dve.wait_ge(P2a.sem, P2a.at("F", n))
                    dve.wait_ge(V2a.sem, V2a.at("Yi", n - 1))
                    dve.tensor_tensor(v4(t1), re, K[0], ALU.mult).then_inc(V2a.sem, V2a.step("t1"))
                    dve.tensor_tensor(v4(t2), im, K[1], ALU.mult).then_inc(V2a.sem, V2a.step("t2"))
                    dve.wait_ge(V2a.sem, V2a.at("t2", n))
                    dve.wait_ge(P2b.sem, P2b.at("G", n - 1))
                    dve.tensor_tensor(Yr, t1, t2, ALU.subtract).then_inc(V2a.sem, V2a.step("Yr"))
                    dve.tensor_tensor(v4(t3), re, K[1], ALU.mult).then_inc(V2a.sem, V2a.step("t3"))
                    dve.tensor_tensor(v4(t4), im, K[2], ALU.mult).then_inc(V2a.sem, V2a.step("t4"))
                    dve.wait_ge(V2a.sem, V2a.at("t4", n))
                    dve.tensor_tensor(Yi, t3, t4, ALU.add).then_inc(V2a.sem, V2a.step("Yi"))

            def f0(u):
                if u[3]:
                    b, n = u[3]
                    dve.wait_ge(G3c.sem, G3c.at("b", n))
                    dve.scalar_tensor_tensor(X[:, b, :], ay[:], tg[:, 0:1], X[:, b, :], ALU.mult, ALU.add).then_inc(V3d.sem, V3d.step("x_out"))
                if u[2]:
                    b, n = u[2]
                    dve.wait_ge(P3c.sem, P3c.at("y", n))
                    dve.wait_ge(V3c.sem, V3c.at("xt", n - 1))
                    dve.tensor_tensor(fb[:, 0:D], pC[:, 0, 0:D], r0("b2"), ALU.add).then_inc(V3c.sem, V3c.step("yb"))
                    dve.wait_ge(V3c.sem, V3c.at("yb", n))
                    dve.wait_ge(V3c.sem, V3c.at("xn", n - 1))
                    dve.tensor_tensor(fb[:, D:2 * D], fb[:, 0:D], U[:, b, :], ALU.add).then_inc(V3c.sem, V3c.step("xt"))
                    dve.wait_ge(V3c.sem, V3c.at("xt", n))
                    dve.wait_ge(G3c.sem, G3c.at("g", n - 1))
                    normalise(dve, V3c, N3c, n, a2[:], fb[:, D:2 * D], N2, s_pass)
                if u[0]:
                    b, n = u[0]
                    dve.wait_ge(V3a.sem, V3a.at("z", n - 1))
                    dve.scalar_tensor_tensor(u1[:], FO[:, b, 0:D], 1.0, U[:, b, :], ALU.add, ALU.mult).then_inc(V3a.sem, V3a.step("z1"))
                    dve.wait_ge(V3a.sem, V3a.at("z1", n))
                    dve.wait_ge(V3a.sem, V3a.at("xt", n - 1))
                    dve.tensor_tensor(fm[:, 0:D], u1[:], FO[:, b, D:2 * D], ALU.add).then_inc(V3a.sem, V3a.step("z"))
                    dve.wait_ge(V3a.sem, V3a.at("z", n))
                    dve.tensor_tensor(U[:, b, :], fm[:, 0:D], XD[:, b, :], ALU.add).then_inc(V3a.sem, V3a.step("xt"))
                    dve.wait_ge(V3a.sem, V3a.at("xt", n))
                    dve.wait_ge(G3a.sem, G3a.at("g", n - 1))
                    normalise(dve, V3a, N3a, n, cx, U[:, b, :], N1, s_pass)

            def route(u):
                if u[2]:
                    b, n = u[2]
                    S = V4c
                    dve.wait_ge(P4b.sem, P4b.at("lg", n))
                    dve.wait_ge(S.sem, S.at("keep", n - 1))
                    dve.tensor_tensor(l8, pA[:, 1, 0:NE], r0("br"), ALU.add).then_inc(S.sem, S.step("lb"))
                    dve.wait_ge(S.sem, S.at("lb", n))
                    dve.sem_inc(s_pass, 1)
                    dve.max(e8, l8).then_inc(S.sem, S.step("max"))
                    dve.wait_ge(S.sem, S.at("max", n))
                    dve.sem_inc(s_pass, 1)
                    dve.max_index(i8.bitcast(mybir.dt.uint32), e8, l8).then_inc(S.sem, S.step("idx"))
                    dve.wait_ge(S.sem, S.at("idx", n))
                    dve.tensor_copy(i8f, i8.bitcast(mybir.dt.uint32)).then_inc(S.sem, S.step("idxf"))
                    dve.tensor_tensor(ed[:, 0:1], e8[:, 1:2], e8[:, 0:1], ALU.subtract).then_inc(S.sem, S.step("gap"))
                if u[3]:
                    b, n = u[3]
                    dve.wait_ge(P4d.sem, P4d.at("bb", n))
                    dve.tensor_copy(ACC[:, b, :], pC[:, 1, 0:D]).then_inc(V4d.sem, V4d.step("acc"))
                if u[0]:
                    b, n = u[0]
                    dve.wait_ge(P4b.sem, P4b.at("xT", n - 1))
                    moments(dve, V4a, N4a, n, X[:, b, :], N1, s_pass)
                if u[2]:
                    b, n = u[2]
                    S = V4c
                    dve.wait_ge(A4c.sem, A4c.at("exp", n))
                    dve.tensor_scalar(ed[:, 2:3], ed[:, 1:2], 1.0, None, ALU.add).then_inc(S.sem, S.step("den"))
                    dve.wait_ge(S.sem, S.at("den", n))
                    dve.reciprocal(ed[:, 3:4], ed[:, 2:3]).then_inc(S.sem, S.step("w0"))
                    dve.wait_ge(S.sem, S.at("w0", n))
                    dve.tensor_tensor(ed[:, 2:3], ed[:, 3:4], ed[:, 1:2], ALU.mult).then_inc(S.sem, S.step("w1"))
                    dve.wait_ge(S.sem, S.at("w1", n))
                    dve.tensor_scalar(c0, r0("experts"), i8f[:, 0:1], ed[:, 3:4], ALU.is_equal, ALU.mult).then_inc(S.sem, S.step("c0"))
                    dve.tensor_scalar(c1, r0("experts"), i8f[:, 1:2], ed[:, 2:3], ALU.is_equal, ALU.mult).then_inc(S.sem, S.step("c1"))
                    dve.wait_ge(S.sem, S.at("c1", n))
                    dve.wait_ge(P4d.sem, P4d.at("cT", n - 1))
                    dve.tensor_tensor(c2, c0, c1, ALU.add).then_inc(S.sem, S.step("cb"))
                    dve.tensor_tensor(CB[:, b, :], c0, c1, ALU.add).then_inc(S.sem, S.step("keep"))
                if u[0]:
                    b, n = u[0]
                    centre(dve, V4a, N4a, n, ax, X[:, b, :], N1)

            def experts(g, n):
                for e in range(NE):
                    dve.wait_ge(P4e.sem, P4e.at(f"y{e}", n))
                    dve.wait_ge(V4e.sem, V4e.at(f"acc{(e - 1) % NE}", n - (e == 0)))
                    for t in range(GB):
                        b = g * GB + t
                        ins = dve.scalar_tensor_tensor(ACC[:, b, :], pC[:, e % 2, 128 * t:128 * t + 128], CB[:, b, e:e + 1], ACC[:, b, :],
                                                       ALU.mult, ALU.add)
                    ins.then_inc(V4e.sem, V4e.step(f"acc{e}"))

            def x1(u):
                if u[2]:
                    b, n = u[2]
                    dve.wait_ge(P5b.sem, P5b.at("S", n))
                    dve.wait_ge(V5c.sem, V5c.at("sub", n - 1))
                    for (h, m), p in zip(SPANS, (pC[:, 0, :], pC[:, 1, :], pD[:, 0, :])):
                        ins = dve.tensor_reduce(dmx[:, h:h + m], p[:, 0:m * S2].rearrange("p (h s) -> p h s", s=S2), AX.X, ALU.max)
                    ins.then_inc(V5c.sem, V5c.step("max"))
                    dve.wait_ge(V5c.sem, V5c.at("max", n))
                    dve.wait_ge(A5c.sem, A5c.at("exp", n - 1))
                    for (h, m), p in zip(SPANS, (pC[:, 0, :], pC[:, 1, :], pD[:, 0, :])):
                        ins = dve.tensor_tensor(dsub[:, h:h + m, :], p[:, 0:m * S2].rearrange("p (h s) -> p h s", s=S2),
                                                dmx[:, h:h + m].unsqueeze(2).to_broadcast([T, m, S2]), ALU.subtract)
                    ins.then_inc(V5c.sem, V5c.step("sub"))
                if u[3]:
                    b, n = u[3]
                    dve.wait_ge(P5d.sem, P5d.at("PT1", n))
                    dve.tensor_copy(dpT[0:S2, 8:16, :], blocks(pB)[0:S2]).then_inc(V5d.sem, V5d.step("pT1"))
                if u[4]:
                    b, n = u[4]
                    dve.wait_ge(V5d.sem, V5d.at("x_out", n))
                    moments(dve, V5e, N5e, n, X[:, b, :], N2, s_pass)
                if u[0]:
                    b, n = u[0]
                    dve.scalar_tensor_tensor(X[:, b, :], ACC[:, b, :], tg[:, 1:2], X[:, b, :], ALU.mult, ALU.add).then_inc(V5a.sem, V5a.step("x_in"))
                    dve.wait_ge(V5a.sem, V5a.at("x_in", n))
                    dve.wait_ge(P5b.sem, P5b.at("xT", n - 1))
                    moments(dve, V5a, N5a, n, X[:, b, :], N1, s_pass)
                if u[4]:
                    b, n = u[4]
                    centre(dve, V5e, N5e, n, XD[:, b, :], X[:, b, :], N2)
                if u[2]:
                    b, n = u[2]
                    dve.wait_ge(A5c.sem, A5c.at("exp", n))
                    dve.tensor_reduce(dsum, dpr, AX.X, ALU.add).then_inc(V5c.sem, V5c.step("sum"))
                    dve.wait_ge(V5c.sem, V5c.at("sum", n))
                    dve.wait_ge(G5c.sem, G5c.at("p", n - 1))
                    dve.reciprocal(dinv, dsum).then_inc(V5c.sem, V5c.step("inv"))
                if u[0]:
                    b, n = u[0]
                    centre(dve, V5a, N5a, n, dx, X[:, b, :], N1)
                if u[3]:
                    b, n = u[3]
                    dve.wait_ge(P5d.sem, P5d.at("y", n))
                    dve.wait_ge(V5d.sem, V5d.at("x_out", n - 1))
                    dve.tensor_tensor(dyb, pD[:, 1, 256:384], r0("bo"), ALU.add).then_inc(V5d.sem, V5d.step("yb"))
                    dve.wait_ge(V5d.sem, V5d.at("yb", n))
                    dve.scalar_tensor_tensor(X[:, b, :], dyb, tg[:, 2:3], X[:, b, :], ALU.mult, ALU.add).then_inc(V5d.sem, V5d.step("x_out"))

            pipeline(dve, x0, 4, B, 0)
            pipeline(dve, conv, 2, NG, 0)
            after(dve, NG - 1, A2b)
            pipeline(dve, f0, 4, B, 0)
            after(dve, B - 1, V3d)
            pipeline(dve, route, 4, B, 0)
            after(dve, B - 1, V4d)
            with dve.Fori(0, NG) as g:
                experts(g, g)
            after(dve, NG - 1, V4e)
            pipeline(dve, x1, 5, B, 0)
            after(dve, B - 1, V5e)
            dve.wait_ge(s_clear, 3)
            dve.wait_ge(GT.sem, GT.at("table", DEPTH - 1))
            pipeline(dve, stack, STAGES, UNITS, 0)
            after(dve, B * DEPTH - 1, FV4)
            for g in range(NG):
                at = slice(GB * g, GB * g + GB)
                dve.scalar_tensor_tensor(X[:, at, :], XD[:, at, :], tg[:, 3:4], X[:, at, :], ALU.mult, ALU.add).then_inc(VF.sem, VF.step("x"))


def rope_tables():
    half = np.arange(0, E, 2, dtype=np.float32)
    inv_freq = (1.0 / 10000.0 ** (half / E)).astype(np.float32)
    t = np.arange(T, dtype=np.float32)
    f = t[:, None] * inv_freq[None, :]
    f = np.concatenate([f, f], -1).astype(np.float32)
    base = (half + 0.4 * E) / (1.4 * E)
    power = (t - T // 2) / (WINDOW // 2)
    s = base[None, :] ** power[:, None]
    s = np.concatenate([s, s], -1)
    sign = np.concatenate([-np.ones(E // 2), np.ones(E // 2)])
    c, sn = np.cos(f), np.sin(f) * sign
    return np.stack([c * s, sn * s, c / s, sn / s], 1).reshape(T, 4 * E).astype(np.float32)


def constants():
    i, j = np.arange(T)[:, None], np.arange(T)[None, :]
    band = np.where((j <= i) & (j >= i - WINDOW), 0.0, BIG16).astype(np.float32)
    return {
        "ident": np.eye(128, dtype=np.float32),
        "band": band,
        "rope": rope_tables(),
    }


def layout(inputs):
    w = {k: np.asarray(x) for k, x in inputs.items()}
    wall = np.zeros((DEPTH, 128, W_ALL), np.float32)
    wall[:, :, W_QKV:W_O] = w["L1_ffn_Wqkv"]
    wall[:, :, W_O:W_1] = w["L1_ffn_Wo"].reshape(DEPTH, 8, 128, D).transpose(0, 2, 1, 3).reshape(DEPTH, 128, 8 * D)
    wall[:, :, W_1:W_2] = w["L1_ffn_W1"]
    w2 = np.zeros((DEPTH, FC * 128, D), np.float32)
    w2[:, :FF] = w["L1_ffn_W2"]
    wall[:, :, W_2:] = w2.reshape(DEPTH, FC, 128, D).transpose(0, 2, 1, 3).reshape(DEPTH, 128, FC * D)
    swap = lambda s: np.concatenate([s[:, E // 2:], s[:, :E // 2]], 1)
    qs, ks = w["L1_ffn_q_scale"], w["L1_ffn_k_scale"]
    rall = np.concatenate([w["L1_ffn_ln_g"], w["L1_ffn_ln_b"], w["L1_ffn_b1"], w["L1_ffn_b2"], qs, swap(qs), ks, swap(ks)], 1)
    def rows(x, k=128):
        y = np.zeros((k, x.shape[1]), np.float32)
        y[:x.shape[0]] = x
        return y

    f, t = np.arange(128.0)[:, None], np.arange(128.0)[None, :]
    ang = 2 * np.pi * f * t / 256
    Fc, Fs, Gc, Gs = np.cos(ang).T.copy(), -np.sin(ang).T.copy(), np.cos(ang) / 128, -np.sin(ang) / 128
    sign = (-1.0) ** np.arange(128)
    Fs[:, 0], Gc[0], Gs[0] = sign, 1 / 256, sign / 256
    twice = lambda m: np.concatenate([m.T, m.T], 0)
    hm = lambda h: np.repeat(np.eye(h), 128 // h, 0)
    l0 = lambda k: w["L0_xattn_" + k]
    l1 = lambda k: w["L1_xattn_" + k]
    parts = {
        "Wq": l0("Wq"), "film": np.concatenate([l0("W_film_in"), l0("W_film_out")], 1), "W1": l0("W1"),
        "W2": l0("W2").reshape(4, 128, D).transpose(1, 0, 2).reshape(128, 4 * D), "Wr": w["L0_ffn_Wr"], "wq1": l1("wq"), "wo1": l1("wo"),
        "k0": rows(l0("Wk")), "v0": rows(l0("Wv")), "k1": rows(np.concatenate([l1("wk"), l1("bk")[None]], 0)),
        "v1": rows(np.concatenate([l1("wv"), l1("bv")[None]], 0)), "Fc": Fc, "Fs": Fs, "Gc": Gc, "Gs": Gs,
        "are": twice(l0("A_re")), "aim": twice(l0("A_im")), "cre": twice(l0("C_re")), "cim": twice(l0("C_im")), "hm0": hm(H0), "hm1": hm(H1),
        "j": np.tile(np.arange(NJ), (128, 1)), "i": np.tile(np.arange(NI) * NJ, (128, 1)),
        "lanes": np.tile(np.repeat(np.eye(4), DH1, 1).reshape(1, 128), (128, 1)),
    }
    w0 = np.concatenate([parts[k].astype(np.float32) for k in W0_AT], 1)
    parts = {
        "g_in": l0("g_norm_in"), "b_in": l0("b_norm_in"), "g_ffn": l0("g_ffn"), "b_ffn": l0("b_ffn"), "g_out": l0("g_norm_out"),
        "b_out": l0("b_norm_out"), "b2": l0("b2"), "film": np.concatenate([l0("b_film_in"), l0("b_film_out")]), "br": w["L0_ffn_br"], "bo": l1("bo"),
        "gates": np.stack([w["g_xattn"][0], w["g_ffn"][0], w["g_xattn"][1], w["g_ffn"][1]]), "mod": l0("mod_gate").reshape(1),
        "log_dt": l0("log_dt"), "dskip": l0("D_skip"), "experts": np.arange(NE),
    }
    r0 = np.concatenate([parts[k].astype(np.float32) for k in R0_AT])
    m0 = (np.arange(128) < NS).astype(np.float32)[:, None]
    z = (np.arange(128) == 0).astype(np.float32)[:, None]
    parts = {"b1": l0("b1").reshape(4, 128).T, "bq": l1("bq")[:, None], "mb1": w["L0_ffn_b1"].reshape(4 * NE, 128).T,
             "m0": m0, "m1": 1 - m0, "-m0": -m0, "-m1": m0 - 1, "off": 0.25 * m0, "nz": 1 - z, "z": z}
    cols = np.concatenate([parts[k].astype(np.float32) for k in C_AT], 1)
    ctx = np.ones((DC + 1, B * S2), np.float32)
    ctx[:DC] = w["ctx_768"].transpose(2, 0, 1).reshape(DC, B * S2)
    return {"w_l1": wall, "r_l1": rall, "w0": w0, "r0": r0, "cols": cols, "ctx": ctx, "b2m": w["L0_ffn_b2"],
            "mw1": w["L0_ffn_W1"].transpose(1, 0, 2).reshape(128, NE * FE),
            "mw2": w["L0_ffn_W2"].reshape(NE, 4, 128, D).transpose(2, 0, 1, 3).reshape(128, NE * 4 * D),
            "tmask": w["mask_BxS_bf1"].T.view(np.uint8), "vmask": w["mask_BxS2_bf1"].reshape(1, B * S2).view(np.uint8),
            "x": w["x"]}


def kernel(**inputs):
    import concourse.bacc as _bacc
    from concourse.bass_utils import run_bass_kernel_spmd

    arrays = dict(constants(), **layout(inputs))
    arrays = {name: np.ascontiguousarray(x) for name, x in arrays.items()}
    nc = _bacc.Bacc("TRN2", target_bir_lowering=False, num_devices=1)
    a = {name: nc.dram_tensor(name, x.shape, mybir.dt.from_np(x.dtype), kind="ExternalInput").ap() for name, x in arrays.items()}
    out = nc.dram_tensor("out", (B, T, D), F32, kind="ExternalOutput").ap()
    flamingo(nc, a, out)
    r = run_bass_kernel_spmd(nc, [arrays], core_ids=[0])
    return r.results[0]["out"]
```
